# Optimizing a Trainium2 kernel written in Bass

```python
import numpy as np
import jax
import jax.numpy as jnp

def _softmax(x, axis=-1):
    return jax.nn.softmax(x, axis=axis)

def _gelu(x):
    return jax.nn.gelu(x, approximate=True)

def _silu(x):
    return jax.nn.silu(x)

def _sigmoid(x):
    return jax.nn.sigmoid(x)

def _layernorm(x, axis=-1, eps=1e-05):
    m = jnp.mean(x, axis=axis, keepdims=True)
    v = jnp.var(x, axis=axis, keepdims=True)
    return (x - m) / jnp.sqrt(v + eps)

def _scatter_add(tgt, idx, src, axis=0):
    return tgt.at[idx].add(src)

def _segment_sum(src, seg, n):
    return jax.ops.segment_sum(src, seg, n)
kernel_name = 'mk_early_fusion_d1_tok_img256_r4_b49295'

def setup_inputs(seed: int=0):
    np.random.seed(seed)
    _w = jnp.asarray

    def _rec_inputs():
        import jax
        import jax.numpy as jnp
        _rk = jax.random.key(seed)
        x = -0.000202321 + 1.00025 * jax.random.normal(jax.random.fold_in(_rk, 1), (8, 64, 56, 56), jnp.float32)
        txt = 0.00140203 + 0.288157 * jax.random.normal(jax.random.fold_in(_rk, 2), (8, 128, 64), jnp.float32)
        return (x, txt)
    x, txt = _rec_inputs()

    def _L0_tok_setup():
        import jax, jax.numpy as jnp
        import numpy as np
        B, C, H, W = (8, 64, 56, 56)
        K = 3

        def _unfold3x3(x):
            b, c, h, w = x.shape
            xp = jnp.pad(x, ((0, 0), (0, 0), (1, 1), (1, 1)))
            patches = jnp.stack([xp[:, :, i:i + h, j:j + w] for i in range(K) for j in range(K)], axis=2)
            return patches.reshape(b, c * K * K, h * w).transpose(0, 2, 1)
        key = jax.random.key(seed)
        ks = jax.random.split(key, 8)
        d = C * K * K
        s1 = 1.0 / np.sqrt(d)
        s2 = 1.0 / np.sqrt(C)
        return {'x': jax.random.normal(ks[0], (B, C, H, W), jnp.float32), 'W1': jax.random.uniform(ks[1], (d, C), jnp.float32, -s1, s1), 'b1': jax.random.uniform(ks[2], (C,), jnp.float32, -s1, s1), 'W2': jax.random.uniform(ks[3], (C, d), jnp.float32, -s2, s2), 'b2': jax.random.uniform(ks[4], (d,), jnp.float32, -s2, s2), 'W3': jax.random.uniform(ks[5], (d, C), jnp.float32, -s1, s1), 'b3': jax.random.uniform(ks[6], (C,), jnp.float32, -s1, s1)}
    _L0_tok_all = _L0_tok_setup()
    _L0_tok_in = {k: v for k, v in _L0_tok_all.items() if k in ('W1', 'b1', 'W2', 'b2', 'W3', 'b3')}
    del _L0_tok_all

    def _L0_attn_setup():
        import jax, jax.numpy as jnp
        import numpy as np
        B, S, H = (2, 1024, 64)
        NH, NKV = (8, 4)
        HD = H // NH
        GROUPS = NH // NKV
        ROPE_BASE = 10000.0

        def _rope_cos_sin(seq_len, dim, dtype):
            inv_freq = 1.0 / ROPE_BASE ** (jnp.arange(0, dim, 2, dtype=jnp.float32) / dim)
            t = jnp.arange(seq_len, dtype=jnp.float32)
            freqs = jnp.outer(t, inv_freq)
            emb = jnp.concatenate([freqs, freqs], -1)
            return (jnp.cos(emb).astype(dtype), jnp.sin(emb).astype(dtype))

        def _rotate_half(x):
            x1, x2 = jnp.split(x, 2, axis=-1)
            return jnp.concatenate([-x2, x1], axis=-1)
        key = jax.random.key(seed)
        k0, k1, k2, k3, k4 = jax.random.split(key, 5)
        return {'hidden_states': jax.random.normal(k0, (B, S, H), jnp.float32), 'Wq': jax.random.normal(k1, (H, H), jnp.float32) * 0.02, 'Wk': jax.random.normal(k2, (NKV * HD, H), jnp.float32) * 0.02, 'Wv': jax.random.normal(k3, (NKV * HD, H), jnp.float32) * 0.02, 'Wo': jax.random.normal(k4, (H, H), jnp.float32) * 0.02}
    _L0_attn_all = _L0_attn_setup()
    _L0_attn_in = {k: v for k, v in _L0_attn_all.items() if k in ('Wq', 'Wk', 'Wv', 'Wo')}
    del _L0_attn_all

    def _L0_ffn_setup():
        import jax, jax.numpy as jnp
        import numpy as np
        B, S, D = (8, 1024, 64)
        H = 4 * D
        CAPACITY = 0.5
        key = jax.random.key(seed)
        ks = jax.random.split(key, 6)
        x = jax.random.normal(ks[0], (B, S, D), dtype=jnp.float32)
        attention_mask = jnp.zeros((B, 1, 1, S), dtype=jnp.float32)
        wr = jax.random.normal(ks[1], (D, 1), dtype=jnp.float32) * 0.02
        br = jnp.zeros((1,), dtype=jnp.float32)
        w1 = jax.random.normal(ks[2], (D, H), dtype=jnp.float32) * 0.02
        b1 = jnp.zeros((H,), dtype=jnp.float32)
        w2 = jax.random.normal(ks[3], (H, D), dtype=jnp.float32) * 0.02
        b2 = jnp.zeros((D,), dtype=jnp.float32)
        return {'x': x, 'attention_mask': attention_mask, 'wr': wr, 'br': br, 'w1': w1, 'b1': b1, 'w2': w2, 'b2': b2}
    _L0_ffn_all = _L0_ffn_setup()
    _L0_ffn_in = {k: v for k, v in _L0_ffn_all.items() if k in ('attention_mask', 'wr', 'br', 'w1', 'b1', 'w2', 'b2')}
    del _L0_ffn_all
    return {'x': x, 'txt': txt, 'L0_tok_W1': _L0_tok_in['W1'], 'L0_tok_b1': _L0_tok_in['b1'], 'L0_tok_W2': _L0_tok_in['W2'], 'L0_tok_b2': _L0_tok_in['b2'], 'L0_tok_W3': _L0_tok_in['W3'], 'L0_tok_b3': _L0_tok_in['b3'], 'L0_attn_Wq': _L0_attn_in['Wq'], 'L0_attn_Wk': _L0_attn_in['Wk'], 'L0_attn_Wv': _L0_attn_in['Wv'], 'L0_attn_Wo': _L0_attn_in['Wo'], 'L0_ffn_attention_mask': _L0_ffn_in['attention_mask'], 'L0_ffn_wr': _L0_ffn_in['wr'], 'L0_ffn_br': _L0_ffn_in['br'], 'L0_ffn_w1': _L0_ffn_in['w1'], 'L0_ffn_b1': _L0_ffn_in['b1'], 'L0_ffn_w2': _L0_ffn_in['w2'], 'L0_ffn_b2': _L0_ffn_in['b2']}

def reference(x, txt, L0_tok_W1, L0_tok_b1, L0_tok_W2, L0_tok_b2, L0_tok_W3, L0_tok_b3, L0_attn_Wq, L0_attn_Wk, L0_attn_Wv, L0_attn_Wo, L0_ffn_attention_mask, L0_ffn_wr, L0_ffn_br, L0_ffn_w1, L0_ffn_b1, L0_ffn_w2, L0_ffn_b2):
    import jax
    import jax.numpy as jnp

    def _L0_tok_ref(x, W1, b1, W2, b2, W3, b3):
        import jax, jax.numpy as jnp
        import numpy as np
        B, C, H, W = (8, 64, 56, 56)
        K = 3

        def _unfold3x3(x):
            b, c, h, w = x.shape
            xp = jnp.pad(x, ((0, 0), (0, 0), (1, 1), (1, 1)))
            patches = jnp.stack([xp[:, :, i:i + h, j:j + w] for i in range(K) for j in range(K)], axis=2)
            return patches.reshape(b, c * K * K, h * w).transpose(0, 2, 1)
        t = _unfold3x3(x)
        h1 = jax.nn.relu(jnp.einsum('bld,dc->blc', t, W1) + b1)
        s = jax.nn.sigmoid(jnp.einsum('blc,cd->bld', h1, W2) + b2)
        out = jnp.einsum('bld,dc->blc', t * s, W3) + b3
        return out

    def _L0_attn_ref(hidden_states, Wq, Wk, Wv, Wo):
        import jax, jax.numpy as jnp
        import numpy as np
        B, S, H = (2, 1024, 64)
        NH, NKV = (8, 4)
        HD = H // NH
        GROUPS = NH // NKV
        ROPE_BASE = 10000.0

        def _rope_cos_sin(seq_len, dim, dtype):
            inv_freq = 1.0 / ROPE_BASE ** (jnp.arange(0, dim, 2, dtype=jnp.float32) / dim)
            t = jnp.arange(seq_len, dtype=jnp.float32)
            freqs = jnp.outer(t, inv_freq)
            emb = jnp.concatenate([freqs, freqs], -1)
            return (jnp.cos(emb).astype(dtype), jnp.sin(emb).astype(dtype))

        def _rotate_half(x):
            x1, x2 = jnp.split(x, 2, axis=-1)
            return jnp.concatenate([-x2, x1], axis=-1)
        b, s, _ = hidden_states.shape
        q = (hidden_states @ Wq.T).reshape(b, s, NH, HD).transpose(0, 2, 1, 3)
        k = (hidden_states @ Wk.T).reshape(b, s, NKV, HD).transpose(0, 2, 1, 3)
        v = (hidden_states @ Wv.T).reshape(b, s, NKV, HD).transpose(0, 2, 1, 3)
        cos, sin = _rope_cos_sin(s, HD, hidden_states.dtype)
        q = q * cos + _rotate_half(q) * sin
        k = k * cos + _rotate_half(k) * sin
        k = jnp.repeat(k, GROUPS, axis=1)
        v = jnp.repeat(v, GROUPS, axis=1)
        scores = jnp.einsum('bhqd,bhkd->bhqk', q, k) / jnp.sqrt(jnp.float32(HD)).astype(q.dtype)
        causal = jnp.triu(jnp.full((s, s), -jnp.inf, dtype=scores.dtype), k=1)
        scores = scores + causal
        attn = jax.nn.softmax(scores.astype(jnp.float32), axis=-1).astype(q.dtype)
        out = jnp.einsum('bhqk,bhkd->bhqd', attn, v)
        out = out.transpose(0, 2, 1, 3).reshape(b, s, NH * HD)
        return out @ Wo.T

    def _L0_ffn_ref(x, attention_mask, wr, br, w1, b1, w2, b2):
        import jax, jax.numpy as jnp
        import numpy as np
        B, S, D = (8, 1024, 64)
        H = 4 * D
        CAPACITY = 0.5
        b, s, d = x.shape
        weights = (jnp.einsum('bsd,do->bso', x, wr) + br)[..., 0]
        k = max(1, int(CAPACITY * s))
        kk = k - 1 if k > 1 else 1
        _, idx = jax.lax.top_k(weights, k)
        sel_idx = idx[:, :kk]
        sel = jnp.take_along_axis(x, sel_idx[:, :, None], axis=1)
        h = jax.nn.gelu(jnp.einsum('bkd,dh->bkh', sel, w1) + b1)
        y = jnp.einsum('bkh,hd->bkd', h, w2) + b2
        w_sel = jnp.take_along_axis(weights, sel_idx, axis=1)
        y = y * w_sel[..., None]
        batch_idx = jnp.arange(b)[:, None]
        processed = jnp.zeros_like(x).at[batch_idx, sel_idx].set(y)
        return processed + x
    h = _L0_tok_ref(x, L0_tok_W1, L0_tok_b1, L0_tok_W2, L0_tok_b2, L0_tok_W3, L0_tok_b3)
    h = jnp.concatenate([h, txt], axis=1)
    h = h + _L0_attn_ref(_layernorm(h, axis=-1), L0_attn_Wq, L0_attn_Wk, L0_attn_Wv, L0_attn_Wo)
    h = h + _L0_ffn_ref(_layernorm(h, axis=-1), L0_ffn_attention_mask, L0_ffn_wr, L0_ffn_br, L0_ffn_w1, L0_ffn_b1, L0_ffn_w2, L0_ffn_b2)
    return h

_drawn_inputs = setup_inputs


def setup_inputs(seed=0):
    import zlib

    import numpy as np

    out = dict(_drawn_inputs(seed))
    spreads = {'L0_ffn_b1': (0.0, 0.8), 'L0_ffn_b2': (0.0, 0.785)}
    factors = {'L0_tok_b1': 8.0,
     'L0_attn_Wq': 8.0,
     'L0_attn_Wk': 8.0,
     'L0_attn_Wv': 6.417,
     'L0_attn_Wo': 5.953,
     'L0_ffn_wr': 6.263,
     'L0_ffn_w1': 8.0,
     'L0_ffn_w2': 8.0}
    for name, (base, spread) in spreads.items():
        noise = np.random.default_rng([zlib.crc32(name.encode()), seed]).standard_normal(out[name].shape)
        drawn = base * np.exp(spread * noise) if base else spread * noise
        out[name] = jnp.asarray(drawn.astype(out[name].dtype))
    for name, factor in factors.items():
        out[name] = (out[name] * factor).astype(out[name].dtype)
    return out
```

```python
from contextlib import ExitStack

import concourse.bass as bass
from concourse import mybir

ALU = mybir.AluOpType
ACT = mybir.ActivationFunctionType
F32 = mybir.dt.float32
BF16 = mybir.dt.bfloat16
U32 = mybir.dt.uint32
AX_X = mybir.AxisListType.X

P = 128
TILE = 512
B, C, H, W = 8, 64, 56, 56
IMG = H * W
TXT = 128
S = IMG + TXT
NH, KV, HD = 8, 4, 8
GROUPS = 2
GH = NH // GROUPS
GKV = KV // GROUPS
KB = -(-S // P)
QT = -(-S // TILE)
QB = TILE // P
VW = 32
ROWS = 96
MAX_PARTS = 2
Q_TERM = (0, 0, 0, 1, 1, 2)
K_TERM = (0, 1, 2, 0, 1, 0)
P_RING = 3
S_RING = 3
M_RING = 3
PAIRS = B // 2
KS = 3
SHIFTS = KS * KS
PH, PW = H + 2, W + 2
IMG_ROWS = 8
CT = IMG_ROWS * W
CTILES = H // IMG_ROWS
PARTS = 3
VB = 8
EPS = 1e-5
TOP = S // 2 - 1
ROWS_PER_BATCH = P // B
SPAN = S // ROWS_PER_BATCH
FF = 4 * C
CHUNKS = 2 * FF // P
TILES = [(t0, min(TILE, S - t0)) for t0 in range(0, S, TILE)]


def tokens(nc, x, txt, conv_w, conv_b, proj_w, tables, h0_out, q_parts, k_parts, v_blocks):
    w1, w2, w3 = conv_w
    b1, b2, b3 = conv_b
    wq, wq_turned, wk, wk_turned, wv = proj_w
    centre, mean, cos, sin, identity = tables
    with ExitStack() as ctx:
        def sbuf(name, shape, dt=F32):
            return ctx.enter_context(nc.sbuf_tensor(name, shape, dt))

        def psum(name, shape):
            return ctx.enter_context(nc.psum_tensor(name, shape, F32))

        def sem(name):
            return ctx.enter_context(nc.semaphore(name))

        x_in = sbuf("x_in", [P, IMG])
        x_pad = sbuf("x_pad", [P, PH, PW])
        txt_in = sbuf("txt_in", [TXT, P])
        w1_sb = sbuf("w1_sb", [P, SHIFTS, P])
        w2_sb = sbuf("w2_sb", [P, SHIFTS, P])
        w3_sb = sbuf("w3_sb", [P, SHIFTS, P])
        wq_sb = sbuf("wq_sb", [P, 2, P])
        wk_sb = sbuf("wk_sb", [P, 2, C])
        wv_sb = sbuf("wv_sb", [P, C])
        b1_sb = sbuf("b1_sb", [P, 1])
        b2_sb = sbuf("b2_sb", [P, SHIFTS])
        b3_sb = sbuf("b3_sb", [P, 1])
        eps_sb = sbuf("eps_sb", [P, 1])
        centre_sb = sbuf("centre_sb", [P, P])
        mean_sb = sbuf("mean_sb", [P, P])
        ident_sb = sbuf("ident_sb", [P, P])
        cos_sb = sbuf("cos_sb", [P, S])
        sin_sb = sbuf("sin_sb", [P, S])
        h1 = sbuf("h1", [P, CT])
        gate = sbuf("gate", [P, 2, CT])
        gated = sbuf("gated", [P, 2, CT])
        h0 = sbuf("h0", [P, S])
        square = sbuf("square", [P, CT])
        std = sbuf("std", [P, CT])
        rstd = sbuf("rstd", [P, CT])
        normed = sbuf("normed", [P, S])
        rot = sbuf("rot", [P, 4, CT])
        full = sbuf("full", [P, 2, CT])
        rest = sbuf("rest", [P, 2, CT])
        q_st = sbuf("q_st", [P, 2, PARTS, CT], BF16)
        k_st = sbuf("k_st", [C, 2, PARTS, CT], BF16)
        v_st = sbuf("v_st", [P, KB, 2 * KV, VW])

        hidden_ps = psum("hidden_ps", [P, 1, TILE])
        gate_ps = psum("gate_ps", [P, 2, TILE])
        token_ps = psum("token_ps", [P, 1, TILE])
        norm_ps = psum("norm_ps", [P, 2, TILE])
        proj_ps = psum("proj_ps", [P, 2, TILE])

        loaded = sem("weights_loaded")
        prepared = sem("weights_prepared")
        x_next = sem("x_next")

        def load_pair(eng, p, done):
            eng.dma_start(x_in[:], x[p]).then_inc(done, 16)
            eng.dma_start(txt_in[:], txt[p].rearrange("b t c -> t b c")).then_inc(done, 16)

        with nc.Block(no_gpsimd_drain=True) as block:
            @block.sync
            def _(sp):
                load_pair(sp, 0, loaded)
                pieces = [(w1_sb[:].rearrange("p s c -> p (s c)"), w1), (w2_sb[:].rearrange("p s c -> p (s c)"), w2),
                          (w3_sb[:].rearrange("p s c -> p (s c)"), w3), (b1_sb[:], b1), (b2_sb[:], b2), (b3_sb[:], b3),
                          (wq_sb[:, 0], wq), (wq_sb[:, 1], wq_turned), (wk_sb[:, 0], wk), (wk_sb[:, 1], wk_turned),
                          (wv_sb[:], wv), (centre_sb[:], centre), (mean_sb[:], mean), (ident_sb[:], identity),
                          (cos_sb[:], cos), (sin_sb[:], sin)]
                for dst, src in pieces:
                    sp.dma_start(dst, src).then_inc(loaded, 16)
                sp.wait_ge(loaded, 16 * (2 + len(pieces)))

            @block.vector
            def _(dve):
                nc.vector.memset(x_pad[:], 0.0).then_inc(prepared, 1)
                nc.vector.memset(eps_sb[:], EPS).then_inc(prepared, 1)
                dve.wait_ge(loaded, 16 * 18)
                nc.vector.tensor_scalar(b2_sb[:], b2_sb[:], 0.5, None, ALU.mult).then_inc(prepared, 1)
                nc.vector.tensor_scalar(w3_sb[:], w3_sb[:], 0.5, None, ALU.mult).then_inc(prepared, 1)
                dve.wait_ge(prepared, 4)

            @block.gpsimd
            def _(pool):
                v_ready = prepared
                nc.gpsimd.memset(v_st[:], 0.0).then_inc(x_next, 1)
                pool.wait_ge(x_next, 1)
                nc.gpsimd.memset(v_st[:, :, :, HD:HD + 1], 1.0).then_inc(x_next, 1)
                pool.wait_ge(x_next, 2)

        x_padded = sem("x_padded")
        txt_turned = sem("txt_turned")
        reload = sem("next_pair_loaded")
        hidden_ready = sem("hidden_ready")
        h1_ready = sem("h1_ready")
        gate_ready = sem("gate_ready")
        tanh_ready = sem("tanh_ready")
        gated_ready = sem("gated_ready")
        gated_used = sem("gated_used")
        token_ready = sem("token_ready")
        h0_ready = sem("h0_ready")
        centred = sem("centred")
        squared = sem("squared")
        var_ready = sem("var_ready")
        std_ready = sem("std_ready")
        rstd_ready = sem("rstd_ready")
        normed_ready = sem("normed_ready")
        proj_ready = sem("proj_ready")
        proj_used = sem("proj_used")
        rot_ready = sem("rot_ready")
        full_ready = sem("full_ready")
        high_ready = sem("high_ready")
        rest_ready = sem("rest_ready")
        mid_ready = sem("mid_ready")
        low_ready = sem("low_ready")
        parts_stored = [sem("parts_stored_even"), sem("parts_stored_odd")]
        v_set = sem("v_set")
        stored = sem("pair_stored")
        step_sems = [x_padded, txt_turned, reload, hidden_ready, h1_ready, gate_ready, tanh_ready, gated_ready,
                     gated_used, token_ready, h0_ready, centred, squared, var_ready, std_ready, rstd_ready,
                     normed_ready, proj_ready, proj_used, rot_ready, full_ready, high_ready, rest_ready, mid_ready,
                     low_ready, *parts_stored, v_set, stored, x_next]

        POST = [(IMG, TXT)] + [(n * CT, CT) for n in range(CTILES)]
        NPOST = len(POST)
        V_GROUPS = [range(v, min(v + VB, KB)) for v in range(0, KB, VB)]
        V_AT = {4: [0], 6: [1], NPOST: [2, 3]}
        slots = []
        for m in range(NPOST + 1):
            slots += [("v", v) for v in V_AT.get(m, [])]
            if m < NPOST:
                slots += [("q", m, 0), ("q", m, 1), ("k", m, 0), ("k", m, 1)]
        slot_of = {op: n for n, op in enumerate(slots)}

        with nc.Fori(0, PAIRS) as p:
            with nc.Block(no_gpsimd_drain=True) as block:
                @block.sync
                def _(sp):
                    sp.wait_ge(x_padded, 1)
                    sp.wait_ge(txt_turned, 1)
                    load_pair(sp, (p + 1) & (PAIRS - 1), reload)
                    for m, (t0, w) in enumerate(POST):
                        sp.wait_ge(low_ready, 2 * m + 2)
                        sp.wait_ge(high_ready, 2 * m + 2)
                        sp.wait_ge(mid_ready, 2 * m + 2)
                        for part in range(PARTS):
                            sp.dma_start(q_parts[part, bass.ds(2 * p, 2)].rearrange("b c s -> (b c) s")[:, t0:t0 + w],
                                         q_st[:, m % 2, part, 0:w]).then_inc(parts_stored[m % 2], 16)
                            sp.dma_start(k_parts[part, bass.ds(2 * p, 2)].rearrange("b c s -> (b c) s")[:, t0:t0 + w],
                                         k_st[:, m % 2, part, 0:w]).then_inc(parts_stored[m % 2], 16)
                    sp.wait_ge(h0_ready, NPOST)
                    sp.dma_start(h0_out[p], h0[:]).then_inc(stored, 16)
                    sp.wait_ge(v_set, len(V_GROUPS))
                    for e in range(2):
                        for g in range(GROUPS):
                            n = e * KV + g * GKV
                            dst = v_blocks[bass.ds(2 * p + e, 1), g].rearrange("b p (k v) -> p (b k) v", v=GKV * VW)
                            sp.dma_start(dst, v_st[:, :, n:n + GKV, :].rearrange("p k v w -> p k (v w)")).then_inc(stored, 16)
                    sp.wait_ge(stored, 16 * 5)
                    sp.wait_ge(reload, 32)
                    for half in range(2):
                        sp.wait_ge(parts_stored[half], 16 * 2 * PARTS * (NPOST // 2))

                @block.tensor
                def _(pe):
                    def post(m, stage):
                        t0, w = POST[m]
                        if stage == 0:
                            pe.wait_ge(h0_ready, m + 1)
                            if m >= 1:
                                pe.wait_ge(normed_ready, m)
                            nc.tensor.matmul(norm_ps[:, 0, 0:w], centre_sb[:], h0[:, t0:t0 + w],
                                             start=True, stop=True).then_inc(centred, 1)
                        elif stage == 1:
                            pe.wait_ge(squared, m + 1)
                            nc.tensor.matmul(norm_ps[:, 1, 0:w], mean_sb[:], square[:, 0:w],
                                             start=True, stop=True).then_inc(var_ready, 1)
                        else:
                            which, rows, w_sb = (("q", P, wq_sb), ("k", C, wk_sb))[stage - 2]
                            pe.wait_ge(normed_ready, m + 1)
                            for turned in range(2):
                                n = slot_of[(which, m, turned)]
                                if n >= 2:
                                    pe.wait_ge(proj_used, n - 1)
                                nc.tensor.matmul(proj_ps[0:rows, n % 2, 0:w], w_sb[:, turned], normed[:, t0:t0 + w],
                                                 start=True, stop=True).then_inc(proj_ready, 1)

                    def values(m):
                        for v in V_AT.get(m, []):
                            n = slot_of[("v", v)]
                            pe.wait_ge(proj_used, n - 1)
                            for i, kb in enumerate(V_GROUPS[v]):
                                rows = min(P, S - kb * P)
                                last = nc.tensor.matmul(proj_ps[0:rows, n % 2, i * C:(i + 1) * C],
                                                        normed[:, kb * P:kb * P + rows], wv_sb[:], start=True, stop=True)
                            last.then_inc(proj_ready, 1)

                    nc.tensor.transpose(token_ps[:, 0, 0:TXT], txt_in[:], ident_sb[:]).then_inc(token_ready, 1)
                    pe.wait_ge(token_ready, 1)
                    nc.tensor.sem_inc(txt_turned, 1)
                    pe.wait_ge(x_padded, 1)
                    for n in range(CTILES):
                        r0 = n * IMG_ROWS
                        if n >= 1:
                            pe.wait_ge(h1_ready, n)
                        for s in range(SHIFTS):
                            i, j = divmod(s, KS)
                            last = nc.tensor.matmul(hidden_ps[:, 0, 0:CT], w1_sb[:, s],
                                                    x_pad[:, r0 + i:r0 + i + IMG_ROWS, j:j + W],
                                                    start=(s == 0), stop=(s == SHIFTS - 1))
                        last.then_inc(hidden_ready, 1)
                        values(n)
                        post(n, 0)
                        pe.wait_ge(h1_ready, n + 1)

                        def gate_product(s):
                            g = n * SHIFTS + s
                            if g >= 2:
                                pe.wait_ge(tanh_ready, g - 1)
                            nc.tensor.matmul(gate_ps[:, g % 2, 0:CT], w2_sb[:, s], h1[:],
                                             start=True, stop=True).then_inc(gate_ready, 1)

                        gate_product(0)
                        gate_product(1)
                        post(n, 1)
                        for s in range(SHIFTS):
                            if s + 2 < SHIFTS:
                                gate_product(s + 2)
                            g = n * SHIFTS + s
                            pe.wait_ge(gated_ready, g + 1)
                            if s == 0:
                                pe.wait_ge(h0_ready, n + 1)
                            last = nc.tensor.matmul(token_ps[:, 0, 0:CT], w3_sb[:, s], gated[:, g % 2],
                                                    start=(s == 0), stop=(s == SHIFTS - 1))
                            last.then_inc(gated_used, 1)
                            if s == 4:
                                post(n, 2)
                        pe.wait_ge(gated_used, (n + 1) * SHIFTS)
                        nc.tensor.sem_inc(token_ready, 1)
                        post(n, 3)
                    for stage in range(4):
                        post(NPOST - 1, stage)
                    values(NPOST)

                @block.scalar
                def _(act):
                    def post(m, stage):
                        t0, w = POST[m]
                        if stage == 0:
                            act.wait_ge(centred, m + 1)
                            if m >= 1:
                                act.wait_ge(var_ready, m)
                            nc.scalar.activation(square[:, 0:w], norm_ps[:, 0, 0:w], ACT.Square).then_inc(squared, 1)
                        elif stage == 1:
                            act.wait_ge(var_ready, m + 1)
                            if m >= 1:
                                act.wait_ge(rstd_ready, m)
                            nc.scalar.activation(std[:, 0:w], norm_ps[:, 1, 0:w], ACT.Sqrt,
                                                 bias=eps_sb[:]).then_inc(std_ready, 1)
                        else:
                            if m >= 2 and stage == 2:
                                act.wait_ge(parts_stored[m % 2], 16 * 2 * PARTS * (m // 2))
                            for i, (rows, st) in enumerate(((P, q_st), (C, k_st))):
                                src, ready, done = (full, full_ready, high_ready) if stage == 2 else (rest, rest_ready, mid_ready)
                                act.wait_ge(ready, 2 * m + i + 1)
                                nc.scalar.copy(st[0:rows, m % 2, stage - 2, 0:w], src[0:rows, i, 0:w]).then_inc(done, 1)

                    for n in range(CTILES):
                        act.wait_ge(hidden_ready, n + 1)
                        if n >= 1:
                            act.wait_ge(gate_ready, n * SHIFTS)
                        nc.scalar.activation(h1[:], hidden_ps[:, 0, 0:CT], ACT.Relu, bias=b1_sb[:]).then_inc(h1_ready, 1)
                        post(n, 0)
                        for s in range(SHIFTS):
                            g = n * SHIFTS + s
                            act.wait_ge(gate_ready, g + 1)
                            if g >= 2:
                                act.wait_ge(gated_ready, g - 1)
                            nc.scalar.activation(gate[:, g % 2], gate_ps[:, g % 2, 0:CT], ACT.Tanh,
                                                 bias=b2_sb[:, s:s + 1], scale=0.5).then_inc(tanh_ready, 1)
                            if s == 1:
                                post(n, 1)
                        post(n, 2)
                        post(n, 3)
                    for stage in range(4):
                        post(NPOST - 1, stage)

                @block.vector
                def _(dve):
                    def take_up(m):
                        t0, w = POST[m]
                        dve.wait_ge(token_ready, m + 1)
                        if m == 0:
                            nc.vector.tensor_copy(h0[:, t0:t0 + w], token_ps[:, 0, 0:w]).then_inc(h0_ready, 1)
                        else:
                            nc.vector.tensor_scalar(h0[:, t0:t0 + w], token_ps[:, 0, 0:w], b3_sb[:], None,
                                                    ALU.add).then_inc(h0_ready, 1)

                    def post(m, stage):
                        t0, w = POST[m]
                        if stage == 1:
                            dve.wait_ge(std_ready, m + 1)
                            nc.vector.reciprocal(rstd[:, 0:w], std[:, 0:w]).then_inc(rstd_ready, 1)
                            dve.wait_ge(rstd_ready, m + 1)
                            nc.vector.tensor_tensor(normed[:, t0:t0 + w], norm_ps[:, 0, 0:w], rstd[:, 0:w],
                                                    ALU.mult).then_inc(normed_ready, 1)
                        else:
                            which, rows = (("q", P), ("k", C))[stage - 2]
                            for turned, table in enumerate((cos_sb, sin_sb)):
                                n = slot_of[(which, m, turned)]
                                dve.wait_ge(proj_ready, n + 1)
                                if m >= 1:
                                    dve.wait_ge(full_ready, 2 * (m - 1) + stage - 1)
                                nc.vector.tensor_tensor(rot[0:rows, 2 * (stage - 2) + turned, 0:w],
                                                        proj_ps[0:rows, n % 2, 0:w], table[0:rows, t0:t0 + w],
                                                        ALU.mult).then_inc(proj_used, 1)
                            dve.wait_ge(proj_used, slot_of[(which, m, 1)] + 1)
                            nc.vector.sem_inc(rot_ready, 1)

                    def values(m):
                        for v in V_AT.get(m, []):
                            n = slot_of[("v", v)]
                            dve.wait_ge(proj_ready, n + 1)
                            whole = [kb for kb in V_GROUPS[v] if (kb + 1) * P <= S]
                            a, k = whole[0], len(whole)
                            src = proj_ps[:, n % 2, 0:k * C].rearrange("p (k v d) -> p k v d", v=2 * KV, d=HD)
                            last = nc.vector.tensor_copy(v_st[:, a:a + k, :, 0:HD], src)
                            if k < len(V_GROUPS[v]):
                                rows = S - (KB - 1) * P
                                last = nc.vector.tensor_copy(
                                    v_st[0:rows, KB - 1, :, 0:HD],
                                    proj_ps[0:rows, n % 2, k * C:(k + 1) * C].rearrange("p (v d) -> p v d", d=HD))
                            last.then_inc(proj_used, 1)
                            dve.wait_ge(proj_used, n + 1)
                            nc.vector.sem_inc(v_set, 1)

                    nc.vector.tensor_copy(x_pad[:, 1:H + 1, 1:W + 1],
                                          x_in[:].rearrange("p (h w) -> p h w", h=H)).then_inc(x_padded, 1)
                    dve.wait_ge(x_padded, 1)
                    for n in range(CTILES):
                        r0 = n * IMG_ROWS
                        take_up(n)
                        values(n)
                        for s in range(SHIFTS):
                            i, j = divmod(s, KS)
                            g = n * SHIFTS + s
                            dve.wait_ge(tanh_ready, g + 1)
                            if g >= 2:
                                dve.wait_ge(gated_used, g - 1)
                            nc.vector.scalar_tensor_tensor(
                                out=gated[:, g % 2].rearrange("p (h w) -> p h w", h=IMG_ROWS),
                                in0=gate[:, g % 2].rearrange("p (h w) -> p h w", h=IMG_ROWS), scalar=1.0,
                                in1=x_pad[:, r0 + i:r0 + i + IMG_ROWS, j:j + W],
                                op0=ALU.add, op1=ALU.mult).then_inc(gated_ready, 1)
                            if s == 2:
                                post(n, 1)
                            if s == 6:
                                post(n, 2)
                        post(n, 3)
                    take_up(NPOST - 1)
                    for stage in (1, 2, 3):
                        post(NPOST - 1, stage)
                    values(NPOST)

                @block.gpsimd
                def _(pool):
                    for m, (t0, w) in enumerate(POST):
                        for i, rows in enumerate((P, C)):
                            pool.wait_ge(rot_ready, 2 * m + i + 1)
                            if m >= 1:
                                pool.wait_ge(high_ready, 2 * (m - 1) + i + 1)
                                pool.wait_ge(rest_ready, 2 * (m - 1) + i + 1)
                            nc.gpsimd.tensor_tensor(full[0:rows, i, 0:w], rot[0:rows, 2 * i, 0:w],
                                                    rot[0:rows, 2 * i + 1, 0:w], ALU.add).then_inc(full_ready, 1)
                        for i, (rows, st) in enumerate(((P, q_st), (C, k_st))):
                            pool.wait_ge(high_ready, 2 * m + i + 1)
                            pool.wait_ge(full_ready, 2 * m + i + 1)
                            if m >= 1:
                                pool.wait_ge(low_ready, 2 * (m - 1) + i + 1)
                            nc.gpsimd.tensor_tensor(rest[0:rows, i, 0:w], full[0:rows, i, 0:w],
                                                    st[0:rows, m % 2, 0, 0:w], ALU.subtract).then_inc(rest_ready, 1)
                        for i, (rows, st) in enumerate(((P, q_st), (C, k_st))):
                            pool.wait_ge(mid_ready, 2 * m + i + 1)
                            nc.gpsimd.tensor_tensor(st[0:rows, m % 2, 2, 0:w], rest[0:rows, i, 0:w],
                                                    st[0:rows, m % 2, 1, 0:w], ALU.subtract).then_inc(low_ready, 1)
            nc.all_engine_barrier(sem_only=True)
            for s in step_sems:
                nc.sync.sem_clear(s)
            nc.all_engine_barrier(sem_only=True)


def attention(nc, q_parts, k_parts, v_blocks, masks, heads_out):
    with ExitStack() as ctx:
        def sbuf(name, shape, dt):
            return ctx.enter_context(nc.sbuf_tensor(name, shape, dt))

        def sem(name):
            return ctx.enter_context(nc.semaphore(name))

        q_rows = sbuf("q_rows", [P, GROUPS, GH, S], BF16)
        k_rows = sbuf("k_rows", [P, GROUPS, S], BF16)
        v_keys = sbuf("v_keys", [P, GROUPS, KB, GKV * VW], F32)
        masks_f32 = sbuf("masks_f32", [P, 3, P], F32)
        masks_sb = sbuf("masks_sb", [P, 3, P], BF16)
        mask_kq, mask_qk, ident = (masks_sb[:, n] for n in range(3))
        part_max = sbuf("part_max", [P, 2, QB, GH, QT], F32)
        row_max = sbuf("row_max", [P, 2, QB, GH], F32)
        max_split = sbuf("max_split", [P, 2, QB, MAX_PARTS, GH], BF16)
        max_rows = sbuf("max_rows", [MAX_PARTS * GH, 2, TILE], BF16)
        probs = sbuf("probs", [P, P_RING, GH, TILE], F32)
        out_sb = sbuf("out_sb", [P, 2, TILE], F32)

        scores = ctx.enter_context(nc.psum_tensor("scores", [P, S_RING, TILE], F32))
        max_scores = ctx.enter_context(nc.psum_tensor("max_scores", [P, M_RING, TILE], F32))
        out_acc = ctx.enter_context(nc.psum_tensor("out_acc", [P, 2, TILE], F32))

        cleared = sem("rows_cleared")
        first_in = sem("first_loads")
        LOADS = 6 * GKV * 2 + 1

        def load_group(eng, b, g, done, share=0, shares=1):
            for n in range(LOADS * share // shares, LOADS * (share + 1) // shares):
                v, term, of_k = n // 12, n // 2 % 6, n % 2
                kv = GKV * g + v
                r = 48 * v + 8 * term
                if n == LOADS - 1:
                    eng.dma_start(v_keys[:, g].rearrange("p k v -> p (k v)"), v_blocks[b, g]).then_inc(done, 16)
                elif of_k:
                    eng.dma_start(k_rows[r:r + HD, g, :],
                                  k_parts[K_TERM[term], b][kv * HD:(kv + 1) * HD, :]).then_inc(done, 16)
                else:
                    q_src = q_parts[Q_TERM[term], b].rearrange("(h d) s -> d h s", d=HD)
                    eng.dma_start(q_rows[r:r + HD, g, 2 * v:2 * v + 2, :],
                                  q_src[:, 2 * kv:2 * kv + 2, :]).then_inc(done, 16)

        with nc.Block(no_gpsimd_drain=True) as block:
            @block.vector
            def _(dve):
                nc.vector.memset(q_rows[:].rearrange("p g h s -> p (g h s)").bitcast(U32), 0).then_inc(cleared, 1)
                nc.vector.memset(part_max[:], 0.0).then_inc(cleared, 1)
                nc.vector.memset(k_rows[ROWS:ROWS + MAX_PARTS], -1.0).then_inc(cleared, 1)
                dve.wait_ge(first_in, 16)
                nc.vector.tensor_copy(masks_sb[:], masks_f32[:]).then_inc(cleared, 1)
                dve.wait_ge(cleared, 4)

            @block.sync
            def _(sp):
                sp.dma_start(masks_f32[:], masks.rearrange("m p n -> p m n")).then_inc(first_in, 16)
                sp.wait_ge(first_in, 16)
                sp.wait_ge(cleared, 3)
                load_group(sp, 0, 0, first_in)
                sp.wait_ge(first_in, 16 * (1 + LOADS))

        g1_loaded = sem("group1_loaded")
        next_loaded = sem("next_batch_loaded")
        max_ready = sem("max_slot_ready")
        max_used = sem("max_slot_used")
        chain = sem("row_max_steps")
        split_ready = sem("max_split_ready")
        rows_copied = sem("max_rows_copied")
        rows_set = [sem("max_rows_in_q_even"), sem("max_rows_in_q_odd")]
        s_ready = sem("scores_ready")
        p_ready = sem("probs_ready")
        p_used = sem("probs_used")
        o_ready = sem("out_ready")
        o_copied = sem("out_copied")
        o_stored = [sem("out_stored_even"), sem("out_stored_odd")]
        step_sems = [g1_loaded, next_loaded, max_ready, max_used, chain, split_ready, rows_copied, *rows_set,
                     s_ready, p_ready, p_used, o_ready, o_copied, *o_stored]

        UNITS = [(g, t) for g in range(GROUPS) for t in range(QT)]
        NU = len(UNITS)
        width = [min(TILE, S - t * TILE) for t in range(QT)]

        STEPS = [(u, j) for u, (g, t) in enumerate(UNITS) for j in range(min(KB, QB * (t + 1)))]
        first_step = [min(k for k, (v, j) in enumerate(STEPS) if v == u) for u in range(NU)] + [len(STEPS)]
        began = [0]
        for u, j in STEPS:
            t = UNITS[u][1]
            began.append(began[-1] + width[t] - max(0, j - QB * t) * P)

        MAX_OPS = []
        for u, (g, t) in enumerate(UNITS):
            MAX_OPS.append([(u, i, c, h) for i in range(-(-width[t] // P)) for c in range(t + 1) for h in range(GH)])

        LEAD, TURN_LEAD = 1500, 900
        slots_at = [[] for _ in range(len(STEPS) + 1)]

        def step_at(x):
            return max([0] + [k for k in range(len(STEPS)) if began[k] <= x])

        timed = []
        for u in range(NU):
            start = began[first_step[u - 1]] - LEAD if u else -2 * LEAD
            end = began[first_step[u]] - LEAD
            n = len(MAX_OPS[u])
            for m, op in enumerate(MAX_OPS[u]):
                timed.append((start + (end - start) * (m + 1) / n, 0, op))
            timed.append((began[first_step[u]] - TURN_LEAD, 1, (u,)))
        timed.sort(key=lambda x: x[0])
        for x, _, op in timed:
            slots_at[0 if x <= 0 else step_at(x) + 1].append(op)
        order = [op for ops in slots_at for op in ops]
        slot_of = {op: n for n, op in enumerate(order)}
        last_slot = [slot_of[MAX_OPS[u][-1]] for u in range(NU)]

        def geometry(op):
            u, i, c, h = op
            t = UNITS[u][1]
            q0 = t * TILE + i * P
            m = min(P, S - q0)
            n = min(TILE, q0 + m - c * TILE)
            return q0, m, c * TILE, n, c * TILE + n == q0 + m

        with nc.Fori(0, B) as b:
            with nc.Block(no_gpsimd_drain=True) as block:
                @block.sync
                def _(sp):
                    def store(u):
                        g, t = UNITS[u]
                        sp.wait_ge(o_copied, u + 1)
                        for h in range(GH):
                            sp.dma_start(heads_out[b, g * GH + h][:, t * TILE:t * TILE + width[t]],
                                         out_sb[VW * h:VW * h + HD + 1, u % 2, 0:width[t]]).then_inc(o_stored[u % 2], 16)

                    for u, (g, t) in enumerate(UNITS):
                        if u == QT:
                            sp.wait_ge(g1_loaded, 16 * LOADS)
                        sp.wait_ge(rows_copied, u + 1)
                        for part in range(MAX_PARTS):
                            sp.dma_start(q_rows[ROWS + part:ROWS + part + 1, g, :, t * TILE:t * TILE + width[t]],
                                         max_rows[part * GH:(part + 1) * GH, u % 2, 0:width[t]]).then_inc(rows_set[u % 2], 16)
                        if u < QT - 2:
                            load_group(sp, b, 1, g1_loaded, u, QT - 2)
                        if u == QT + 2:
                            sp.wait_ge(o_ready, QT)
                        if u >= QT + 2:
                            load_group(sp, (b + 1) & (B - 1), 0, next_loaded, u - QT - 2, QT - 2)
                        if u >= 2:
                            store(u - 2)
                    sp.wait_ge(next_loaded, 16 * LOADS)
                    store(NU - 2)
                    store(NU - 1)
                    for half in range(2):
                        sp.wait_ge(o_stored[half], 16 * GH * (NU // 2))

                @block.vector
                def _(dve):
                    chained = [0]

                    def link(ins):
                        chained[0] += 1
                        ins.then_inc(chain, 1)
                        dve.wait_ge(chain, chained[0])

                    for n, op in enumerate(order):
                        dve.wait_ge(max_ready, n + 1)
                        if len(op) == 1:
                            u, = op
                            w = width[UNITS[u][1]]
                            if u >= 2:
                                dve.wait_ge(rows_set[u % 2], 16 * MAX_PARTS * (u // 2))
                            turned = max_scores[0:MAX_PARTS * GH, n % M_RING, :].bitcast(BF16)
                            nc.vector.tensor_copy(max_rows[:, u % 2, 0:w], turned[:, 0:w]).then_inc(rows_copied, 1)
                            dve.wait_ge(rows_copied, u + 1)
                            nc.vector.sem_inc(max_used, 1)
                            continue
                        u, i, c, h = op
                        _, m, _, keys, _ = geometry(op)
                        nc.vector.tensor_reduce(part_max[0:m, u % 2, i, h, c:c + 1], max_scores[0:m, n % M_RING, 0:keys],
                                                AX_X, ALU.max).then_inc(max_used, 1)
                        if n == last_slot[u]:
                            t = UNITS[u][1]
                            dve.wait_ge(max_used, n + 1)
                            if u >= 2:
                                dve.wait_ge(max_ready, slot_of[(u - 2,)] + 1)
                            link(nc.vector.tensor_reduce(row_max[:, u % 2], part_max[:, u % 2, :, :, 0:t + 1],
                                                         AX_X, ALU.max))
                            high = max_split[:, u % 2, :, 0, :]
                            link(nc.vector.tensor_copy(high, row_max[:, u % 2]))
                            nc.vector.tensor_tensor(max_split[:, u % 2, :, 1, :], row_max[:, u % 2], high,
                                                    ALU.subtract).then_inc(split_ready, 1)

                @block.scalar
                def _(act):
                    def copy_out(u):
                        w = width[UNITS[u][1]]
                        act.wait_ge(o_ready, u + 1)
                        if u >= 2:
                            act.wait_ge(o_stored[u % 2], 16 * GH * (u // 2))
                        nc.scalar.copy(out_sb[:, u % 2, 0:w], out_acc[:, u % 2, 0:w]).then_inc(o_copied, 1)

                    for k, (u, j) in enumerate(STEPS):
                        t = UNITS[u][1]
                        o = max(0, j - QB * t) * P
                        keys = min(P, S - j * P)
                        if k >= P_RING:
                            act.wait_ge(p_used, k - P_RING + 1)
                        for h in range(GH):
                            act.wait_ge(s_ready, GH * k + h + 1)
                            nc.scalar.activation(probs[0:keys, k % P_RING, h, o:width[t]],
                                                 scores[0:keys, (GH * k + h) % S_RING, o:width[t]], ACT.Exp,
                                                 scale=float(HD) ** -0.5).then_inc(p_ready, 1)
                        if u >= 1 and k == first_step[u] + 2:
                            copy_out(u - 1)
                    copy_out(NU - 1)

                @block.tensor
                def _(pe):
                    slots = [0]

                    def run_slot(op):
                        n = slots[0]
                        slots[0] += 1
                        if n >= M_RING:
                            pe.wait_ge(max_used, n - M_RING + 1)
                        u = op[0]
                        g, t = UNITS[u]
                        if len(op) == 1:
                            pe.wait_ge(split_ready, u + 1)
                            turned = max_scores[0:MAX_PARTS * GH, n % M_RING, :].bitcast(BF16)
                            for i in range(-(-width[t] // P)):
                                m = min(P, width[t] - i * P)
                                last = nc.tensor.transpose(turned[:, i * P:i * P + m],
                                                           max_split[0:m, u % 2, i].rearrange("p a h -> p (a h)"),
                                                           ident[0:m, 0:m])
                            last.then_inc(max_ready, 1)
                            return
                        _, i, c, h = op
                        q0, m, k0, keys, diagonal = geometry(op)
                        if u == QT and op == MAX_OPS[u][0]:
                            pe.wait_ge(g1_loaded, 16 * LOADS)
                        last = nc.tensor.matmul(max_scores[0:m, n % M_RING, 0:keys], q_rows[0:ROWS, g, h, q0:q0 + m],
                                                k_rows[0:ROWS, g, k0:k0 + keys], start=True, stop=not diagonal)
                        if diagonal:
                            last = nc.tensor.matmul(max_scores[0:m, n % M_RING, keys - m:keys], ident[0:m, 0:m],
                                                    mask_qk[0:m, 0:m], start=False, stop=True)
                        last.then_inc(max_ready, 1)

                    def score(k, h):
                        u, j = STEPS[k]
                        g, t = UNITS[u]
                        o = max(0, j - QB * t) * P
                        keys = min(P, S - j * P)
                        n = GH * k + h
                        if n >= S_RING:
                            pe.wait_ge(p_ready, n - S_RING + 1)
                        if k == first_step[u] and h == 0:
                            pe.wait_ge(rows_set[u % 2], 16 * MAX_PARTS * (u // 2 + 1))
                        diagonal = j >= QB * t
                        last = nc.tensor.matmul(scores[0:keys, n % S_RING, o:width[t]],
                                                k_rows[0:ROWS + MAX_PARTS, g, j * P:j * P + keys],
                                                q_rows[0:ROWS + MAX_PARTS, g, h, t * TILE + o:t * TILE + width[t]],
                                                start=True, stop=not diagonal)
                        if diagonal:
                            last = nc.tensor.matmul(scores[0:keys, n % S_RING, o:o + keys], ident[0:keys, 0:keys],
                                                    mask_kq[0:keys, 0:keys], start=False, stop=True)
                        last.then_inc(s_ready, 1)

                    def outputs(k):
                        u, j = STEPS[k]
                        g, t = UNITS[u]
                        o = max(0, j - QB * t) * P
                        keys = min(P, S - j * P)
                        pe.wait_ge(p_ready, GH * (k + 1))
                        if j == 0 and u >= 2:
                            pe.wait_ge(o_copied, u - 1)
                        end = k == first_step[u + 1] - 1
                        for h in range(GH):
                            v = h // 2
                            last = nc.tensor.matmul(out_acc[VW * h:VW * h + VW, u % 2, o:width[t]],
                                                    v_keys[0:keys, g, j, v * VW:(v + 1) * VW],
                                                    probs[0:keys, k % P_RING, h, o:width[t]],
                                                    start=(j == 0), stop=end)
                        last.then_inc(p_used, 1)
                        if end:
                            pe.wait_ge(p_used, k + 1)
                            nc.tensor.sem_inc(o_ready, 1)

                    for op in slots_at[0]:
                        run_slot(op)
                    for k in range(len(STEPS)):
                        ops = slots_at[k + 1]
                        cut = [len(ops) * x // 5 for x in range(6)]
                        for h in range(GH):
                            score(k, h)
                            for op in ops[cut[h]:cut[h + 1]]:
                                run_slot(op)
                        if k >= 1:
                            outputs(k - 1)
                        for op in ops[cut[4]:]:
                            run_slot(op)
                    outputs(len(STEPS) - 1)
            nc.all_engine_barrier(sem_only=True)
            for s in step_sems:
                nc.sync.sem_clear(s)
            nc.all_engine_barrier(sem_only=True)


def inverse_sums(nc, heads_out, inverse):
    with ExitStack() as ctx:
        sums = ctx.enter_context(nc.sbuf_tensor("sums", [P, B, NH * S // P], F32))
        inv = ctx.enter_context(nc.sbuf_tensor("inv", [P, B, NH * S // P], F32))
        loaded = ctx.enter_context(nc.semaphore("sums_loaded"))
        done = ctx.enter_context(nc.semaphore("sums_inverted"))
        stored = ctx.enter_context(nc.semaphore("inverses_stored"))
        with nc.Block(no_gpsimd_drain=True) as block:
            @block.sync
            def _(sp):
                per = P // NH
                for b in range(B):
                    for h in range(NH):
                        sp.dma_start(sums[h * per:(h + 1) * per, b, :],
                                     heads_out[b, h, HD].rearrange("(c n) -> c n", c=per)).then_inc(loaded, 16)
                sp.wait_ge(done, 1)
                for b in range(B):
                    sp.dma_start(inverse[b].rearrange("h (c n) -> (h c) n", c=per), inv[:, b, :]).then_inc(stored, 16)
                sp.wait_ge(stored, 16 * B)

            @block.vector
            def _(dve):
                dve.wait_ge(loaded, 16 * B * NH)
                nc.vector.reciprocal(inv[:], sums[:]).then_inc(done, 1)
                dve.wait_ge(done, 1)


def second_norm(nc, heads_out, inverse, h0_in, wo, wr, br, tables, normed_out, sum_out, weights_out):
    centre, mean = tables
    with ExitStack() as ctx:
        def sbuf(name, shape, dt=F32):
            return ctx.enter_context(nc.sbuf_tensor(name, shape, dt))

        def psum(name, shape):
            return ctx.enter_context(nc.psum_tensor(name, shape, F32))

        def sem(name):
            return ctx.enter_context(nc.semaphore(name))

        wo_sb = sbuf("wo_sb", [P, P])
        wr_sb = sbuf("wr_sb", [P, 2])
        br_sb = sbuf("br_sb", [2, 1])
        eps_sb = sbuf("eps2_sb", [P, 1])
        centre_sb = sbuf("centre2_sb", [P, P])
        mean_sb = sbuf("mean2_sb", [P, P])
        heads = sbuf("heads", [P, 2, TILE])
        inv = sbuf("inv_rows", [P, 2, TILE])
        h0 = sbuf("h0_tile", [P, 2, TILE])
        attn = sbuf("attn", [P, 2, TILE])
        h2 = sbuf("h2", [P, 2, TILE])
        square = sbuf("square2", [P, 2, TILE])
        std = sbuf("std2", [P, 2, TILE])
        rstd = sbuf("rstd2", [P, 2, TILE])
        normed = sbuf("normed2", [P, 2, TILE])
        total = sbuf("total", [P, 2, TILE])
        router = sbuf("router", [2, S])
        proj_ps = psum("proj2_ps", [P, 2, TILE])
        centred_ps = psum("centred2_ps", [P, 2, TILE])
        var_ps = psum("var2_ps", [P, 2, TILE])
        router_ps = psum("router_ps", [2, 2, TILE])

        const_in = sem("const2_loaded")
        with nc.Block(no_gpsimd_drain=True) as block:
            @block.sync
            def _(sp):
                pieces = [(wo_sb[:], wo), (wr_sb[:], wr), (br_sb[:], br), (centre_sb[:], centre), (mean_sb[:], mean)]
                for dst, src in pieces:
                    sp.dma_start(dst, src).then_inc(const_in, 16)
                sp.wait_ge(const_in, 16 * len(pieces) + 1)

            @block.vector
            def _(dve):
                nc.vector.memset(eps_sb[:], EPS).then_inc(const_in, 1)

        loaded = [sem("tile_loaded_even"), sem("tile_loaded_odd")]
        stored = [sem("tile_stored_even"), sem("tile_stored_odd")]
        attn_ready = sem("attn_ready")
        proj_ready = sem("proj2_ready")
        h2_ready = sem("h2_ready")
        centred = sem("centred2")
        squared = sem("squared2")
        var_ready = sem("var2_ready")
        std_ready = sem("std2_ready")
        rstd_ready = sem("rstd2_ready")
        normed_ready = sem("normed2_ready")
        total_ready = sem("total_ready")
        router_ready = sem("router_ready")
        router_set = sem("router_set")
        router_out = sem("router_stored")
        step_sems = [*loaded, *stored, attn_ready, proj_ready, h2_ready, centred, squared, var_ready, std_ready,
                     rstd_ready, normed_ready, total_ready, router_ready, router_set, router_out]
        NT = len(TILES)

        with nc.Fori(0, PAIRS) as p:
            with nc.Block(no_gpsimd_drain=True) as block:
                @block.sync
                def _(sp):
                    for m, (t0, w) in enumerate(TILES):
                        if m >= 2:
                            sp.wait_ge(attn_ready, m - 1)
                            sp.wait_ge(h2_ready, m - 1)
                        two = heads_out[bass.ds(2 * p, 2)].rearrange("b h r s -> (b h) r s")
                        sp.dma_start(heads[:, m % 2, 0:w], two[:, 0:HD, t0:t0 + w]).then_inc(loaded[m % 2], 16)
                        ones = inverse[bass.ds(2 * p, 2)].rearrange("b h s -> (b h) s")[:, None, t0:t0 + w]
                        sp.dma_start(inv[:, m % 2, 0:w], ones.to_broadcast([2 * NH, HD, w])).then_inc(loaded[m % 2], 16)
                        sp.dma_start(h0[:, m % 2, 0:w], h0_in[p][:, t0:t0 + w]).then_inc(loaded[m % 2], 16)

                @block.scalar
                def _(act):
                    def store(m):
                        t0, w = TILES[m]
                        act.wait_ge(normed_ready, m + 1)
                        act.dma_start(normed_out[p][:, t0:t0 + w], normed[:, m % 2, 0:w]).then_inc(stored[m % 2], 16)
                        act.wait_ge(total_ready, m + 1)
                        act.dma_start(sum_out[p][:, t0:t0 + w], total[:, m % 2, 0:w]).then_inc(stored[m % 2], 16)
                        act.wait_ge(router_ready, m + 1)
                        nc.scalar.activation(router[:, t0:t0 + w], router_ps[:, m % 2, 0:w], ACT.Identity,
                                             bias=br_sb[:]).then_inc(router_set, 1)

                    for m, (t0, w) in enumerate(TILES):
                        act.wait_ge(centred, m + 1)
                        if m >= 2:
                            act.wait_ge(var_ready, m - 1)
                        nc.scalar.activation(square[:, m % 2, 0:w], centred_ps[:, m % 2, 0:w], ACT.Square).then_inc(squared, 1)
                        act.wait_ge(var_ready, m + 1)
                        if m >= 2:
                            act.wait_ge(rstd_ready, m - 1)
                        nc.scalar.activation(std[:, m % 2, 0:w], var_ps[:, m % 2, 0:w], ACT.Sqrt,
                                             bias=eps_sb[:]).then_inc(std_ready, 1)
                        if m >= 1:
                            store(m - 1)
                    store(NT - 1)
                    act.wait_ge(router_set, NT)
                    act.dma_start(weights_out[bass.ds(2 * p, 2)], router[:]).then_inc(router_out, 16)
                    act.wait_ge(router_out, 16)
                    act.wait_ge(stored[0], 16 * 2 * ((NT + 1) // 2))
                    act.wait_ge(stored[1], 16 * 2 * (NT // 2))

                @block.gpsimd
                def _(pool):
                    for m in range(NT + 1):
                        if m < NT:
                            t0, w = TILES[m]
                            pool.wait_ge(loaded[m % 2], 16 * 3 * (m // 2 + 1))
                            if m >= 2:
                                pool.wait_ge(proj_ready, m - 1)
                            nc.gpsimd.tensor_tensor(attn[:, m % 2, 0:w], heads[:, m % 2, 0:w], inv[:, m % 2, 0:w],
                                                    ALU.mult).then_inc(attn_ready, 1)
                        if m >= 1:
                            w = TILES[m - 1][1]
                            pool.wait_ge(normed_ready, m)
                            pool.wait_ge(h2_ready, m)
                            if m >= 3:
                                pool.wait_ge(stored[(m - 1) % 2], 16 * 2 * ((m - 1) // 2))
                            nc.gpsimd.tensor_tensor(total[:, (m - 1) % 2, 0:w], normed[:, (m - 1) % 2, 0:w],
                                                    h2[:, (m - 1) % 2, 0:w], ALU.add).then_inc(total_ready, 1)

                @block.vector
                def _(dve):
                    def residual(m):
                        w = TILES[m][1]
                        dve.wait_ge(proj_ready, m + 1)
                        dve.wait_ge(loaded[m % 2], 16 * 3 * (m // 2 + 1))
                        if m >= 2:
                            dve.wait_ge(total_ready, m - 1)
                            dve.wait_ge(centred, m - 1)
                        nc.vector.tensor_tensor(h2[:, m % 2, 0:w], proj_ps[:, m % 2, 0:w], h0[:, m % 2, 0:w],
                                                ALU.add).then_inc(h2_ready, 1)

                    residual(0)
                    for m in range(NT):
                        w = TILES[m][1]
                        if m + 1 < NT:
                            residual(m + 1)
                        dve.wait_ge(std_ready, m + 1)
                        nc.vector.reciprocal(rstd[:, m % 2, 0:w], std[:, m % 2, 0:w]).then_inc(rstd_ready, 1)
                        dve.wait_ge(rstd_ready, m + 1)
                        dve.wait_ge(centred, m + 1)
                        if m >= 2:
                            dve.wait_ge(stored[m % 2], 16 * 2 * (m // 2))
                            dve.wait_ge(router_ready, m - 1)
                        nc.vector.tensor_tensor(normed[:, m % 2, 0:w], centred_ps[:, m % 2, 0:w], rstd[:, m % 2, 0:w],
                                                ALU.mult).then_inc(normed_ready, 1)

                @block.tensor
                def _(pe):
                    def project(m):
                        w = TILES[m][1]
                        pe.wait_ge(attn_ready, m + 1)
                        if m >= 2:
                            pe.wait_ge(h2_ready, m - 1)
                        nc.tensor.matmul(proj_ps[:, m % 2, 0:w], wo_sb[:], attn[:, m % 2, 0:w],
                                         start=True, stop=True).then_inc(proj_ready, 1)

                    def centre_tile(m):
                        w = TILES[m][1]
                        pe.wait_ge(h2_ready, m + 1)
                        if m >= 2:
                            pe.wait_ge(normed_ready, m - 1)
                        nc.tensor.matmul(centred_ps[:, m % 2, 0:w], centre_sb[:], h2[:, m % 2, 0:w],
                                         start=True, stop=True).then_inc(centred, 1)

                    project(0)
                    project(1)
                    centre_tile(0)
                    for m in range(NT):
                        w = TILES[m][1]
                        if m + 1 < NT:
                            centre_tile(m + 1)
                        pe.wait_ge(squared, m + 1)
                        if m >= 2:
                            pe.wait_ge(std_ready, m - 1)
                        nc.tensor.matmul(var_ps[:, m % 2, 0:w], mean_sb[:], square[:, m % 2, 0:w],
                                         start=True, stop=True).then_inc(var_ready, 1)
                        if m + 2 < NT:
                            project(m + 2)
                        pe.wait_ge(normed_ready, m + 1)
                        if m >= 2:
                            pe.wait_ge(router_set, m - 1)
                        nc.tensor.matmul(router_ps[:, m % 2, 0:w], wr_sb[:], normed[:, m % 2, 0:w],
                                         start=True, stop=True).then_inc(router_ready, 1)
            nc.all_engine_barrier(sem_only=True)
            for s in step_sems:
                nc.sync.sem_clear(s)
            nc.all_engine_barrier(sem_only=True)


def select(nc, weights_in, batch_sum, batch_before, chosen_out):
    with ExitStack() as ctx:
        def sbuf(name, shape, dt=F32):
            return ctx.enter_context(nc.sbuf_tensor(name, shape, dt))

        def sem(name):
            return ctx.enter_context(nc.semaphore(name))

        I32 = mybir.dt.int32
        w = sbuf("weights", [P, SPAN])
        v = sbuf("signed_weights", [P, SPAN])
        ones_block = sbuf("batch_sum_sb", [P, P])
        before_block = sbuf("batch_before_sb", [P, P])
        flags = sbuf("flags", [P, SPAN])
        equal = sbuf("equal", [P, SPAN])
        above = sbuf("above", [P, SPAN])
        rank = sbuf("rank", [P, SPAN])
        zeros = sbuf("zeros", [P, SPAN])
        chosen = sbuf("chosen", [P, SPAN])
        count = sbuf("count", [P, 2])
        level = sbuf("level", [P, 1], I32)
        trial = sbuf("trial", [P, 1], I32)
        keep = sbuf("keep", [P, 1], I32)
        positive = sbuf("positive", [P, 1])
        sign = sbuf("sign", [P, 1])
        wanted = sbuf("wanted", [P, 1])
        threshold = sbuf("threshold", [P, 1])
        room = sbuf("room", [P, 1])
        count_ps = ctx.enter_context(nc.psum_tensor("count_ps", [P, 2], F32))
        loaded = sem("weights_in")
        chain = sem("select_steps")
        counted = sem("counted")
        summed = sem("summed")
        stored = sem("chosen_stored")
        BITS = 31

        with nc.Block(no_gpsimd_drain=True) as block:
            @block.sync
            def _(sp):
                sp.dma_start(w[:], weights_in.rearrange("b (c n) -> (b c) n", c=ROWS_PER_BATCH)).then_inc(loaded, 16)
                sp.dma_start(ones_block[:], batch_sum).then_inc(loaded, 16)
                sp.dma_start(before_block[:], batch_before).then_inc(loaded, 16)
                sp.wait_ge(counted, BITS + 3)
                sp.dma_start(chosen_out.rearrange("b (c n) -> (b c) n", c=ROWS_PER_BATCH), chosen[:]).then_inc(stored, 16)
                sp.wait_ge(stored, 16)

            @block.tensor
            def _(pe):
                pe.wait_ge(loaded, 48)
                for n in range(BITS + 1):
                    pe.wait_ge(counted, n + 1)
                    nc.tensor.matmul(count_ps[:, 0:1], ones_block[:], count[:, 0:1], start=True, stop=True).then_inc(summed, 1)
                pe.wait_ge(counted, BITS + 2)
                nc.tensor.matmul(count_ps[:, 0:1], ones_block[:], count[:, 0:1], start=True, stop=True)
                nc.tensor.matmul(count_ps[:, 1:2], before_block[:], count[:, 1:2], start=True, stop=True).then_inc(summed, 1)

            @block.vector
            def _(dve):
                steps = [0]

                def link(ins):
                    steps[0] += 1
                    ins.then_inc(chain, 1)
                    dve.wait_ge(chain, steps[0])

                link(nc.vector.memset(level[:], 0))
                link(nc.vector.memset(zeros[:], 0.0))
                dve.wait_ge(loaded, 48)
                nc.vector.tensor_scalar(flags[:], w[:], 0.0, 0.0, ALU.is_ge, ALU.add, accum_out=count[:, 0:1]).then_inc(counted, 1)
                dve.wait_ge(summed, 1)
                link(nc.vector.tensor_scalar(positive[:], count_ps[:, 0:1], float(TOP), None, ALU.is_ge))
                link(nc.vector.tensor_scalar(sign[:], positive[:], 2.0, -1.0, ALU.mult, ALU.add))
                link(nc.vector.tensor_scalar(wanted[:], positive[:], float(2 * TOP - S - 1), float(S - TOP + 1), ALU.mult, ALU.add))
                link(nc.vector.tensor_scalar(v[:], w[:], sign[:], None, ALU.mult))
                for n in range(BITS):
                    link(nc.vector.tensor_scalar(trial[:], level[:], 1 << (BITS - 1 - n), None, ALU.bitwise_or))
                    nc.vector.tensor_scalar(flags[:], v[:], trial[:].bitcast(F32), 0.0, ALU.is_ge, ALU.add,
                                            accum_out=count[:, 0:1]).then_inc(counted, 1)
                    dve.wait_ge(summed, n + 2)
                    link(nc.vector.tensor_scalar(keep[:], count_ps[:, 0:1], wanted[:], None, ALU.is_ge))
                    link(nc.vector.copy_predicated(level[:], keep[:], trial[:]))
                link(nc.vector.tensor_scalar(threshold[:], level[:].bitcast(F32), sign[:], None, ALU.mult))
                link(nc.vector.tensor_scalar(equal[:], w[:], threshold[:], None, ALU.is_equal))
                link(nc.vector.tensor_scalar(above[:], w[:], threshold[:], 0.0, ALU.is_gt, ALU.add, accum_out=count[:, 0:1]))
                link(nc.vector.tensor_tensor_scan(rank[:], equal[:], zeros[:], 0.0, ALU.add, ALU.add))
                nc.vector.tensor_copy(count[:, 1:2], rank[:, SPAN - 1:SPAN]).then_inc(counted, 1)
                dve.wait_ge(summed, BITS + 2)
                link(nc.vector.tensor_scalar(room[:], count_ps[:, 0:1], -1.0, float(TOP), ALU.mult, ALU.add))
                link(nc.vector.tensor_tensor(room[:], room[:], count_ps[:, 1:2], ALU.subtract))
                link(nc.vector.scalar_tensor_tensor(out=flags[:], in0=rank[:], scalar=room[:], in1=equal[:],
                                                    op0=ALU.is_le, op1=ALU.mult))
                link(nc.vector.tensor_tensor(above[:], above[:], flags[:], ALU.add))
                nc.vector.tensor_tensor(chosen[:], w[:], above[:], ALU.mult).then_inc(counted, 1)


def feed_forward(nc, normed_in, sum_in, chosen_in, ff_w, ff_b, identity, out):
    w1, w2 = ff_w
    b1, b2 = ff_b
    with ExitStack() as ctx:
        def sbuf(name, shape, dt=F32):
            return ctx.enter_context(nc.sbuf_tensor(name, shape, dt))

        def psum(name, shape):
            return ctx.enter_context(nc.psum_tensor(name, shape, F32))

        def sem(name):
            return ctx.enter_context(nc.semaphore(name))

        w1_sb = sbuf("ff_w1_sb", [P, CHUNKS, P])
        w2_sb = sbuf("ff_w2_sb", [P, 2, C])
        b1_sb = sbuf("ff_b1_sb", [P, 2])
        b2_sb = sbuf("ff_b2_sb", [P, 1])
        ident_sb = sbuf("ident3_sb", [P, P])
        normed = sbuf("normed3", [P, 2, TILE])
        total = sbuf("total3", [P, 2, TILE])
        chosen = sbuf("chosen3", [P, 2, TILE])
        hidden = sbuf("hidden3", [P, 2, CHUNKS, TILE])
        scaled = sbuf("scaled3", [P, 2, TILE])
        final = sbuf("final3", [P, 2, TILE])
        turned = sbuf("turned3", [P, 2, TILE // P, P])
        hidden_ps = psum("hidden3_ps", [P, CHUNKS, TILE])
        y_ps = psum("y3_ps", [P, 2, TILE])
        turned_ps = psum("turned3_ps", [P, 2, TILE // P, P])

        const_in = sem("const3_loaded")
        with nc.Block(no_gpsimd_drain=True) as block:
            @block.sync
            def _(sp):
                pieces = [(w1_sb[:].rearrange("p c m -> p (c m)"), w1), (w2_sb[:].rearrange("p c m -> p (c m)"), w2),
                          (b1_sb[:], b1), (b2_sb[:], b2), (ident_sb[:], identity)]
                for dst, src in pieces:
                    sp.dma_start(dst, src).then_inc(const_in, 16)
                sp.wait_ge(const_in, 16 * len(pieces))

        loaded = [sem("tile3_loaded_even"), sem("tile3_loaded_odd")]
        hidden_ready = sem("hidden3_ready")
        gelu_ready = sem("gelu_ready")
        y_ready = sem("y3_ready")
        scaled_ready = sem("scaled_ready")
        final_ready = sem("final_ready")
        turned_ready = sem("turned3_ready")
        turned_set = sem("turned3_set")
        stored = [sem("out3_stored_even"), sem("out3_stored_odd")]
        step_sems = [*loaded, hidden_ready, gelu_ready, y_ready, scaled_ready, final_ready, turned_ready,
                     turned_set, *stored]
        NT = len(TILES)

        def stores(m):
            w = TILES[m][1]
            return 2 * ((w >= P) + (w % P > 0))

        def stored_by(m, half):
            return 16 * sum(stores(n) for n in range(m) if n % 2 == half)

        with nc.Fori(0, PAIRS) as p:
            with nc.Block(no_gpsimd_drain=True) as block:
                @block.sync
                def _(sp):
                    def store(m):
                        t0, w = TILES[m]
                        sp.wait_ge(turned_set, m + 1)
                        k, rest = divmod(w, P)
                        for e in range(2):
                            rows = out[bass.ds(2 * p + e, 1)].rearrange("o s c -> (o s) c")
                            sp.dma_start(rows[t0:t0 + k * P].rearrange("(k p) c -> p k c", p=P),
                                         turned[:, m % 2, 0:k, e * C:(e + 1) * C]).then_inc(stored[m % 2], 16)
                            if rest:
                                sp.dma_start(rows[t0 + k * P:t0 + w],
                                             turned[0:rest, m % 2, k, e * C:(e + 1) * C]).then_inc(stored[m % 2], 16)

                    for m, (t0, w) in enumerate(TILES):
                        if m >= 2:
                            sp.wait_ge(hidden_ready, CHUNKS * (m - 1))
                            sp.wait_ge(final_ready, m - 1)
                        sp.dma_start(normed[:, m % 2, 0:w], normed_in[p][:, t0:t0 + w]).then_inc(loaded[m % 2], 16)
                        sp.dma_start(total[:, m % 2, 0:w], sum_in[p][:, t0:t0 + w]).then_inc(loaded[m % 2], 16)
                        rows = chosen_in[bass.ds(2 * p, 2)][:, None, t0:t0 + w]
                        sp.dma_start(chosen[:, m % 2, 0:w], rows.to_broadcast([2, C, w])).then_inc(loaded[m % 2], 16)
                        if m >= 3:
                            store(m - 3)
                    for m in range(NT - 3, NT):
                        store(m)
                    for half in range(2):
                        sp.wait_ge(stored[half], stored_by(NT, half))

                @block.tensor
                def _(pe):
                    def turn(m):
                        w = TILES[m][1]
                        pe.wait_ge(final_ready, m + 1)
                        if m >= 2:
                            pe.wait_ge(turned_set, m - 1)
                        for k in range(-(-w // P)):
                            n = min(P, w - k * P)
                            last = nc.tensor.transpose(turned_ps[0:n, m % 2, k], final[:, m % 2, k * P:k * P + n],
                                                       ident_sb[:])
                        last.then_inc(turned_ready, 1)

                    def second(m):
                        w = TILES[m][1]
                        if m >= 2:
                            pe.wait_ge(scaled_ready, m - 1)
                        for half in range(2):
                            for e in range(2):
                                pe.wait_ge(gelu_ready, CHUNKS * m + 2 * e + half + 1)
                                last = nc.tensor.matmul(y_ps[e * C:(e + 1) * C, m % 2, 0:w], w2_sb[:, half],
                                                        hidden[:, m % 2, 2 * e + half, 0:w],
                                                        start=(half == 0), stop=(half == 1))
                        last.then_inc(y_ready, 1)

                    for m in range(NT):
                        w = TILES[m][1]
                        pe.wait_ge(loaded[m % 2], 16 * 3 * (m // 2 + 1))
                        for c in range(CHUNKS):
                            if m >= 1:
                                pe.wait_ge(gelu_ready, CHUNKS * (m - 1) + c + 1)
                            nc.tensor.matmul(hidden_ps[:, c, 0:w], w1_sb[:, c], normed[:, m % 2, 0:w],
                                             start=True, stop=True).then_inc(hidden_ready, 1)
                        if m >= 1:
                            second(m - 1)
                        if m >= 2:
                            turn(m - 2)
                    second(NT - 1)
                    turn(NT - 2)
                    turn(NT - 1)

                @block.scalar
                def _(act):
                    def copy_turned(m):
                        w = TILES[m][1]
                        act.wait_ge(turned_ready, m + 1)
                        if m >= 2:
                            act.wait_ge(stored[m % 2], stored_by(m, m % 2))
                        k, rest = divmod(w, P)
                        last = nc.scalar.copy(turned[:, m % 2, 0:k], turned_ps[:, m % 2, 0:k])
                        if rest:
                            last = nc.scalar.copy(turned[0:rest, m % 2, k], turned_ps[0:rest, m % 2, k])
                        last.then_inc(turned_set, 1)

                    for m in range(NT):
                        w = TILES[m][1]
                        for c in range(CHUNKS):
                            act.wait_ge(hidden_ready, CHUNKS * m + c + 1)
                            if m >= 2:
                                act.wait_ge(y_ready, m - 1)
                            nc.scalar.activation(hidden[:, m % 2, c, 0:w], hidden_ps[:, c, 0:w], ACT.Gelu_apprx_tanh,
                                                 bias=b1_sb[:, c % 2:c % 2 + 1]).then_inc(gelu_ready, 1)
                        if m >= 3:
                            copy_turned(m - 3)
                    for m in range(NT - 3, NT):
                        copy_turned(m)

                @block.vector
                def _(dve):
                    for m in range(NT):
                        w = TILES[m][1]
                        dve.wait_ge(y_ready, m + 1)
                        dve.wait_ge(loaded[m % 2], 16 * 3 * (m // 2 + 1))
                        nc.vector.scalar_tensor_tensor(out=scaled[:, m % 2, 0:w], in0=y_ps[:, m % 2, 0:w], scalar=b2_sb[:],
                                                       in1=chosen[:, m % 2, 0:w], op0=ALU.add,
                                                       op1=ALU.mult).then_inc(scaled_ready, 1)
                        dve.wait_ge(scaled_ready, m + 1)
                        if m >= 2:
                            dve.wait_ge(turned_ready, m - 1)
                        nc.vector.tensor_tensor(final[:, m % 2, 0:w], scaled[:, m % 2, 0:w], total[:, m % 2, 0:w],
                                                ALU.add).then_inc(final_ready, 1)
            nc.all_engine_barrier(sem_only=True)
            for s in step_sems:
                nc.sync.sem_clear(s)
            nc.all_engine_barrier(sem_only=True)


def program(nc, a, out):
    def scratch(name, shape, dt=F32):
        return nc.dram_tensor(name, shape, dt, kind="Internal").ap()

    h0 = scratch("h0_dram", (PAIRS, P, S))
    q_parts = scratch("q_parts_dram", (PARTS, B, NH * HD, S), BF16)
    k_parts = scratch("k_parts_dram", (PARTS, B, KV * HD, S), BF16)
    v_blocks = scratch("v_blocks_dram", (B, GROUPS, P, KB * GKV * VW))
    heads = scratch("heads_dram", (B, NH, HD + 1, S))
    inverse = scratch("inverse_dram", (B, NH, S))
    normed = scratch("normed_dram", (PAIRS, P, S))
    total = scratch("total_dram", (PAIRS, P, S))
    weights = scratch("weights_dram", (B, S))
    chosen = scratch("chosen_dram", (B, S))
    tokens(nc, a["x"], a["txt"], (a["w1"], a["w2"], a["w3"]), (a["b1"], a["b2"], a["b3"]),
           (a["wq"], a["wq_turned"], a["wk"], a["wk_turned"], a["wv"]),
           (a["centre"], a["mean"], a["cos"], a["sin"], a["identity"]), h0, q_parts, k_parts, v_blocks)
    attention(nc, q_parts, k_parts, v_blocks, a["masks"], heads)
    inverse_sums(nc, heads, inverse)
    second_norm(nc, heads, inverse, h0, a["wo"], a["wr"], a["br"], (a["centre"], a["mean"]), normed, total, weights)
    select(nc, weights, a["batch_sum"], a["batch_before"], chosen)
    feed_forward(nc, normed, total, chosen, (a["ff_w1"], a["ff_w2"]), (a["ff_b1"], a["ff_b2"]), a["identity"], out)


def arranged(i):
    import numpy as np

    def two(w):
        k, m = w.shape
        o = np.zeros((2 * k, 2 * m), w.dtype)
        o[:k, :m] = w
        o[k:, m:] = w
        return o

    def by_shift(w):
        return np.ascontiguousarray(np.stack([two(w[:, s, :]) for s in range(SHIFTS)], 1).reshape(P, SHIFTS * P))

    def both(b):
        return np.ascontiguousarray(np.concatenate([b.reshape(C, -1)] * 2, 0))

    turn = np.arange(NH * HD).reshape(NH, 2, HD // 2)[:, ::-1].reshape(NH * HD)
    wq, wk, wv = i["L0_attn_Wq"], i["L0_attn_Wk"], i["L0_attn_Wv"]
    inv_freq = (1.0 / 10000.0 ** (np.arange(0, HD, 2, dtype=np.float32) / np.float32(HD))).astype(np.float32)
    angle = np.outer(np.arange(S, dtype=np.float32), inv_freq).astype(np.float32)
    angle = np.concatenate([angle, angle], -1)
    sign = np.where(np.arange(HD) < HD // 2, -1, 1).astype(np.float32)
    mean = two(np.full((C, C), 1 / C, np.float32))
    at = np.arange(P)
    after = np.where(at[:, None] > at[None, :], -3e38, 0).astype(np.float32)
    same = at[:, None] // ROWS_PER_BATCH == at[None, :] // ROWS_PER_BATCH
    ff_w1 = np.zeros((2, C, CHUNKS, P), np.float32)
    for e in range(2):
        for half in range(2):
            ff_w1[e, :, 2 * e + half] = i["L0_ffn_w1"][:, half * P:(half + 1) * P]
    return {
        "x": i["x"].reshape(PAIRS, P, IMG),
        "txt": i["txt"].reshape(PAIRS, 2, TXT, C),
        "w1": by_shift(i["L0_tok_W1"].reshape(C, SHIFTS, C)),
        "w2": by_shift(i["L0_tok_W2"].reshape(C, C, SHIFTS).transpose(0, 2, 1)),
        "w3": by_shift(i["L0_tok_W3"].reshape(C, SHIFTS, C)),
        "b1": both(i["L0_tok_b1"]),
        "b2": both(i["L0_tok_b2"]),
        "b3": both(i["L0_tok_b3"]),
        "wq": two(wq.T),
        "wq_turned": two(wq[turn].T),
        "wk": two(wk.T),
        "wk_turned": two(wk[turn[:KV * HD]].T),
        "wv": two(wv.T),
        "wo": two(i["L0_attn_Wo"].T),
        "wr": two(i["L0_ffn_wr"]),
        "br": np.concatenate([i["L0_ffn_br"].reshape(1, 1)] * 2, 0),
        "ff_w1": ff_w1.reshape(P, CHUNKS * P),
        "ff_w2": np.ascontiguousarray(i["L0_ffn_w2"].reshape(2, P, C).transpose(1, 0, 2).reshape(P, 2 * C)),
        "ff_b1": np.ascontiguousarray(i["L0_ffn_b1"].reshape(2, P).T),
        "ff_b2": both(i["L0_ffn_b2"]),
        "centre": np.eye(P, dtype=np.float32) - mean,
        "mean": mean,
        "cos": np.ascontiguousarray(np.tile(np.cos(angle).T, (P // HD, 1))),
        "sin": np.ascontiguousarray(np.tile((np.sin(angle) * sign).T, (P // HD, 1))),
        "identity": np.eye(P, dtype=np.float32),
        "masks": np.stack([after, after.T, np.eye(P, dtype=np.float32)]),
        "batch_sum": same.astype(np.float32),
        "batch_before": (same & (at[:, None] < at[None, :])).astype(np.float32),
    }


def kernel(**inputs):
    import numpy as np
    import concourse.bacc as bacc
    from concourse.bass_utils import run_bass_kernel_spmd

    nc = bacc.Bacc("TRN2", target_bir_lowering=False, num_devices=1)
    arrays, aps = {}, {}
    for name, array in arranged({k: np.asarray(v) for k, v in inputs.items()}).items():
        arrays["in_" + name] = np.ascontiguousarray(array)
        aps[name] = nc.dram_tensor("in_" + name, array.shape, mybir.dt.from_np(array.dtype), kind="ExternalInput").ap()
    out = nc.dram_tensor("out_0", (B, S, C), F32, kind="ExternalOutput").ap()
    program(nc, aps, out)
    r = run_bass_kernel_spmd(nc, [arrays], core_ids=[0])
    return r.results[0]["out_0"]
```

```python
from contextlib import ExitStack

import concourse.bass as bass
from concourse import mybir

ALU = mybir.AluOpType
ACT = mybir.ActivationFunctionType
F32 = mybir.dt.float32
BF16 = mybir.dt.bfloat16
U32 = mybir.dt.uint32
AX_X = mybir.AxisListType.X

P = 128
TILE = 512
B, C, H, W = 8, 64, 56, 56
IMG = H * W
TXT = 128
S = IMG + TXT
NH, KV, HD = 8, 4, 8
GROUPS = 2
GH = NH // GROUPS
GKV = KV // GROUPS
KB = -(-S // P)
QB = TILE // P
Q_TILES = [(0, TILE // 2)] + [(t0, min(TILE, S - t0)) for t0 in range(TILE // 2, S, TILE)]
QT = len(Q_TILES)
VW = 32
HEAD_ROWS = 6 * HD
ROWS = GKV * HEAD_ROWS
MAX_PARTS = 2
Q_TERM = (0, 0, 0, 1, 1, 2)
K_TERM = (0, 1, 2, 0, 1, 0)
P_RING = 3
S_RING = 3
M_RING = 3
PAIRS = B // 2
KS = 3
SHIFTS = KS * KS
PH, PW = H + 2, W + 2
IMG_ROWS = 8
CT = IMG_ROWS * W
CTILES = H // IMG_ROWS
PARTS = 3
TERMS = len(Q_TERM)
VB = 8
EPS = 1e-5
TOP = S // 2 - 1
ROWS_PER_BATCH = P // B
SPAN = S // ROWS_PER_BATCH
FF = 4 * C
CHUNKS = 2 * FF // P
RING = 4
TILES = [(t0, min(TILE, S - t0)) for t0 in range(0, S, TILE)]


def tokens(nc, x, txt, conv_w, conv_b, proj_w, tables, h0_out, q_terms, k_terms, v_blocks):
    w1, w2, w3 = conv_w
    b1, b2, b3 = conv_b
    wq, wq_turned, wk, wk_turned, wv = proj_w
    centre, mean, cos, sin, identity = tables
    with ExitStack() as ctx:
        def sbuf(name, shape, dt=F32):
            return ctx.enter_context(nc.sbuf_tensor(name, shape, dt))

        def psum(name, shape):
            return ctx.enter_context(nc.psum_tensor(name, shape, F32))

        def sem(name):
            return ctx.enter_context(nc.semaphore(name))

        x_in = sbuf("x_in", [P, IMG])
        x_pad = sbuf("x_pad", [P, PH, PW])
        txt_in = sbuf("txt_in", [TXT, P])
        w1_sb = sbuf("w1_sb", [P, SHIFTS, P])
        w2_sb = sbuf("w2_sb", [P, SHIFTS, P])
        w3_sb = sbuf("w3_sb", [P, SHIFTS, P])
        wq_sb = sbuf("wq_sb", [P, 2, P])
        wk_sb = sbuf("wk_sb", [P, 2, C])
        wv_sb = sbuf("wv_sb", [P, C])
        b1_sb = sbuf("b1_sb", [P, 1])
        b2_sb = sbuf("b2_sb", [P, SHIFTS])
        b3_sb = sbuf("b3_sb", [P, 1])
        eps_sb = sbuf("eps_sb", [P, 1])
        centre_sb = sbuf("centre_sb", [P, P])
        mean_sb = sbuf("mean_sb", [P, P])
        ident_sb = sbuf("ident_sb", [P, P])
        cos_sb = sbuf("cos_sb", [P, S])
        sin_sb = sbuf("sin_sb", [P, S])
        h1 = sbuf("h1", [P, CT])
        gate = sbuf("gate", [P, 2, CT])
        gated = sbuf("gated", [P, 2, CT])
        h0 = sbuf("h0", [P, S])
        square = sbuf("square", [P, CT])
        std = sbuf("std", [P, CT])
        rstd = sbuf("rstd", [P, CT])
        normed = sbuf("normed", [P, S])
        rot = sbuf("rot", [P, 4, CT])
        full = sbuf("full", [P, 2, CT])
        rest = sbuf("rest", [P, 2, CT])
        q_st = sbuf("q_st", [P, 2, PARTS, CT], BF16)
        k_st = sbuf("k_st", [C, 2, PARTS, CT], BF16)
        v_st = sbuf("v_st", [P, 2, GROUPS, KB, GKV, VW])

        hidden_ps = psum("hidden_ps", [P, 1, TILE])
        gate_ps = psum("gate_ps", [P, 2, TILE])
        token_ps = psum("token_ps", [P, 1, TILE])
        norm_ps = psum("norm_ps", [P, 2, TILE])
        proj_ps = psum("proj_ps", [P, 2, TILE])

        loaded = sem("weights_loaded")
        prepared = sem("weights_prepared")
        x_next = sem("x_next")

        def load_pair(eng, p, done):
            eng.dma_start(x_in[:], x[p]).then_inc(done, 16)
            eng.dma_start(txt_in[:], txt[p].rearrange("b t c -> t b c")).then_inc(done, 16)

        with nc.Block(no_gpsimd_drain=True) as block:
            @block.sync
            def _(sp):
                load_pair(sp, 0, loaded)
                pieces = [(w1_sb[:].rearrange("p s c -> p (s c)"), w1), (w2_sb[:].rearrange("p s c -> p (s c)"), w2),
                          (w3_sb[:].rearrange("p s c -> p (s c)"), w3), (b1_sb[:], b1), (b2_sb[:], b2), (b3_sb[:], b3),
                          (wq_sb[:, 0], wq), (wq_sb[:, 1], wq_turned), (wk_sb[:, 0], wk), (wk_sb[:, 1], wk_turned),
                          (wv_sb[:], wv), (centre_sb[:], centre), (mean_sb[:], mean), (ident_sb[:], identity),
                          (cos_sb[:], cos), (sin_sb[:], sin)]
                for dst, src in pieces:
                    sp.dma_start(dst, src).then_inc(loaded, 16)
                sp.wait_ge(loaded, 16 * (2 + len(pieces)))

            @block.vector
            def _(dve):
                nc.vector.memset(x_pad[:], 0.0).then_inc(prepared, 1)
                nc.vector.memset(eps_sb[:], EPS).then_inc(prepared, 1)
                dve.wait_ge(loaded, 16 * 18)
                nc.vector.tensor_scalar(b2_sb[:], b2_sb[:], 0.5, None, ALU.mult).then_inc(prepared, 1)
                nc.vector.tensor_scalar(w3_sb[:], w3_sb[:], 0.5, None, ALU.mult).then_inc(prepared, 1)
                dve.wait_ge(prepared, 4)

            @block.gpsimd
            def _(pool):
                v_ready = prepared
                nc.gpsimd.memset(v_st[:], 0.0).then_inc(x_next, 1)
                pool.wait_ge(x_next, 1)
                nc.gpsimd.memset(v_st[:].rearrange("p e g k v w -> p (e g k v) w")[:, :, HD:HD + 1], 1.0).then_inc(x_next, 1)
                pool.wait_ge(x_next, 2)

        x_padded = sem("x_padded")
        txt_turned = sem("txt_turned")
        reload = sem("next_pair_loaded")
        hidden_ready = sem("hidden_ready")
        h1_ready = sem("h1_ready")
        gate_ready = sem("gate_ready")
        tanh_ready = sem("tanh_ready")
        gated_ready = sem("gated_ready")
        gated_used = sem("gated_used")
        token_ready = sem("token_ready")
        h0_ready = sem("h0_ready")
        centred = sem("centred")
        squared = sem("squared")
        var_ready = sem("var_ready")
        std_ready = sem("std_ready")
        rstd_ready = sem("rstd_ready")
        normed_ready = sem("normed_ready")
        proj_ready = sem("proj_ready")
        proj_used = sem("proj_used")
        rot_ready = sem("rot_ready")
        full_ready = sem("full_ready")
        high_ready = sem("high_ready")
        rest_ready = sem("rest_ready")
        mid_ready = sem("mid_ready")
        low_ready = sem("low_ready")
        parts_stored = [sem("parts_stored_even"), sem("parts_stored_odd")]
        v_set = sem("v_set")
        stored = sem("pair_stored")
        step_sems = [x_padded, txt_turned, reload, hidden_ready, h1_ready, gate_ready, tanh_ready, gated_ready,
                     gated_used, token_ready, h0_ready, centred, squared, var_ready, std_ready, rstd_ready,
                     normed_ready, proj_ready, proj_used, rot_ready, full_ready, high_ready, rest_ready, mid_ready,
                     low_ready, *parts_stored, v_set, stored, x_next]

        POST = [(IMG, TXT)] + [(n * CT, CT) for n in range(CTILES)]
        NPOST = len(POST)
        V_GROUPS = [range(v, min(v + VB, KB)) for v in range(0, KB, VB)]
        V_AT = {4: [0], 6: [1], NPOST: [2, 3]}
        slots = []
        for m in range(NPOST + 1):
            slots += [("v", v) for v in V_AT.get(m, [])]
            if m < NPOST:
                slots += [("q", m, 0), ("q", m, 1), ("k", m, 0), ("k", m, 1)]
        slot_of = {op: n for n, op in enumerate(slots)}

        with nc.Fori(0, PAIRS) as p:
            with nc.Block(no_gpsimd_drain=True) as block:
                @block.sync
                def _(sp):
                    sp.wait_ge(x_padded, 1)
                    sp.wait_ge(txt_turned, 1)
                    load_pair(sp, (p + 1) & (PAIRS - 1), reload)
                    def store_values(m):
                        for v in V_AT.get(m, []):
                            sp.wait_ge(v_set, v + 1)
                            k = V_GROUPS[v]
                            for e in range(2):
                                for g in range(GROUPS):
                                    dst = v_blocks[bass.ds(2 * p + e, 1), g].rearrange("b p (k v) -> p (b k) v", v=GKV * VW)
                                    sp.dma_start(dst[:, k[0]:k[-1] + 1],
                                                 v_st[:, e, g, k[0]:k[-1] + 1].rearrange("p k v w -> p k (v w)")).then_inc(stored, 16)

                    for m, (t0, w) in enumerate(POST):
                        sp.wait_ge(h0_ready, m + 1)
                        sp.dma_start(h0_out[p][:, t0:t0 + w], h0[:, t0:t0 + w]).then_inc(stored, 16)
                        store_values(m)
                        sp.wait_ge(low_ready, 2 * m + 2)
                        sp.wait_ge(high_ready, 2 * m + 2)
                        sp.wait_ge(mid_ready, 2 * m + 2)
                        for term in range(TERMS):
                            for dst, st, part in ((q_terms, q_st, Q_TERM[term]), (k_terms, k_st, K_TERM[term])):
                                rows = dst[bass.ds(2 * p, 2)].rearrange("b h r s -> (b h) r s")
                                sp.dma_start(rows[:, term * HD:(term + 1) * HD, t0:t0 + w],
                                             st[:, m % 2, part, 0:w]).then_inc(parts_stored[m % 2], 16)
                    store_values(NPOST)
                    sp.wait_ge(stored, 16 * (NPOST + 2 * GROUPS * len(V_GROUPS)))
                    sp.wait_ge(reload, 32)
                    for half in range(2):
                        sp.wait_ge(parts_stored[half], 16 * 2 * TERMS * (NPOST // 2))

                @block.tensor
                def _(pe):
                    def post(m, stage):
                        t0, w = POST[m]
                        if stage == 0:
                            pe.wait_ge(h0_ready, m + 1)
                            if m >= 1:
                                pe.wait_ge(normed_ready, m)
                            nc.tensor.matmul(norm_ps[:, 0, 0:w], centre_sb[:], h0[:, t0:t0 + w],
                                             start=True, stop=True).then_inc(centred, 1)
                        elif stage == 1:
                            pe.wait_ge(squared, m + 1)
                            nc.tensor.matmul(norm_ps[:, 1, 0:w], mean_sb[:], square[:, 0:w],
                                             start=True, stop=True).then_inc(var_ready, 1)
                        else:
                            which, rows, w_sb = (("q", P, wq_sb), ("k", C, wk_sb))[stage - 2]
                            pe.wait_ge(normed_ready, m + 1)
                            for turned in range(2):
                                n = slot_of[(which, m, turned)]
                                if n >= 2:
                                    pe.wait_ge(proj_used, n - 1)
                                nc.tensor.matmul(proj_ps[0:rows, n % 2, 0:w], w_sb[:, turned], normed[:, t0:t0 + w],
                                                 start=True, stop=True).then_inc(proj_ready, 1)

                    def values(m):
                        for v in V_AT.get(m, []):
                            n = slot_of[("v", v)]
                            pe.wait_ge(proj_used, n - 1)
                            for i, kb in enumerate(V_GROUPS[v]):
                                rows = min(P, S - kb * P)
                                last = nc.tensor.matmul(proj_ps[0:rows, n % 2, i * C:(i + 1) * C],
                                                        normed[:, kb * P:kb * P + rows], wv_sb[:], start=True, stop=True)
                            last.then_inc(proj_ready, 1)

                    nc.tensor.transpose(token_ps[:, 0, 0:TXT], txt_in[:], ident_sb[:]).then_inc(token_ready, 1)
                    pe.wait_ge(token_ready, 1)
                    nc.tensor.sem_inc(txt_turned, 1)
                    pe.wait_ge(x_padded, 1)
                    for n in range(CTILES):
                        r0 = n * IMG_ROWS
                        if n >= 1:
                            pe.wait_ge(h1_ready, n)
                        for s in range(SHIFTS):
                            i, j = divmod(s, KS)
                            last = nc.tensor.matmul(hidden_ps[:, 0, 0:CT], w1_sb[:, s],
                                                    x_pad[:, r0 + i:r0 + i + IMG_ROWS, j:j + W],
                                                    start=(s == 0), stop=(s == SHIFTS - 1))
                        last.then_inc(hidden_ready, 1)
                        values(n)
                        post(n, 0)
                        pe.wait_ge(h1_ready, n + 1)

                        def gate_product(s):
                            g = n * SHIFTS + s
                            if g >= 2:
                                pe.wait_ge(tanh_ready, g - 1)
                            nc.tensor.matmul(gate_ps[:, g % 2, 0:CT], w2_sb[:, s], h1[:],
                                             start=True, stop=True).then_inc(gate_ready, 1)

                        gate_product(0)
                        gate_product(1)
                        post(n, 1)
                        for s in range(SHIFTS):
                            if s + 2 < SHIFTS:
                                gate_product(s + 2)
                            g = n * SHIFTS + s
                            pe.wait_ge(gated_ready, g + 1)
                            if s == 0:
                                pe.wait_ge(h0_ready, n + 1)
                            last = nc.tensor.matmul(token_ps[:, 0, 0:CT], w3_sb[:, s], gated[:, g % 2],
                                                    start=(s == 0), stop=(s == SHIFTS - 1))
                            last.then_inc(gated_used, 1)
                            if s == 4:
                                post(n, 2)
                        pe.wait_ge(gated_used, (n + 1) * SHIFTS)
                        nc.tensor.sem_inc(token_ready, 1)
                        post(n, 3)
                    for stage in range(4):
                        post(NPOST - 1, stage)
                    values(NPOST)

                @block.scalar
                def _(act):
                    def post(m, stage):
                        t0, w = POST[m]
                        if stage == 0:
                            act.wait_ge(centred, m + 1)
                            if m >= 1:
                                act.wait_ge(var_ready, m)
                            nc.scalar.activation(square[:, 0:w], norm_ps[:, 0, 0:w], ACT.Square).then_inc(squared, 1)
                        elif stage == 1:
                            act.wait_ge(var_ready, m + 1)
                            if m >= 1:
                                act.wait_ge(rstd_ready, m)
                            nc.scalar.activation(std[:, 0:w], norm_ps[:, 1, 0:w], ACT.Sqrt,
                                                 bias=eps_sb[:]).then_inc(std_ready, 1)
                        else:
                            if m >= 2 and stage == 2:
                                act.wait_ge(parts_stored[m % 2], 16 * 2 * TERMS * (m // 2))
                            for i, (rows, st) in enumerate(((P, q_st), (C, k_st))):
                                src, ready, done = (full, full_ready, high_ready) if stage == 2 else (rest, rest_ready, mid_ready)
                                act.wait_ge(ready, 2 * m + i + 1)
                                nc.scalar.copy(st[0:rows, m % 2, stage - 2, 0:w], src[0:rows, i, 0:w]).then_inc(done, 1)

                    for n in range(CTILES):
                        act.wait_ge(hidden_ready, n + 1)
                        if n >= 1:
                            act.wait_ge(gate_ready, n * SHIFTS)
                        nc.scalar.activation(h1[:], hidden_ps[:, 0, 0:CT], ACT.Relu, bias=b1_sb[:]).then_inc(h1_ready, 1)
                        post(n, 0)
                        for s in range(SHIFTS):
                            g = n * SHIFTS + s
                            act.wait_ge(gate_ready, g + 1)
                            if g >= 2:
                                act.wait_ge(gated_ready, g - 1)
                            nc.scalar.activation(gate[:, g % 2], gate_ps[:, g % 2, 0:CT], ACT.Tanh,
                                                 bias=b2_sb[:, s:s + 1], scale=0.5).then_inc(tanh_ready, 1)
                            if s == 1:
                                post(n, 1)
                        post(n, 2)
                        post(n, 3)
                    for stage in range(4):
                        post(NPOST - 1, stage)

                @block.vector
                def _(dve):
                    def take_up(m):
                        t0, w = POST[m]
                        dve.wait_ge(token_ready, m + 1)
                        if m == 0:
                            nc.vector.tensor_copy(h0[:, t0:t0 + w], token_ps[:, 0, 0:w]).then_inc(h0_ready, 1)
                        else:
                            nc.vector.tensor_scalar(h0[:, t0:t0 + w], token_ps[:, 0, 0:w], b3_sb[:], None,
                                                    ALU.add).then_inc(h0_ready, 1)

                    def post(m, stage):
                        t0, w = POST[m]
                        if stage == 1:
                            dve.wait_ge(std_ready, m + 1)
                            nc.vector.reciprocal(rstd[:, 0:w], std[:, 0:w]).then_inc(rstd_ready, 1)
                            dve.wait_ge(rstd_ready, m + 1)
                            nc.vector.tensor_tensor(normed[:, t0:t0 + w], norm_ps[:, 0, 0:w], rstd[:, 0:w],
                                                    ALU.mult).then_inc(normed_ready, 1)
                        else:
                            which, rows = (("q", P), ("k", C))[stage - 2]
                            for turned, table in enumerate((cos_sb, sin_sb)):
                                n = slot_of[(which, m, turned)]
                                dve.wait_ge(proj_ready, n + 1)
                                if m >= 1:
                                    dve.wait_ge(full_ready, 2 * (m - 1) + stage - 1)
                                nc.vector.tensor_tensor(rot[0:rows, 2 * (stage - 2) + turned, 0:w],
                                                        proj_ps[0:rows, n % 2, 0:w], table[0:rows, t0:t0 + w],
                                                        ALU.mult).then_inc(proj_used, 1)
                            dve.wait_ge(proj_used, slot_of[(which, m, 1)] + 1)
                            nc.vector.sem_inc(rot_ready, 1)

                    def values(m):
                        for v in V_AT.get(m, []):
                            n = slot_of[("v", v)]
                            dve.wait_ge(proj_ready, n + 1)
                            whole = [kb for kb in V_GROUPS[v] if (kb + 1) * P <= S]
                            a, k = whole[0], len(whole)
                            src = proj_ps[:, n % 2].rearrange("p (k e g v d) -> p e g k v d", e=2, g=GROUPS, v=GKV, d=HD)
                            rows = S - (KB - 1) * P
                            for e in range(2):
                                for g in range(GROUPS):
                                    last = nc.vector.tensor_copy(v_st[:, e, g, a:a + k, :, 0:HD], src[:, e, g, 0:k])
                                    if k < len(V_GROUPS[v]):
                                        last = nc.vector.tensor_copy(v_st[0:rows, e, g, KB - 1, :, 0:HD],
                                                                     src[0:rows, e, g, k])
                            last.then_inc(proj_used, 1)
                            dve.wait_ge(proj_used, n + 1)
                            nc.vector.sem_inc(v_set, 1)

                    nc.vector.tensor_copy(x_pad[:, 1:H + 1, 1:W + 1],
                                          x_in[:].rearrange("p (h w) -> p h w", h=H)).then_inc(x_padded, 1)
                    dve.wait_ge(x_padded, 1)
                    for n in range(CTILES):
                        r0 = n * IMG_ROWS
                        take_up(n)
                        values(n)
                        for s in range(SHIFTS):
                            i, j = divmod(s, KS)
                            g = n * SHIFTS + s
                            dve.wait_ge(tanh_ready, g + 1)
                            if g >= 2:
                                dve.wait_ge(gated_used, g - 1)
                            nc.vector.scalar_tensor_tensor(
                                out=gated[:, g % 2].rearrange("p (h w) -> p h w", h=IMG_ROWS),
                                in0=gate[:, g % 2].rearrange("p (h w) -> p h w", h=IMG_ROWS), scalar=1.0,
                                in1=x_pad[:, r0 + i:r0 + i + IMG_ROWS, j:j + W],
                                op0=ALU.add, op1=ALU.mult).then_inc(gated_ready, 1)
                            if s == 2:
                                post(n, 1)
                            if s == 6:
                                post(n, 2)
                        post(n, 3)
                    take_up(NPOST - 1)
                    for stage in (1, 2, 3):
                        post(NPOST - 1, stage)
                    values(NPOST)

                @block.gpsimd
                def _(pool):
                    for m, (t0, w) in enumerate(POST):
                        for i, rows in enumerate((P, C)):
                            pool.wait_ge(rot_ready, 2 * m + i + 1)
                            if m >= 1:
                                pool.wait_ge(high_ready, 2 * (m - 1) + i + 1)
                                pool.wait_ge(rest_ready, 2 * (m - 1) + i + 1)
                            nc.gpsimd.tensor_tensor(full[0:rows, i, 0:w], rot[0:rows, 2 * i, 0:w],
                                                    rot[0:rows, 2 * i + 1, 0:w], ALU.add).then_inc(full_ready, 1)
                        for i, (rows, st) in enumerate(((P, q_st), (C, k_st))):
                            pool.wait_ge(high_ready, 2 * m + i + 1)
                            pool.wait_ge(full_ready, 2 * m + i + 1)
                            if m >= 1:
                                pool.wait_ge(low_ready, 2 * (m - 1) + i + 1)
                            nc.gpsimd.tensor_tensor(rest[0:rows, i, 0:w], full[0:rows, i, 0:w],
                                                    st[0:rows, m % 2, 0, 0:w], ALU.subtract).then_inc(rest_ready, 1)
                        for i, (rows, st) in enumerate(((P, q_st), (C, k_st))):
                            pool.wait_ge(mid_ready, 2 * m + i + 1)
                            nc.gpsimd.tensor_tensor(st[0:rows, m % 2, 2, 0:w], rest[0:rows, i, 0:w],
                                                    st[0:rows, m % 2, 1, 0:w], ALU.subtract).then_inc(low_ready, 1)
            nc.all_engine_barrier(sem_only=True)
            for s in step_sems:
                nc.sync.sem_clear(s)
            nc.all_engine_barrier(sem_only=True)


def attention(nc, q_terms, k_terms, v_blocks, masks, heads_out):
    with ExitStack() as ctx:
        def sbuf(name, shape, dt):
            return ctx.enter_context(nc.sbuf_tensor(name, shape, dt))

        def sem(name):
            return ctx.enter_context(nc.semaphore(name))

        q_rows = sbuf("q_rows", [P, GROUPS, GH, S], BF16)
        k_rows = sbuf("k_rows", [P, GROUPS, S], BF16)
        v_keys = sbuf("v_keys", [P, GROUPS, KB, GKV * VW], F32)
        k_next = sbuf("k_next", [ROWS, GROUPS, S], BF16)
        v_next = sbuf("v_next", [P, GROUPS, KB, GKV * VW], F32)
        masks_f32 = sbuf("masks_f32", [P, 3, P], F32)
        masks_sb = sbuf("masks_sb", [P, 3, P], BF16)
        mask_kq, mask_qk, ident = (masks_sb[:, n] for n in range(3))
        part_max = sbuf("part_max", [P, 2, QB, GH, QT], F32)
        row_max = sbuf("row_max", [P, 2, QB, GH], F32)
        max_split = sbuf("max_split", [P, 2, QB, MAX_PARTS, GH], BF16)
        max_rows = sbuf("max_rows", [MAX_PARTS * GH, 2, TILE], BF16)
        probs = sbuf("probs", [P, P_RING, GH, TILE], F32)
        out_sb = sbuf("out_sb", [P, 2, TILE], F32)

        scores = ctx.enter_context(nc.psum_tensor("scores", [P, S_RING, TILE], F32))
        max_scores = ctx.enter_context(nc.psum_tensor("max_scores", [P, M_RING, TILE], F32))
        out_acc = ctx.enter_context(nc.psum_tensor("out_acc", [P, 2, TILE], F32))

        cleared = sem("rows_cleared")
        first_in = sem("first_loads")
        Q_LOADS = GKV
        KV_LOADS = GROUPS * (GKV + 1)

        def load_queries(eng, b, g, t, done):
            t0, w = Q_TILES[t]
            for v in range(GKV):
                h = GH * g + 2 * v
                src = q_terms[b, h:h + 2].rearrange("h r s -> r h s")[:, :, t0:t0 + w]
                eng.dma_start(q_rows[HEAD_ROWS * v:HEAD_ROWS * (v + 1), g, 2 * v:2 * v + 2, t0:t0 + w], src).then_inc(done, 16)

        def load_keys(eng, b, done):
            for g in range(GROUPS):
                for v in range(GKV):
                    eng.dma_start(k_next[HEAD_ROWS * v:HEAD_ROWS * (v + 1), g, :],
                                  k_terms[b, GKV * g + v]).then_inc(done, 16)
                eng.dma_start(v_next[:, g].rearrange("p k v -> p (k v)"), v_blocks[b, g]).then_inc(done, 16)

        with nc.Block(no_gpsimd_drain=True) as block:
            @block.vector
            def _(dve):
                nc.vector.memset(q_rows[:].rearrange("p g h s -> p (g h s)").bitcast(U32), 0).then_inc(cleared, 1)
                nc.vector.memset(part_max[:], 0.0).then_inc(cleared, 1)
                nc.vector.memset(k_rows[ROWS:ROWS + MAX_PARTS], -1.0).then_inc(cleared, 1)
                dve.wait_ge(first_in, 16)
                nc.vector.tensor_copy(masks_sb[:], masks_f32[:]).then_inc(cleared, 1)
                dve.wait_ge(cleared, 4)

            @block.sync
            def _(sp):
                sp.dma_start(masks_f32[:], masks.rearrange("m p n -> p m n")).then_inc(first_in, 16)
                sp.wait_ge(first_in, 16)
                sp.wait_ge(cleared, 3)
                for g in range(GROUPS):
                    for t in range(QT):
                        load_queries(sp, 0, g, t, first_in)
                load_keys(sp, 0, first_in)
                sp.wait_ge(first_in, 16 * (1 + GROUPS * QT * Q_LOADS + KV_LOADS))

        keys_copied = sem("keys_copied")
        next_keys = sem("next_keys_loaded")
        next_loaded = sem("next_batch_loaded")
        early_loaded = [sem(f"next_unit{u}_loaded") for u in range(6)]
        max_ready = sem("max_slot_ready")
        max_used = sem("max_slot_used")
        chain = sem("row_max_steps")
        split_ready = sem("max_split_ready")
        rows_copied = sem("max_rows_copied")
        rows_set = [sem("max_rows_in_q_even"), sem("max_rows_in_q_odd")]
        s_ready = sem("scores_ready")
        p_masked = sem("probs_masked")
        p_ready = sem("probs_ready")
        p_used = sem("probs_used")
        o_ready = sem("out_ready")
        o_copied = sem("out_copied")
        o_stored = [sem("out_stored_even"), sem("out_stored_odd")]
        step_sems = [keys_copied, next_keys, next_loaded, *early_loaded, max_ready, max_used, chain, split_ready, rows_copied, *rows_set,
                     s_ready, p_ready, p_masked, p_used, o_ready, o_copied, *o_stored]

        def clear_step():
            nc.all_engine_barrier(sem_only=True)
            for s in step_sems:
                nc.sync.sem_clear(s)
            nc.all_engine_barrier(sem_only=True)

        UNITS = [(g, t) for t in range(QT) for g in range(GROUPS)]
        NU = len(UNITS)
        begin = [t0 for t0, w in Q_TILES]
        width = [w for t0, w in Q_TILES]

        STEPS = [(u, j) for u, (g, t) in enumerate(UNITS) for j in range(-(-(begin[t] + width[t]) // P))]
        DIAGONAL = [k for k, (u, j) in enumerate(STEPS) if j * P >= begin[UNITS[u][1]]]
        first_step = [min(k for k, (v, j) in enumerate(STEPS) if v == u) for u in range(NU)] + [len(STEPS)]
        began = [0]
        for u, j in STEPS:
            t = UNITS[u][1]
            began.append(began[-1] + width[t] - max(0, j * P - begin[t]))

        def key_chunks(t, i):
            return -(-min(S, begin[t] + (i + 1) * P) // TILE)

        AHEAD = 6
        LAST = NU + AHEAD

        def unit(u):
            return UNITS[u % NU]

        MAX_OPS = {}
        for u in range(AHEAD, LAST):
            t = unit(u)[1]
            MAX_OPS[u] = [(u, i, c, h) for i in range(-(-width[t] // P)) for c in range(key_chunks(t, i)) for h in range(GH)]

        place = [began[first_step[u]] for u in range(NU + 1)]
        place += [place[NU] + place[u] for u in range(1, AHEAD + 1)]
        complete = {u: place[u + 1] - place[AHEAD] for u in range(AHEAD, LAST)}
        TURN_AFTER = 300

        def turn_place(u):
            return min(complete[u] + TURN_AFTER, place[NU])

        timed = []
        for u in range(AHEAD, LAST):
            n = len(MAX_OPS[u])
            start = place[u] - place[AHEAD]
            timed += [(start + (complete[u] - start) * (m + 1) / n, op) for m, op in enumerate(MAX_OPS[u])]
            timed.append((turn_place(u), (u,)))
        timed.sort(key=lambda x: x[0])
        slots_at = [[] for _ in STEPS]
        for x, op in timed:
            slots_at[max(k for k in range(len(STEPS)) if began[k] < max(x, 1))].append(op)
        order = [op for ops in slots_at for op in ops]
        first_order = [op for u in range(NU, LAST) for op in MAX_OPS[u] + [(u,)]]

        transfers = [(turn_place(u), 0, u) for u in range(AHEAD, LAST)] + [(place[u + 1] + TURN_AFTER, 1, u) for u in range(NU)]
        transfers.sort()

        def geometry(op):
            u, i, c, h = op
            q0 = begin[unit(u)[1]] + i * P
            m = min(P, S - q0)
            n = min(TILE, q0 + m - c * TILE)
            return q0, m, c * TILE, n, c * TILE + n == q0 + m

        def maximum_products(pe, op, n, base):
            if n >= M_RING:
                pe.wait_ge(max_used, n - M_RING + 1)
            u = op[0]
            g, t = unit(u)
            if len(op) == 1:
                pe.wait_ge(split_ready, u - base + 1)
                turned = max_scores[0:MAX_PARTS * GH, n % M_RING, :].bitcast(BF16)
                for i in range(-(-width[t] // P)):
                    m = min(P, width[t] - i * P)
                    last = nc.tensor.transpose(turned[:, i * P:i * P + m],
                                               max_split[0:m, u % 2, i].rearrange("p a h -> p (a h)"),
                                               ident[0:m, 0:m])
                last.then_inc(max_ready, 1)
                return
            q0, m, k0, keys, diagonal = geometry(op)
            k_src = k_rows if u < NU else k_next
            last = nc.tensor.matmul(max_scores[0:m, n % M_RING, 0:keys], q_rows[0:ROWS, g, op[3], q0:q0 + m],
                                    k_src[0:ROWS, g, k0:k0 + keys], start=True, stop=not diagonal)
            if diagonal:
                last = nc.tensor.matmul(max_scores[0:m, n % M_RING, keys - m:keys], ident[0:m, 0:m],
                                        mask_qk[0:m, 0:m], start=False, stop=True)
            last.then_inc(max_ready, 1)

        def maximum_reductions(dve, order, base):
            slot_of = {op: n for n, op in enumerate(order)}
            chained = [0]

            def link(ins):
                chained[0] += 1
                ins.then_inc(chain, 1)
                dve.wait_ge(chain, chained[0])

            for n, op in enumerate(order):
                dve.wait_ge(max_ready, n + 1)
                u = op[0]
                t = unit(u)[1]
                if len(op) == 1:
                    if u >= base + 2:
                        dve.wait_ge(rows_set[u % 2], 16 * MAX_PARTS * ((u - base) // 2))
                    turned = max_scores[0:MAX_PARTS * GH, n % M_RING, :].bitcast(BF16)
                    nc.vector.tensor_copy(max_rows[:, u % 2, 0:width[t]], turned[:, 0:width[t]]).then_inc(rows_copied, 1)
                    dve.wait_ge(rows_copied, u - base + 1)
                    nc.vector.sem_inc(max_used, 1)
                    continue
                _, i, c, h = op
                _, m, _, keys, _ = geometry(op)
                nc.vector.tensor_reduce(part_max[0:m, u % 2, i, h, c:c + 1], max_scores[0:m, n % M_RING, 0:keys],
                                        AX_X, ALU.max).then_inc(max_used, 1)
                if op != MAX_OPS[u][-1]:
                    continue
                dve.wait_ge(max_used, n + 1)
                if u >= base + 2:
                    dve.wait_ge(max_ready, slot_of[(u - 2,)] + 1)
                blocks = -(-width[t] // P)
                counts = [key_chunks(t, i) for i in range(blocks)]
                for c in sorted(set(counts)):
                    i, k = counts.index(c), counts.count(c)
                    link(nc.vector.tensor_reduce(row_max[:, u % 2, i:i + k], part_max[:, u % 2, i:i + k, :, 0:c],
                                                 AX_X, ALU.max))
                high = max_split[:, u % 2, 0:blocks, 0, :]
                link(nc.vector.tensor_copy(high, row_max[:, u % 2, 0:blocks]))
                nc.vector.tensor_tensor(max_split[:, u % 2, 0:blocks, 1, :], row_max[:, u % 2, 0:blocks], high,
                                        ALU.subtract).then_inc(split_ready, 1)

        def maximum_rows(sp, u, base):
            g, t = unit(u)
            sp.wait_ge(rows_copied, u - base + 1)
            for part in range(MAX_PARTS):
                sp.dma_start(q_rows[ROWS + part:ROWS + part + 1, g, :, begin[t]:begin[t] + width[t]],
                             max_rows[part * GH:(part + 1) * GH, u % 2, 0:width[t]]).then_inc(rows_set[u % 2], 16)

        with nc.Block(no_gpsimd_drain=True) as block:
            @block.tensor
            def _(pe):
                for n, op in enumerate(first_order):
                    maximum_products(pe, op, n, NU)

            @block.vector
            def _(dve):
                maximum_reductions(dve, first_order, NU)

            @block.sync
            def _(sp):
                for u in range(NU, LAST):
                    maximum_rows(sp, u, NU)
                for half in range(2):
                    sp.wait_ge(rows_set[half], 16 * MAX_PARTS * (AHEAD // 2))
        clear_step()

        with nc.Fori(0, B) as b:
            with nc.Block(no_gpsimd_drain=True) as block:
                @block.sync
                def _(sp):
                    def store(u):
                        g, t = UNITS[u]
                        sp.wait_ge(o_copied, u + 1)
                        for h in range(GH):
                            sp.dma_start(heads_out[b, g * GH + h][:, begin[t]:begin[t] + width[t]],
                                         out_sb[VW * h:VW * h + HD + 1, u % 2, 0:width[t]]).then_inc(o_stored[u % 2], 16)

                    def reload(u):
                        g, t = UNITS[u]
                        sp.wait_ge(s_ready, GH * first_step[u + 1])
                        load_queries(sp, (b + 1) & (B - 1), g, t, early_loaded[u] if u < AHEAD else next_loaded)

                    sp.wait_ge(keys_copied, 2)
                    load_keys(sp, (b + 1) & (B - 1), next_keys)
                    for _, kind, u in transfers:
                        if kind == 0:
                            maximum_rows(sp, u, AHEAD)
                        else:
                            reload(u)
                            store(u)
                    for half in range(2):
                        sp.wait_ge(o_stored[half], 16 * GH * (NU // 2))
                        sp.wait_ge(rows_set[half], 16 * MAX_PARTS * (NU // 2))
                    sp.wait_ge(next_loaded, 16 * (NU - AHEAD) * Q_LOADS)

                @block.vector
                def _(dve):
                    nc.vector.tensor_copy(k_rows[0:ROWS], k_next[:]).then_inc(keys_copied, 1)
                    nc.vector.tensor_copy(v_keys[:], v_next[:]).then_inc(keys_copied, 1)
                    maximum_reductions(dve, order, AHEAD)

                @block.gpsimd
                def _(pool):
                    for n, k in enumerate(DIAGONAL):
                        u, j = STEPS[k]
                        o = j * P - begin[UNITS[u][1]]
                        keys = min(P, S - j * P)
                        pool.wait_ge(p_ready, GH * (k + 1))
                        block_probs = probs[0:keys, k % P_RING, :, o:o + keys]
                        nc.gpsimd.affine_select(block_probs, block_probs, [[0, GH], [1, keys]], ALU.is_ge, 0.0,
                                                base=0, channel_multiplier=-1).then_inc(p_masked, 1)

                @block.scalar
                def _(act):
                    def copy_out(u):
                        w = width[UNITS[u][1]]
                        act.wait_ge(o_ready, u + 1)
                        if u >= 2:
                            act.wait_ge(o_stored[u % 2], 16 * GH * (u // 2))
                        nc.scalar.copy(out_sb[:, u % 2, 0:w], out_acc[:, u % 2, 0:w]).then_inc(o_copied, 1)

                    for k, (u, j) in enumerate(STEPS):
                        t = UNITS[u][1]
                        o = max(0, j * P - begin[t])
                        keys = min(P, S - j * P)
                        if k >= P_RING:
                            act.wait_ge(p_used, k - P_RING + 1)
                        for h in range(GH):
                            act.wait_ge(s_ready, GH * k + h + 1)
                            nc.scalar.activation(probs[0:keys, k % P_RING, h, o:width[t]],
                                                 scores[0:keys, (GH * k + h) % S_RING, o:width[t]], ACT.Exp,
                                                 scale=float(HD) ** -0.5).then_inc(p_ready, 1)
                        if u >= 1 and k == first_step[u] + 1:
                            copy_out(u - 1)
                    copy_out(NU - 1)

                @block.tensor
                def _(pe):
                    slots = [0]

                    def run_slot(op):
                        if len(op) == 4 and op[0] >= NU and op == MAX_OPS[op[0]][0]:
                            pe.wait_ge(early_loaded[op[0] - NU], 16 * Q_LOADS)
                            pe.wait_ge(next_keys, 16 * KV_LOADS)
                        maximum_products(pe, op, slots[0], AHEAD)
                        slots[0] += 1

                    def score(k, h):
                        u, j = STEPS[k]
                        g, t = UNITS[u]
                        o = max(0, j * P - begin[t])
                        keys = min(P, S - j * P)
                        n = GH * k + h
                        if n >= S_RING:
                            pe.wait_ge(p_ready, n - S_RING + 1)
                        if u >= AHEAD and k == first_step[u] and h == 0:
                            pe.wait_ge(rows_set[u % 2], 16 * MAX_PARTS * ((u - AHEAD) // 2 + 1))
                        nc.tensor.matmul(scores[0:keys, n % S_RING, o:width[t]],
                                         k_rows[0:ROWS + MAX_PARTS, g, j * P:j * P + keys],
                                         q_rows[0:ROWS + MAX_PARTS, g, h, begin[t] + o:begin[t] + width[t]],
                                         start=True, stop=True).then_inc(s_ready, 1)

                    def outputs(k):
                        u, j = STEPS[k]
                        g, t = UNITS[u]
                        o = max(0, j * P - begin[t])
                        keys = min(P, S - j * P)
                        pe.wait_ge(p_ready, GH * (k + 1))
                        if k in DIAGONAL:
                            pe.wait_ge(p_masked, DIAGONAL.index(k) + 1)
                        if j == 0 and u >= 2:
                            pe.wait_ge(o_copied, u - 1)
                        end = k == first_step[u + 1] - 1
                        for h in range(GH):
                            v = h // 2
                            last = nc.tensor.matmul(out_acc[VW * h:VW * h + VW, u % 2, o:width[t]],
                                                    v_keys[0:keys, g, j, v * VW:(v + 1) * VW],
                                                    probs[0:keys, k % P_RING, h, o:width[t]],
                                                    start=(j == 0), stop=end)
                        last.then_inc(p_used, 1)
                        if end:
                            pe.wait_ge(p_used, k + 1)
                            nc.tensor.sem_inc(o_ready, 1)

                    pe.wait_ge(keys_copied, 2)
                    for k in range(len(STEPS)):
                        ops = slots_at[k]
                        cut = [len(ops) * x // 5 for x in range(6)]
                        for h in range(GH):
                            score(k, h)
                            for op in ops[cut[h]:cut[h + 1]]:
                                run_slot(op)
                        if k >= 1:
                            outputs(k - 1)
                        for op in ops[cut[4]:]:
                            run_slot(op)
                    outputs(len(STEPS) - 1)
            clear_step()


def inverse_sums(nc, heads_out, inverse):
    with ExitStack() as ctx:
        sums = ctx.enter_context(nc.sbuf_tensor("sums", [P, B, NH * S // P], F32))
        inv = ctx.enter_context(nc.sbuf_tensor("inv", [P, B, NH * S // P], F32))
        loaded = [ctx.enter_context(nc.semaphore(f"sums{b}_loaded")) for b in range(B)]
        done = ctx.enter_context(nc.semaphore("sums_inverted"))
        stored = ctx.enter_context(nc.semaphore("inverses_stored"))
        with nc.Block(no_gpsimd_drain=True) as block:
            @block.sync
            def _(sp):
                per = P // NH
                for b in range(B):
                    sp.dma_start(sums[:, b, :], heads_out[b, :, HD].rearrange("h (c n) -> h c n", c=per)).then_inc(loaded[b], 16)
                for b in range(B):
                    sp.wait_ge(done, b + 1)
                    sp.dma_start(inverse[b].rearrange("h (c n) -> (h c) n", c=per), inv[:, b, :]).then_inc(stored, 16)
                sp.wait_ge(stored, 16 * B)

            @block.vector
            def _(dve):
                for b in range(B):
                    dve.wait_ge(loaded[b], 16)
                    nc.vector.reciprocal(inv[:, b], sums[:, b]).then_inc(done, 1)


def second_norm(nc, heads_out, inverse, h0_in, wo, wr, br, tables, normed_out, sum_out, weights_out):
    centre, mean = tables
    with ExitStack() as ctx:
        def sbuf(name, shape, dt=F32):
            return ctx.enter_context(nc.sbuf_tensor(name, shape, dt))

        def psum(name, shape):
            return ctx.enter_context(nc.psum_tensor(name, shape, F32))

        def sem(name):
            return ctx.enter_context(nc.semaphore(name))

        wo_sb = sbuf("wo_sb", [P, P])
        wr_sb = sbuf("wr_sb", [P, 2])
        br_sb = sbuf("br_sb", [2, 1])
        eps_sb = sbuf("eps2_sb", [P, 1])
        centre_sb = sbuf("centre2_sb", [P, P])
        mean_sb = sbuf("mean2_sb", [P, P])
        heads = sbuf("heads", [P, RING, TILE])
        inv = sbuf("inv_rows", [P, RING, TILE])
        h0 = sbuf("h0_tile", [P, RING, TILE])
        attn = sbuf("attn", [P, 2, TILE])
        h2 = sbuf("h2", [P, RING, TILE])
        square = sbuf("square2", [P, 2, TILE])
        std = sbuf("std2", [P, 2, TILE])
        rstd = sbuf("rstd2", [P, 2, TILE])
        normed = sbuf("normed2", [P, RING, TILE])
        total = sbuf("total", [P, RING, TILE])
        router = sbuf("router", [2, S])
        proj_ps = psum("proj2_ps", [P, 2, TILE])
        centred_ps = psum("centred2_ps", [P, 2, TILE])
        var_ps = psum("var2_ps", [P, 2, TILE])
        router_ps = psum("router_ps", [2, 2, TILE])

        const_in = sem("const2_loaded")
        with nc.Block(no_gpsimd_drain=True) as block:
            @block.sync
            def _(sp):
                pieces = [(wo_sb[:], wo), (wr_sb[:], wr), (br_sb[:], br), (centre_sb[:], centre), (mean_sb[:], mean)]
                for dst, src in pieces:
                    sp.dma_start(dst, src).then_inc(const_in, 16)
                sp.wait_ge(const_in, 16 * len(pieces) + 1)

            @block.vector
            def _(dve):
                nc.vector.memset(eps_sb[:], EPS).then_inc(const_in, 1)

        loaded = [sem(f"tile_loaded{n}") for n in range(RING)]
        stored = [sem(f"tile_stored{n}") for n in range(RING)]
        attn_ready = sem("attn_ready")
        proj_ready = sem("proj2_ready")
        h2_ready = sem("h2_ready")
        centred = sem("centred2")
        squared = sem("squared2")
        var_ready = sem("var2_ready")
        std_ready = sem("std2_ready")
        rstd_ready = sem("rstd2_ready")
        normed_ready = sem("normed2_ready")
        total_ready = sem("total_ready")
        router_ready = sem("router_ready")
        router_set = sem("router_set")
        router_out = sem("router_stored")
        step_sems = [*loaded, *stored, attn_ready, proj_ready, h2_ready, centred, squared, var_ready, std_ready,
                     rstd_ready, normed_ready, total_ready, router_ready, router_set, router_out]
        NT = len(TILES)

        with nc.Fori(0, PAIRS) as p:
            with nc.Block(no_gpsimd_drain=True) as block:
                def tile_in(m):
                    return m % RING, loaded[m % RING], 16 * 3 * (m // RING + 1)

                def tile_out(m):
                    return m % RING, stored[m % RING], 16 * 2 * (m // RING)

                @block.sync
                def _(sp):
                    def load(m):
                        t0, w = TILES[m]
                        r = m % RING
                        if m >= RING:
                            sp.wait_ge(attn_ready, m - RING + 1)
                            sp.wait_ge(h2_ready, m - RING + 1)
                        two = heads_out[bass.ds(2 * p, 2)].rearrange("b h r s -> (b h) r s")
                        sp.dma_start(heads[:, r, 0:w], two[:, 0:HD, t0:t0 + w]).then_inc(loaded[r], 16)
                        ones = inverse[bass.ds(2 * p, 2)].rearrange("b h s -> (b h) s")[:, None, t0:t0 + w]
                        sp.dma_start(inv[:, r, 0:w], ones.to_broadcast([2 * NH, HD, w])).then_inc(loaded[r], 16)
                        sp.dma_start(h0[:, r, 0:w], h0_in[p][:, t0:t0 + w]).then_inc(loaded[r], 16)

                    for m in range(min(RING, NT)):
                        load(m)
                    for m, (t0, w) in enumerate(TILES):
                        r = m % RING
                        sp.wait_ge(normed_ready, m + 1)
                        sp.dma_start(normed_out[p][:, t0:t0 + w], normed[:, r, 0:w]).then_inc(stored[r], 16)
                        sp.wait_ge(total_ready, m + 1)
                        sp.dma_start(sum_out[p][:, t0:t0 + w], total[:, r, 0:w]).then_inc(stored[r], 16)
                        if m + RING < NT:
                            load(m + RING)
                    sp.wait_ge(router_set, NT)
                    sp.dma_start(weights_out[bass.ds(2 * p, 2)], router[:]).then_inc(router_out, 16)
                    sp.wait_ge(router_out, 16)
                    for r in range(RING):
                        sp.wait_ge(stored[r], 16 * 2 * len(range(r, NT, RING)))

                @block.scalar
                def _(act):
                    def squares(m):
                        w = TILES[m][1]
                        act.wait_ge(centred, m + 1)
                        if m >= 2:
                            act.wait_ge(var_ready, m - 1)
                        nc.scalar.activation(square[:, m % 2, 0:w], centred_ps[:, m % 2, 0:w], ACT.Square).then_inc(squared, 1)

                    def route(m):
                        t0, w = TILES[m]
                        act.wait_ge(router_ready, m + 1)
                        nc.scalar.activation(router[:, t0:t0 + w], router_ps[:, m % 2, 0:w], ACT.Identity,
                                             bias=br_sb[:]).then_inc(router_set, 1)

                    squares(0)
                    for m, (t0, w) in enumerate(TILES):
                        if m + 1 < NT:
                            squares(m + 1)
                        act.wait_ge(var_ready, m + 1)
                        if m >= 2:
                            act.wait_ge(rstd_ready, m - 1)
                        nc.scalar.activation(std[:, m % 2, 0:w], var_ps[:, m % 2, 0:w], ACT.Sqrt,
                                             bias=eps_sb[:]).then_inc(std_ready, 1)
                        if m >= 2:
                            route(m - 2)
                    route(NT - 2)
                    route(NT - 1)

                @block.gpsimd
                def _(pool):
                    def multiply(m):
                        w = TILES[m][1]
                        r, landed, count = tile_in(m)
                        pool.wait_ge(landed, count)
                        if m >= 2:
                            pool.wait_ge(proj_ready, m - 1)
                        nc.gpsimd.tensor_tensor(attn[:, m % 2, 0:w], heads[:, r, 0:w], inv[:, r, 0:w],
                                                ALU.mult).then_inc(attn_ready, 1)

                    def add(m):
                        w = TILES[m][1]
                        r, left, count = tile_out(m)
                        pool.wait_ge(normed_ready, m + 1)
                        if m >= RING:
                            pool.wait_ge(left, count)
                        nc.gpsimd.tensor_tensor(total[:, r, 0:w], normed[:, r, 0:w], h2[:, r, 0:w],
                                                ALU.add).then_inc(total_ready, 1)

                    multiply(0)
                    multiply(1)
                    for m in range(NT):
                        if m + 2 < NT:
                            multiply(m + 2)
                        if m >= 1:
                            add(m - 1)
                    add(NT - 1)

                @block.vector
                def _(dve):
                    def residual(m):
                        w = TILES[m][1]
                        dve.wait_ge(proj_ready, m + 1)
                        r, landed, count = tile_in(m)
                        dve.wait_ge(landed, count)
                        if m >= RING:
                            dve.wait_ge(total_ready, m - RING + 1)
                            dve.wait_ge(centred, m - RING + 1)
                        nc.vector.tensor_tensor(h2[:, r, 0:w], proj_ps[:, m % 2, 0:w], h0[:, r, 0:w],
                                                ALU.add).then_inc(h2_ready, 1)

                    residual(0)
                    residual(1)
                    for m in range(NT):
                        w = TILES[m][1]
                        dve.wait_ge(std_ready, m + 1)
                        nc.vector.reciprocal(rstd[:, m % 2, 0:w], std[:, m % 2, 0:w]).then_inc(rstd_ready, 1)
                        if m + 2 < NT:
                            residual(m + 2)
                        dve.wait_ge(rstd_ready, m + 1)
                        r, left, count = tile_out(m)
                        if m >= RING:
                            dve.wait_ge(left, count)
                            dve.wait_ge(router_ready, m - RING + 1)
                        nc.vector.tensor_tensor(normed[:, r, 0:w], centred_ps[:, m % 2, 0:w], rstd[:, m % 2, 0:w],
                                                ALU.mult).then_inc(normed_ready, 1)

                @block.tensor
                def _(pe):
                    def project(m):
                        w = TILES[m][1]
                        pe.wait_ge(attn_ready, m + 1)
                        if m >= 2:
                            pe.wait_ge(h2_ready, m - 1)
                        nc.tensor.matmul(proj_ps[:, m % 2, 0:w], wo_sb[:], attn[:, m % 2, 0:w],
                                         start=True, stop=True).then_inc(proj_ready, 1)

                    def centre_tile(m):
                        w = TILES[m][1]
                        pe.wait_ge(h2_ready, m + 1)
                        if m >= 2:
                            pe.wait_ge(normed_ready, m - 1)
                        nc.tensor.matmul(centred_ps[:, m % 2, 0:w], centre_sb[:], h2[:, m % RING, 0:w],
                                         start=True, stop=True).then_inc(centred, 1)

                    def route(m):
                        w = TILES[m][1]
                        pe.wait_ge(normed_ready, m + 1)
                        if m >= 2:
                            pe.wait_ge(router_set, m - 1)
                        nc.tensor.matmul(router_ps[:, m % 2, 0:w], wr_sb[:], normed[:, m % RING, 0:w],
                                         start=True, stop=True).then_inc(router_ready, 1)

                    project(0)
                    project(1)
                    centre_tile(0)
                    for m in range(NT):
                        w = TILES[m][1]
                        if m + 1 < NT:
                            centre_tile(m + 1)
                        pe.wait_ge(squared, m + 1)
                        if m >= 2:
                            pe.wait_ge(std_ready, m - 1)
                        nc.tensor.matmul(var_ps[:, m % 2, 0:w], mean_sb[:], square[:, m % 2, 0:w],
                                         start=True, stop=True).then_inc(var_ready, 1)
                        if m + 2 < NT:
                            project(m + 2)
                        if m >= 1:
                            route(m - 1)
                    route(NT - 1)
            nc.all_engine_barrier(sem_only=True)
            for s in step_sems:
                nc.sync.sem_clear(s)
            nc.all_engine_barrier(sem_only=True)


def select(nc, weights_in, batch_sum, batch_before, chosen_out):
    with ExitStack() as ctx:
        def sbuf(name, shape, dt=F32):
            return ctx.enter_context(nc.sbuf_tensor(name, shape, dt))

        def sem(name):
            return ctx.enter_context(nc.semaphore(name))

        I32 = mybir.dt.int32
        w = sbuf("weights", [P, SPAN])
        v = sbuf("signed_weights", [P, SPAN])
        ones_block = sbuf("batch_sum_sb", [P, P])
        before_block = sbuf("batch_before_sb", [P, P])
        flags = sbuf("flags", [P, SPAN])
        equal = sbuf("equal", [P, SPAN])
        above = sbuf("above", [P, SPAN])
        rank = sbuf("rank", [P, SPAN])
        zeros = sbuf("zeros", [P, SPAN])
        chosen = sbuf("chosen", [P, SPAN])
        count = sbuf("count", [P, 2])
        level = sbuf("level", [P, 1], I32)
        trial = sbuf("trial", [P, 1], I32)
        keep = sbuf("keep", [P, 1], I32)
        positive = sbuf("positive", [P, 1])
        sign = sbuf("sign", [P, 1])
        wanted = sbuf("wanted", [P, 1])
        threshold = sbuf("threshold", [P, 1])
        room = sbuf("room", [P, 1])
        count_ps = ctx.enter_context(nc.psum_tensor("count_ps", [P, 2], F32))
        loaded = sem("weights_in")
        chain = sem("select_steps")
        counted = sem("counted")
        summed = sem("summed")
        stored = sem("chosen_stored")
        BITS = 31

        with nc.Block(no_gpsimd_drain=True) as block:
            @block.sync
            def _(sp):
                sp.dma_start(w[:], weights_in.rearrange("b (c n) -> (b c) n", c=ROWS_PER_BATCH)).then_inc(loaded, 16)
                sp.dma_start(ones_block[:], batch_sum).then_inc(loaded, 16)
                sp.dma_start(before_block[:], batch_before).then_inc(loaded, 16)
                sp.wait_ge(counted, BITS + 3)
                sp.dma_start(chosen_out.rearrange("b (c n) -> (b c) n", c=ROWS_PER_BATCH), chosen[:]).then_inc(stored, 16)
                sp.wait_ge(stored, 16)

            @block.tensor
            def _(pe):
                pe.wait_ge(loaded, 48)
                for n in range(BITS + 1):
                    pe.wait_ge(counted, n + 1)
                    nc.tensor.matmul(count_ps[:, 0:1], ones_block[:], count[:, 0:1], start=True, stop=True).then_inc(summed, 1)
                pe.wait_ge(counted, BITS + 2)
                nc.tensor.matmul(count_ps[:, 0:1], ones_block[:], count[:, 0:1], start=True, stop=True)
                nc.tensor.matmul(count_ps[:, 1:2], before_block[:], count[:, 1:2], start=True, stop=True).then_inc(summed, 1)

            @block.vector
            def _(dve):
                steps = [0]

                def link(ins):
                    steps[0] += 1
                    ins.then_inc(chain, 1)
                    dve.wait_ge(chain, steps[0])

                link(nc.vector.memset(level[:], 0))
                link(nc.vector.memset(zeros[:], 0.0))
                dve.wait_ge(loaded, 48)
                nc.vector.tensor_scalar(flags[:], w[:], 0.0, 0.0, ALU.is_ge, ALU.add, accum_out=count[:, 0:1]).then_inc(counted, 1)
                dve.wait_ge(summed, 1)
                link(nc.vector.tensor_scalar(positive[:], count_ps[:, 0:1], float(TOP), None, ALU.is_ge))
                link(nc.vector.tensor_scalar(sign[:], positive[:], 2.0, -1.0, ALU.mult, ALU.add))
                link(nc.vector.tensor_scalar(wanted[:], positive[:], float(2 * TOP - S - 1), float(S - TOP + 1), ALU.mult, ALU.add))
                link(nc.vector.tensor_scalar(v[:], w[:], sign[:], None, ALU.mult))
                for n in range(BITS):
                    link(nc.vector.tensor_scalar(trial[:], level[:], 1 << (BITS - 1 - n), None, ALU.bitwise_or))
                    nc.vector.tensor_scalar(flags[:], v[:], trial[:].bitcast(F32), 0.0, ALU.is_ge, ALU.add,
                                            accum_out=count[:, 0:1]).then_inc(counted, 1)
                    dve.wait_ge(summed, n + 2)
                    link(nc.vector.tensor_scalar(keep[:], count_ps[:, 0:1], wanted[:], None, ALU.is_ge))
                    link(nc.vector.copy_predicated(level[:], keep[:], trial[:]))
                link(nc.vector.tensor_scalar(threshold[:], level[:].bitcast(F32), sign[:], None, ALU.mult))
                link(nc.vector.tensor_scalar(equal[:], w[:], threshold[:], None, ALU.is_equal))
                link(nc.vector.tensor_scalar(above[:], w[:], threshold[:], 0.0, ALU.is_gt, ALU.add, accum_out=count[:, 0:1]))
                link(nc.vector.tensor_tensor_scan(rank[:], equal[:], zeros[:], 0.0, ALU.add, ALU.add))
                nc.vector.tensor_copy(count[:, 1:2], rank[:, SPAN - 1:SPAN]).then_inc(counted, 1)
                dve.wait_ge(summed, BITS + 2)
                link(nc.vector.tensor_scalar(room[:], count_ps[:, 0:1], -1.0, float(TOP), ALU.mult, ALU.add))
                link(nc.vector.tensor_tensor(room[:], room[:], count_ps[:, 1:2], ALU.subtract))
                link(nc.vector.scalar_tensor_tensor(out=flags[:], in0=rank[:], scalar=room[:], in1=equal[:],
                                                    op0=ALU.is_le, op1=ALU.mult))
                link(nc.vector.tensor_tensor(above[:], above[:], flags[:], ALU.add))
                nc.vector.tensor_tensor(chosen[:], w[:], above[:], ALU.mult).then_inc(counted, 1)


def feed_forward(nc, normed_in, sum_in, chosen_in, ff_w, ff_b, identity, out):
    w1, w2 = ff_w
    b1, b2 = ff_b
    with ExitStack() as ctx:
        def sbuf(name, shape, dt=F32):
            return ctx.enter_context(nc.sbuf_tensor(name, shape, dt))

        def psum(name, shape):
            return ctx.enter_context(nc.psum_tensor(name, shape, F32))

        def sem(name):
            return ctx.enter_context(nc.semaphore(name))

        w1_sb = sbuf("ff_w1_sb", [P, CHUNKS, P])
        w2_sb = sbuf("ff_w2_sb", [P, 2, C])
        b1_sb = sbuf("ff_b1_sb", [P, 2])
        b2_sb = sbuf("ff_b2_sb", [P, 1])
        ident_sb = sbuf("ident3_sb", [P, P])
        normed = sbuf("normed3", [P, RING, TILE])
        total = sbuf("total3", [P, RING, TILE])
        chosen = sbuf("chosen3", [P, RING, TILE])
        hidden = sbuf("hidden3", [P, 2, CHUNKS, TILE])
        scaled = sbuf("scaled3", [P, 2, TILE])
        final = sbuf("final3", [P, 2, TILE])
        turned = sbuf("turned3", [P, 2, TILE // P, P])
        hidden_ps = psum("hidden3_ps", [P, CHUNKS, TILE])
        y_ps = psum("y3_ps", [P, 2, TILE])
        turned_ps = psum("turned3_ps", [P, 2, TILE // P, P])

        const_in = sem("const3_loaded")
        with nc.Block(no_gpsimd_drain=True) as block:
            @block.sync
            def _(sp):
                pieces = [(w1_sb[:].rearrange("p c m -> p (c m)"), w1), (w2_sb[:].rearrange("p c m -> p (c m)"), w2),
                          (b1_sb[:], b1), (b2_sb[:], b2), (ident_sb[:], identity)]
                for dst, src in pieces:
                    sp.dma_start(dst, src).then_inc(const_in, 16)
                sp.wait_ge(const_in, 16 * len(pieces))

        loaded = [sem(f"tile3_loaded{n}") for n in range(RING)]
        hidden_ready = sem("hidden3_ready")
        gelu_ready = sem("gelu_ready")
        y_ready = sem("y3_ready")
        scaled_ready = sem("scaled_ready")
        final_ready = sem("final_ready")
        turned_ready = sem("turned3_ready")
        turned_set = sem("turned3_set")
        stored = [sem("out3_stored_even"), sem("out3_stored_odd")]
        step_sems = [*loaded, hidden_ready, gelu_ready, y_ready, scaled_ready, final_ready, turned_ready,
                     turned_set, *stored]
        NT = len(TILES)

        def stores(m):
            w = TILES[m][1]
            return 2 * ((w >= P) + (w % P > 0))

        def stored_by(m, half):
            return 16 * sum(stores(n) for n in range(m) if n % 2 == half)

        with nc.Fori(0, PAIRS) as p:
            with nc.Block(no_gpsimd_drain=True) as block:
                @block.sync
                def _(sp):
                    def store(m):
                        t0, w = TILES[m]
                        sp.wait_ge(turned_set, m + 1)
                        k, rest = divmod(w, P)
                        for e in range(2):
                            rows = out[bass.ds(2 * p + e, 1)].rearrange("o s c -> (o s) c")
                            sp.dma_start(rows[t0:t0 + k * P].rearrange("(k p) c -> p k c", p=P),
                                         turned[:, m % 2, 0:k, e * C:(e + 1) * C]).then_inc(stored[m % 2], 16)
                            if rest:
                                sp.dma_start(rows[t0 + k * P:t0 + w],
                                             turned[0:rest, m % 2, k, e * C:(e + 1) * C]).then_inc(stored[m % 2], 16)

                    def load(m):
                        t0, w = TILES[m]
                        r = m % RING
                        if m >= RING:
                            sp.wait_ge(hidden_ready, CHUNKS * (m - RING + 1))
                            sp.wait_ge(final_ready, m - RING + 1)
                        sp.dma_start(normed[:, r, 0:w], normed_in[p][:, t0:t0 + w]).then_inc(loaded[r], 16)
                        sp.dma_start(total[:, r, 0:w], sum_in[p][:, t0:t0 + w]).then_inc(loaded[r], 16)
                        rows = chosen_in[bass.ds(2 * p, 2)][:, None, t0:t0 + w]
                        sp.dma_start(chosen[:, r, 0:w], rows.to_broadcast([2, C, w])).then_inc(loaded[r], 16)

                    for m in range(min(RING, NT)):
                        load(m)
                    for m in range(NT):
                        if m + RING < NT:
                            load(m + RING)
                        store(m)
                    for half in range(2):
                        sp.wait_ge(stored[half], stored_by(NT, half))

                @block.tensor
                def _(pe):
                    def turn(m):
                        w = TILES[m][1]
                        pe.wait_ge(final_ready, m + 1)
                        if m >= 2:
                            pe.wait_ge(turned_set, m - 1)
                        for k in range(-(-w // P)):
                            n = min(P, w - k * P)
                            last = nc.tensor.transpose(turned_ps[0:n, m % 2, k], final[:, m % 2, k * P:k * P + n],
                                                       ident_sb[:])
                        last.then_inc(turned_ready, 1)

                    def second(m):
                        w = TILES[m][1]
                        if m >= 2:
                            pe.wait_ge(scaled_ready, m - 1)
                        for half in range(2):
                            for e in range(2):
                                pe.wait_ge(gelu_ready, CHUNKS * m + 2 * e + half + 1)
                                last = nc.tensor.matmul(y_ps[e * C:(e + 1) * C, m % 2, 0:w], w2_sb[:, half],
                                                        hidden[:, m % 2, 2 * e + half, 0:w],
                                                        start=(half == 0), stop=(half == 1))
                        last.then_inc(y_ready, 1)

                    for m in range(NT):
                        w = TILES[m][1]
                        pe.wait_ge(loaded[m % RING], 16 * 3 * (m // RING + 1))
                        for c in range(CHUNKS):
                            if m >= 1:
                                pe.wait_ge(gelu_ready, CHUNKS * (m - 1) + c + 1)
                            nc.tensor.matmul(hidden_ps[:, c, 0:w], w1_sb[:, c], normed[:, m % RING, 0:w],
                                             start=True, stop=True).then_inc(hidden_ready, 1)
                        if m >= 1:
                            second(m - 1)
                        if m >= 2:
                            turn(m - 2)
                    second(NT - 1)
                    turn(NT - 2)
                    turn(NT - 1)

                @block.scalar
                def _(act):
                    def copy_turned(m):
                        w = TILES[m][1]
                        act.wait_ge(turned_ready, m + 1)
                        if m >= 2:
                            act.wait_ge(stored[m % 2], stored_by(m, m % 2))
                        k, rest = divmod(w, P)
                        last = nc.scalar.copy(turned[:, m % 2, 0:k], turned_ps[:, m % 2, 0:k])
                        if rest:
                            last = nc.scalar.copy(turned[0:rest, m % 2, k], turned_ps[0:rest, m % 2, k])
                        last.then_inc(turned_set, 1)

                    for m in range(NT):
                        w = TILES[m][1]
                        for c in range(CHUNKS):
                            act.wait_ge(hidden_ready, CHUNKS * m + c + 1)
                            if m >= 2:
                                act.wait_ge(y_ready, m - 1)
                            nc.scalar.activation(hidden[:, m % 2, c, 0:w], hidden_ps[:, c, 0:w], ACT.Gelu_apprx_tanh,
                                                 bias=b1_sb[:, c % 2:c % 2 + 1]).then_inc(gelu_ready, 1)
                        if m >= 3:
                            copy_turned(m - 3)
                    for m in range(NT - 3, NT):
                        copy_turned(m)

                @block.vector
                def _(dve):
                    for m in range(NT):
                        w = TILES[m][1]
                        dve.wait_ge(y_ready, m + 1)
                        dve.wait_ge(loaded[m % RING], 16 * 3 * (m // RING + 1))
                        nc.vector.scalar_tensor_tensor(out=scaled[:, m % 2, 0:w], in0=y_ps[:, m % 2, 0:w], scalar=b2_sb[:],
                                                       in1=chosen[:, m % RING, 0:w], op0=ALU.add,
                                                       op1=ALU.mult).then_inc(scaled_ready, 1)
                        dve.wait_ge(scaled_ready, m + 1)
                        if m >= 2:
                            dve.wait_ge(turned_ready, m - 1)
                        nc.vector.tensor_tensor(final[:, m % 2, 0:w], scaled[:, m % 2, 0:w], total[:, m % RING, 0:w],
                                                ALU.add).then_inc(final_ready, 1)
            nc.all_engine_barrier(sem_only=True)
            for s in step_sems:
                nc.sync.sem_clear(s)
            nc.all_engine_barrier(sem_only=True)


def program(nc, a, out):
    def scratch(name, shape, dt=F32):
        return nc.dram_tensor(name, shape, dt, kind="Internal").ap()

    h0 = scratch("h0_dram", (PAIRS, P, S))
    q_terms = scratch("q_terms_dram", (B, NH, HEAD_ROWS, S), BF16)
    k_terms = scratch("k_terms_dram", (B, KV, HEAD_ROWS, S), BF16)
    v_blocks = scratch("v_blocks_dram", (B, GROUPS, P, KB * GKV * VW))
    heads = scratch("heads_dram", (B, NH, HD + 1, S))
    inverse = scratch("inverse_dram", (B, NH, S))
    normed = scratch("normed_dram", (PAIRS, P, S))
    total = scratch("total_dram", (PAIRS, P, S))
    weights = scratch("weights_dram", (B, S))
    chosen = scratch("chosen_dram", (B, S))
    tokens(nc, a["x"], a["txt"], (a["w1"], a["w2"], a["w3"]), (a["b1"], a["b2"], a["b3"]),
           (a["wq"], a["wq_turned"], a["wk"], a["wk_turned"], a["wv"]),
           (a["centre"], a["mean"], a["cos"], a["sin"], a["identity"]), h0, q_terms, k_terms, v_blocks)
    attention(nc, q_terms, k_terms, v_blocks, a["masks"], heads)
    inverse_sums(nc, heads, inverse)
    second_norm(nc, heads, inverse, h0, a["wo"], a["wr"], a["br"], (a["centre"], a["mean"]), normed, total, weights)
    select(nc, weights, a["batch_sum"], a["batch_before"], chosen)
    feed_forward(nc, normed, total, chosen, (a["ff_w1"], a["ff_w2"]), (a["ff_b1"], a["ff_b2"]), a["identity"], out)


def arranged(i):
    import numpy as np

    def two(w):
        k, m = w.shape
        o = np.zeros((2 * k, 2 * m), w.dtype)
        o[:k, :m] = w
        o[k:, m:] = w
        return o

    def by_shift(w):
        return np.ascontiguousarray(np.stack([two(w[:, s, :]) for s in range(SHIFTS)], 1).reshape(P, SHIFTS * P))

    def both(b):
        return np.ascontiguousarray(np.concatenate([b.reshape(C, -1)] * 2, 0))

    turn = np.arange(NH * HD).reshape(NH, 2, HD // 2)[:, ::-1].reshape(NH * HD)
    wq, wk, wv = i["L0_attn_Wq"], i["L0_attn_Wk"], i["L0_attn_Wv"]
    inv_freq = (1.0 / 10000.0 ** (np.arange(0, HD, 2, dtype=np.float32) / np.float32(HD))).astype(np.float32)
    angle = np.outer(np.arange(S, dtype=np.float32), inv_freq).astype(np.float32)
    angle = np.concatenate([angle, angle], -1)
    sign = np.where(np.arange(HD) < HD // 2, -1, 1).astype(np.float32)
    mean = two(np.full((C, C), 1 / C, np.float32))
    at = np.arange(P)
    after = np.where(at[:, None] > at[None, :], -3e38, 0).astype(np.float32)
    same = at[:, None] // ROWS_PER_BATCH == at[None, :] // ROWS_PER_BATCH
    ff_w1 = np.zeros((2, C, CHUNKS, P), np.float32)
    for e in range(2):
        for half in range(2):
            ff_w1[e, :, 2 * e + half] = i["L0_ffn_w1"][:, half * P:(half + 1) * P]
    return {
        "x": i["x"].reshape(PAIRS, P, IMG),
        "txt": i["txt"].reshape(PAIRS, 2, TXT, C),
        "w1": by_shift(i["L0_tok_W1"].reshape(C, SHIFTS, C)),
        "w2": by_shift(i["L0_tok_W2"].reshape(C, C, SHIFTS).transpose(0, 2, 1)),
        "w3": by_shift(i["L0_tok_W3"].reshape(C, SHIFTS, C)),
        "b1": both(i["L0_tok_b1"]),
        "b2": both(i["L0_tok_b2"]),
        "b3": both(i["L0_tok_b3"]),
        "wq": two(wq.T),
        "wq_turned": two(wq[turn].T),
        "wk": two(wk.T),
        "wk_turned": two(wk[turn[:KV * HD]].T),
        "wv": two(wv.T),
        "wo": two(i["L0_attn_Wo"].T),
        "wr": two(i["L0_ffn_wr"]),
        "br": np.concatenate([i["L0_ffn_br"].reshape(1, 1)] * 2, 0),
        "ff_w1": ff_w1.reshape(P, CHUNKS * P),
        "ff_w2": np.ascontiguousarray(i["L0_ffn_w2"].reshape(2, P, C).transpose(1, 0, 2).reshape(P, 2 * C)),
        "ff_b1": np.ascontiguousarray(i["L0_ffn_b1"].reshape(2, P).T),
        "ff_b2": both(i["L0_ffn_b2"]),
        "centre": np.eye(P, dtype=np.float32) - mean,
        "mean": mean,
        "cos": np.ascontiguousarray(np.tile(np.cos(angle).T, (P // HD, 1))),
        "sin": np.ascontiguousarray(np.tile((np.sin(angle) * sign).T, (P // HD, 1))),
        "identity": np.eye(P, dtype=np.float32),
        "masks": np.stack([after, after.T, np.eye(P, dtype=np.float32)]),
        "batch_sum": same.astype(np.float32),
        "batch_before": (same & (at[:, None] < at[None, :])).astype(np.float32),
    }


def kernel(**inputs):
    import numpy as np
    import concourse.bacc as bacc
    from concourse.bass_utils import run_bass_kernel_spmd

    nc = bacc.Bacc("TRN2", target_bir_lowering=False, num_devices=1)
    arrays, aps = {}, {}
    for name, array in arranged({k: np.asarray(v) for k, v in inputs.items()}).items():
        arrays["in_" + name] = np.ascontiguousarray(array)
        aps[name] = nc.dram_tensor("in_" + name, array.shape, mybir.dt.from_np(array.dtype), kind="ExternalInput").ap()
    out = nc.dram_tensor("out_0", (B, S, C), F32, kind="ExternalOutput").ap()
    program(nc, aps, out)
    r = run_bass_kernel_spmd(nc, [arrays], core_ids=[0])
    return r.results[0]["out_0"]
```

```python
from contextlib import ExitStack

import concourse.bass as bass
from concourse import mybir

ALU = mybir.AluOpType
ACT = mybir.ActivationFunctionType
F32 = mybir.dt.float32
BF16 = mybir.dt.bfloat16
U32 = mybir.dt.uint32
AX_X = mybir.AxisListType.X

P = 128
TILE = 512
B, C, H, W = 8, 64, 56, 56
IMG = H * W
TXT = 128
S = IMG + TXT
NH, KV, HD = 8, 4, 8
GROUPS = 2
GH = NH // GROUPS
GKV = KV // GROUPS
KB = -(-S // P)
QB = TILE // P
Q_TILES = [(0, TILE // 2)] + [(t0, min(TILE, S - t0)) for t0 in range(TILE // 2, S, TILE)]
QT = len(Q_TILES)
VW = 32
HEAD_ROWS = 6 * HD
ROWS = GKV * HEAD_ROWS
MAX_PARTS = 2
Q_TERM = (0, 0, 0, 1, 1, 2)
K_TERM = (0, 1, 2, 0, 1, 0)
P_RING = 3
S_RING = 4
M_RING = 3
O_RING = 4
AHEAD = 6
STEP_B = 2
PAIRS = B // 2
KS = 3
SHIFTS = KS * KS
PH, PW = H + 2, W + 2
IMG_ROWS = 8
CT = IMG_ROWS * W
CTILES = H // IMG_ROWS
PARTS = 3
TERMS = len(Q_TERM)
VB = 8
EPS = 1e-5
GATE_RING = 4
GATES_AHEAD = 3
TOP = S // 2 - 1
ROWS_PER_BATCH = P // B
SPAN = S // ROWS_PER_BATCH
FF = 4 * C
CHUNKS = 2 * FF // P
RING = 4
TILES = [(t0, min(TILE, S - t0)) for t0 in range(0, S, TILE)]
STEP_PAIRS = 2
STEP_TILES = [(q, t0, w) for q in range(STEP_PAIRS) for t0, w in TILES]


def tokens(nc, x, txt, conv_w, conv_b, proj_w, tables, h0_out, q_terms, k_terms, v_blocks):
    w1, w2, w3 = conv_w
    b1, b2, b3 = conv_b
    wq, wq_turned, wk, wk_turned, wv = proj_w
    centre, mean, cos, sin, identity = tables
    with ExitStack() as ctx:
        def sbuf(name, shape, dt=F32):
            return ctx.enter_context(nc.sbuf_tensor(name, shape, dt))

        def psum(name, shape):
            return ctx.enter_context(nc.psum_tensor(name, shape, F32))

        def sem(name):
            return ctx.enter_context(nc.semaphore(name))

        x_in = sbuf("x_in", [P, IMG])
        x_pad = sbuf("x_pad", [P, PH, PW])
        txt_in = sbuf("txt_in", [TXT, P])
        w1_sb = sbuf("w1_sb", [P, SHIFTS, P])
        w2_sb = sbuf("w2_sb", [P, SHIFTS, P])
        w3_sb = sbuf("w3_sb", [P, SHIFTS, P])
        wq_sb = sbuf("wq_sb", [P, 2, P])
        wk_sb = sbuf("wk_sb", [P, 2, C])
        wv_sb = sbuf("wv_sb", [P, C])
        b1_sb = sbuf("b1_sb", [P, 1])
        b2_sb = sbuf("b2_sb", [P, SHIFTS])
        b3_sb = sbuf("b3_sb", [P, 1])
        eps_sb = sbuf("eps_sb", [P, 1])
        centre_sb = sbuf("centre_sb", [P, P])
        mean_sb = sbuf("mean_sb", [P, P])
        ident_sb = sbuf("ident_sb", [P, P])
        cos_sb = sbuf("cos_sb", [P, S])
        sin_sb = sbuf("sin_sb", [P, S])
        h1 = sbuf("h1", [P, CT])
        gate = sbuf("gate", [P, GATE_RING, CT])
        gated = sbuf("gated", [P, GATE_RING, CT])
        h0 = sbuf("h0", [P, S])
        square = sbuf("square", [P, CT])
        std = sbuf("std", [P, CT])
        rstd = sbuf("rstd", [P, CT])
        normed = sbuf("normed", [P, S])
        rot = sbuf("rot", [P, 4, CT])
        full = sbuf("full", [P, 2, CT])
        rest = sbuf("rest", [P, 2, CT])
        q_st = sbuf("q_st", [P, 2, PARTS, CT], BF16)
        k_st = sbuf("k_st", [C, 2, PARTS, CT], BF16)
        v_st = sbuf("v_st", [P, 2, GROUPS, KB, GKV, VW])

        hidden_ps = psum("hidden_ps", [P, 1, TILE])
        gate_ps = psum("gate_ps", [P, 2, TILE])
        token_ps = psum("token_ps", [P, 1, TILE])
        norm_ps = psum("norm_ps", [P, 2, TILE])
        proj_ps = psum("proj_ps", [P, 2, TILE])

        loaded = sem("weights_loaded")
        tables_loaded = sem("rotary_tables_loaded")
        prepared = sem("weights_prepared")
        values_set = sem("value_ones_set")

        def load_pair(eng, p, done):
            eng.dma_start(x_in[:], x[p]).then_inc(done, 16)
            eng.dma_start(txt_in[:], txt[p].rearrange("b t c -> t b c")).then_inc(done, 16)

        with nc.Block(no_gpsimd_drain=True) as block:
            @block.sync
            def _(sp):
                load_pair(sp, 0, loaded)
                pieces = [(w1_sb[:].rearrange("p s c -> p (s c)"), w1), (w2_sb[:].rearrange("p s c -> p (s c)"), w2),
                          (w3_sb[:].rearrange("p s c -> p (s c)"), w3), (b1_sb[:], b1), (b2_sb[:], b2), (b3_sb[:], b3),
                          (wq_sb[:, 0], wq), (wq_sb[:, 1], wq_turned), (wk_sb[:, 0], wk), (wk_sb[:, 1], wk_turned),
                          (wv_sb[:], wv), (centre_sb[:], centre), (mean_sb[:], mean), (ident_sb[:], identity)]
                for dst, src in pieces:
                    sp.dma_start(dst, src).then_inc(loaded, 16)
                sp.dma_start(cos_sb[:], cos).then_inc(tables_loaded, 16)
                sp.dma_start(sin_sb[:], sin).then_inc(tables_loaded, 16)
                sp.wait_ge(loaded, 16 * (2 + len(pieces)))

            @block.vector
            def _(dve):
                nc.vector.memset(x_pad[:], 0.0).then_inc(prepared, 1)
                nc.vector.memset(eps_sb[:], EPS).then_inc(prepared, 1)
                nc.vector.memset(h0[:, IMG - CT:IMG], 0.0).then_inc(prepared, 1)
                nc.vector.memset(normed[:], 0.0).then_inc(prepared, 1)
                dve.wait_ge(loaded, 16 * 16)
                dve.wait_ge(prepared, 4)
                nc.vector.tensor_scalar(b2_sb[:], b2_sb[:], 0.5, None, ALU.mult).then_inc(prepared, 1)
                nc.vector.tensor_scalar(w3_sb[:], w3_sb[:], 0.5, None, ALU.mult).then_inc(prepared, 1)
                nc.vector.tensor_copy(x_pad[:, 1:H + 1, 1:W + 1],
                                      x_in[:].rearrange("p (h w) -> p h w", h=H)).then_inc(prepared, 1)
                dve.wait_ge(prepared, 7)

            @block.gpsimd
            def _(pool):
                nc.gpsimd.memset(v_st[:], 0.0).then_inc(values_set, 1)
                pool.wait_ge(values_set, 1)
                nc.gpsimd.memset(v_st[:].rearrange("p e g k v w -> p (e g k v) w")[:, :, HD:HD + 1], 1.0).then_inc(values_set, 1)
                pool.wait_ge(values_set, 2)

        x_padded = sem("x_padded")
        txt_turned = sem("txt_turned")
        reload = sem("next_pair_loaded")
        hidden_ready = sem("hidden_ready")
        h1_ready = sem("h1_ready")
        gate_ready = sem("gate_ready")
        tanh_ready = sem("tanh_ready")
        gated_ready = sem("gated_ready")
        gated_used = sem("gated_used")
        token_ready = sem("token_ready")
        h0_ready = sem("h0_ready")
        centred = sem("centred")
        squared = sem("squared")
        var_ready = sem("var_ready")
        std_ready = sem("std_ready")
        rstd_ready = sem("rstd_ready")
        normed_ready = sem("normed_ready")
        proj_ready = sem("proj_ready")
        proj_used = sem("proj_used")
        rot_ready = sem("rot_ready")
        full_ready = sem("full_ready")
        high_ready = sem("high_ready")
        rest_ready = sem("rest_ready")
        mid_ready = sem("mid_ready")
        low_ready = sem("low_ready")
        parts_stored = [sem("parts_stored_even"), sem("parts_stored_odd")]
        v_set = sem("v_set")
        stored = sem("pair_stored")
        step_sems = [x_padded, txt_turned, reload, hidden_ready, h1_ready, gate_ready, tanh_ready, gated_ready,
                     gated_used, token_ready, h0_ready, centred, squared, var_ready, std_ready, rstd_ready,
                     normed_ready, proj_ready, proj_used, rot_ready, full_ready, high_ready, rest_ready, mid_ready,
                     low_ready, *parts_stored, v_set, stored, values_set]

        TAKEN = [(IMG, TXT)] + [(n * CT, CT) for n in range(CTILES)]
        POST = [TAKEN[-1]] + TAKEN[:-1]
        NPOST = len(POST)
        V_GROUPS = [range(v, min(v + VB, KB)) for v in range(0, KB, VB)]
        V_AT = {0: [2, 3], 4: [0], 6: [1]}
        V_ORDER = [v for n in sorted(V_AT) for v in V_AT[n]]
        slots = []
        for m in range(NPOST):
            slots += [("v", v) for v in V_AT.get(m - 1, []) if m > 1]
            slots += [("q", m, 0), ("q", m, 1), ("k", m, 0), ("k", m, 1)]
            slots += [("v", v) for v in V_AT[0] if m == 0]
        slot_of = {op: n for n, op in enumerate(slots)}
        POST_AT = {"hidden": (1, 4), "pe": (0, 2), "act": (5, 7), "dve": (1, 4)}
        TEXT_AT = {"pe": (2, 4, 7, 8), "act": (4, 6, 8, 8), "dve": (None, 6, 8, 8)}

        def due(n):
            return 0 if n == 0 else n + 1

        def store_values(sp, pair, n_tile):
            for v in V_AT.get(n_tile, []):
                sp.wait_ge(v_set, V_ORDER.index(v) + 1)
                k = V_GROUPS[v]
                for e in range(2):
                    dst = v_blocks[bass.ds(2 * pair + e, 1)].rearrange("b g p x -> p (b g) x")
                    src = v_st[:, e].rearrange("p g k v w -> p g (k v w)")
                    cols = slice(k[0] * GKV * VW, (k[-1] + 1) * GKV * VW)
                    sp.dma_start(dst[:, :, cols], src[:, :, cols]).then_inc(stored, 16)

        def store_parts(sp, pair, m):
            t0, w = POST[m]
            for part, ready in enumerate((high_ready, mid_ready, low_ready)):
                sp.wait_ge(ready, 2 * m + 2)
                for dst, st, parts in ((q_terms, q_st, Q_TERM), (k_terms, k_st, K_TERM)):
                    rows = dst[bass.ds(2 * pair, 2)].rearrange("b h r s -> (b h) r s")
                    for term in [n for n in range(TERMS) if parts[n] == part]:
                        sp.dma_start(rows[:, term * HD:(term + 1) * HD, t0:t0 + w],
                                     st[:, m % 2, part, 0:w]).then_inc(parts_stored[m % 2], 16)

        def product_stage(pe, m, stage):
            t0, w = POST[m]
            if stage == 0:
                if m >= 1:
                    pe.wait_ge(h0_ready, m)
                if m >= 1:
                    pe.wait_ge(normed_ready, m)
                nc.tensor.matmul(norm_ps[:, 0, 0:w], centre_sb[:], h0[:, t0:t0 + w],
                                 start=True, stop=True).then_inc(centred, 1)
            elif stage == 1:
                pe.wait_ge(squared, m + 1)
                nc.tensor.matmul(norm_ps[:, 1, 0:w], mean_sb[:], square[:, 0:w],
                                 start=True, stop=True).then_inc(var_ready, 1)
            else:
                which, rows, w_sb = (("q", P, wq_sb), ("k", C, wk_sb))[stage - 2]
                pe.wait_ge(normed_ready, m + 1)
                for turned in range(2):
                    n = slot_of[(which, m, turned)]
                    if n >= 2:
                        pe.wait_ge(proj_used, n - 1)
                    nc.tensor.matmul(proj_ps[0:rows, n % 2, 0:w], w_sb[:, turned], normed[:, t0:t0 + w],
                                     start=True, stop=True).then_inc(proj_ready, 1)

        def value_products(pe, n_tile):
            for v in V_AT.get(n_tile, []):
                n = slot_of[("v", v)]
                pe.wait_ge(proj_used, n - 1)
                for i, kb in enumerate(V_GROUPS[v]):
                    rows = min(P, S - kb * P)
                    last = nc.tensor.matmul(proj_ps[0:rows, n % 2, i * C:(i + 1) * C],
                                            normed[:, kb * P:kb * P + rows], wv_sb[:], start=True, stop=True)
                last.then_inc(proj_ready, 1)

        def activation_stage(act, m, stage):
            t0, w = POST[m]
            if stage == 0:
                act.wait_ge(centred, m + 1)
                if m >= 1:
                    act.wait_ge(var_ready, m)
                nc.scalar.activation(square[:, 0:w], norm_ps[:, 0, 0:w], ACT.Square).then_inc(squared, 1)
            elif stage == 1:
                act.wait_ge(var_ready, m + 1)
                if m >= 1:
                    act.wait_ge(rstd_ready, m)
                nc.scalar.activation(std[:, 0:w], norm_ps[:, 1, 0:w], ACT.Sqrt,
                                     bias=eps_sb[:]).then_inc(std_ready, 1)
            else:
                if m >= 2 and stage == 2:
                    act.wait_ge(parts_stored[m % 2], 16 * 2 * TERMS * (m // 2))
                for i, (rows, st) in enumerate(((P, q_st), (C, k_st))):
                    src, ready, done = (full, full_ready, high_ready) if stage == 2 else (rest, rest_ready, mid_ready)
                    act.wait_ge(ready, 2 * m + i + 1)
                    nc.scalar.copy(st[0:rows, m % 2, stage - 2, 0:w], src[0:rows, i, 0:w]).then_inc(done, 1)


        def vector_stage(dve, m, stage):
            t0, w = POST[m]
            if stage == 1:
                dve.wait_ge(std_ready, m + 1)
                nc.vector.reciprocal(rstd[:, 0:w], std[:, 0:w]).then_inc(rstd_ready, 1)
                dve.wait_ge(rstd_ready, m + 1)
                nc.vector.tensor_tensor(normed[:, t0:t0 + w], norm_ps[:, 0, 0:w], rstd[:, 0:w],
                                        ALU.mult).then_inc(normed_ready, 1)
            else:
                which, rows = (("q", P), ("k", C))[stage - 2]
                if m == 0:
                    dve.wait_ge(tables_loaded, 32)
                for turned, table in enumerate((cos_sb, sin_sb)):
                    n = slot_of[(which, m, turned)]
                    dve.wait_ge(proj_ready, n + 1)
                    if m >= 1:
                        dve.wait_ge(full_ready, 2 * (m - 1) + stage - 1)
                    nc.vector.tensor_tensor(rot[0:rows, 2 * (stage - 2) + turned, 0:w],
                                            proj_ps[0:rows, n % 2, 0:w], table[0:rows, t0:t0 + w],
                                            ALU.mult).then_inc(proj_used, 1)
                dve.wait_ge(proj_used, slot_of[(which, m, 1)] + 1)
                nc.vector.sem_inc(rot_ready, 1)

        def value_copies(dve, n_tile):
            for v in V_AT.get(n_tile, []):
                n = slot_of[("v", v)]
                dve.wait_ge(proj_ready, n + 1)
                whole = [kb for kb in V_GROUPS[v] if (kb + 1) * P <= S]
                a, k = whole[0], len(whole)
                src = proj_ps[:, n % 2].rearrange("p (k e g v d) -> p e g k v d", e=2, g=GROUPS, v=GKV, d=HD)
                rows = S - (KB - 1) * P
                for e in range(2):
                    for g in range(GROUPS):
                        last = nc.vector.tensor_copy(v_st[:, e, g, a:a + k, :, 0:HD], src[:, e, g, 0:k])
                        if k < len(V_GROUPS[v]):
                            last = nc.vector.tensor_copy(v_st[0:rows, e, g, KB - 1, :, 0:HD],
                                                         src[0:rows, e, g, k])
                last.then_inc(proj_used, 1)
                dve.wait_ge(proj_used, n + 1)
                nc.vector.sem_inc(v_set, 1)

        def sum_and_rest(pool, m):
            t0, w = POST[m]
            for i, rows in enumerate((P, C)):
                pool.wait_ge(rot_ready, 2 * m + i + 1)
                if m >= 1:
                    pool.wait_ge(high_ready, 2 * (m - 1) + i + 1)
                    pool.wait_ge(rest_ready, 2 * (m - 1) + i + 1)
                nc.gpsimd.tensor_tensor(full[0:rows, i, 0:w], rot[0:rows, 2 * i, 0:w],
                                        rot[0:rows, 2 * i + 1, 0:w], ALU.add).then_inc(full_ready, 1)
            for i, (rows, st) in enumerate(((P, q_st), (C, k_st))):
                pool.wait_ge(high_ready, 2 * m + i + 1)
                pool.wait_ge(full_ready, 2 * m + i + 1)
                if m >= 1:
                    pool.wait_ge(low_ready, 2 * (m - 1) + i + 1)
                nc.gpsimd.tensor_tensor(rest[0:rows, i, 0:w], full[0:rows, i, 0:w],
                                        st[0:rows, m % 2, 0, 0:w], ALU.subtract).then_inc(rest_ready, 1)
            for i, (rows, st) in enumerate(((P, q_st), (C, k_st))):
                pool.wait_ge(mid_ready, 2 * m + i + 1)
                nc.gpsimd.tensor_tensor(st[0:rows, m % 2, 2, 0:w], rest[0:rows, i, 0:w],
                                        st[0:rows, m % 2, 1, 0:w], ALU.subtract).then_inc(low_ready, 1)

        with nc.Fori(0, PAIRS) as p:
            before = (p + PAIRS - 1) & (PAIRS - 1)
            with nc.Block(no_gpsimd_drain=True) as block:
                @block.sync
                def _(sp):
                    sp.wait_ge(txt_turned, 1)
                    load_pair(sp, (p + 1) & (PAIRS - 1), reload)
                    for n, (t0, w) in enumerate(TAKEN):
                        sp.wait_ge(h0_ready, n + 1)
                        sp.dma_start(h0_out[p][:, t0:t0 + w], h0[:, t0:t0 + w]).then_inc(stored, 16)
                        if n == 0:
                            store_parts(sp, before, 0)
                            store_values(sp, before, 0)
                            store_parts(sp, p, 1)
                        elif n < CTILES:
                            store_values(sp, p, n)
                            store_parts(sp, p, n + 1)
                    sp.wait_ge(stored, 16 * (len(TAKEN) + 2 * len(V_GROUPS)))
                    sp.wait_ge(reload, 32)
                    for half in range(2):
                        sp.wait_ge(parts_stored[half], 16 * 2 * TERMS * (NPOST // 2))

                @block.tensor
                def _(pe):
                    nc.tensor.transpose(token_ps[:, 0, 0:TXT], txt_in[:], ident_sb[:]).then_inc(token_ready, 1)
                    pe.wait_ge(token_ready, 1)
                    nc.tensor.sem_inc(txt_turned, 1)
                    for n in range(CTILES):
                        r0 = n * IMG_ROWS
                        if n >= 1:
                            pe.wait_ge(h1_ready, n)
                        for s in range(SHIFTS):
                            i, j = divmod(s, KS)
                            last = nc.tensor.matmul(hidden_ps[:, 0, 0:CT], w1_sb[:, s],
                                                    x_pad[:, r0 + i:r0 + i + IMG_ROWS, j:j + W],
                                                    start=(s == 0), stop=(s == SHIFTS - 1))
                            if s in POST_AT["hidden"]:
                                product_stage(pe, due(n), POST_AT["hidden"].index(s))
                        last.then_inc(hidden_ready, 1)
                        if n >= 1:
                            value_products(pe, n)
                        pe.wait_ge(h1_ready, n + 1)

                        def gate_product(s):
                            g = n * SHIFTS + s
                            if g >= 2:
                                pe.wait_ge(tanh_ready, g - 1)
                            nc.tensor.matmul(gate_ps[:, g % 2, 0:CT], w2_sb[:, s], h1[:],
                                             start=True, stop=True).then_inc(gate_ready, 1)

                        for s in range(GATES_AHEAD):
                            gate_product(s)
                        for s in range(SHIFTS):
                            if s + GATES_AHEAD < SHIFTS:
                                gate_product(s + GATES_AHEAD)
                            g = n * SHIFTS + s
                            pe.wait_ge(gated_ready, g + 1)
                            if s == 0:
                                pe.wait_ge(h0_ready, n + 1)
                            last = nc.tensor.matmul(token_ps[:, 0, 0:CT], w3_sb[:, s], gated[:, g % GATE_RING],
                                                    start=(s == 0), stop=(s == SHIFTS - 1))
                            last.then_inc(gated_used, 1)
                            if s in POST_AT["pe"]:
                                product_stage(pe, due(n), 2 + POST_AT["pe"].index(s))
                            if n == 0:
                                if s == POST_AT["pe"][1]:
                                    value_products(pe, 0)
                                for stage in range(4):
                                    if s == TEXT_AT["pe"][stage]:
                                        product_stage(pe, 1, stage)
                        pe.wait_ge(gated_used, (n + 1) * SHIFTS)
                        nc.tensor.sem_inc(token_ready, 1)

                @block.scalar
                def _(act):
                    for n in range(CTILES):
                        activation_stage(act, due(n), 0)
                        activation_stage(act, due(n), 1)
                        act.wait_ge(hidden_ready, n + 1)
                        if n >= 1:
                            act.wait_ge(gate_ready, n * SHIFTS)
                        nc.scalar.activation(h1[:], hidden_ps[:, 0, 0:CT], ACT.Relu, bias=b1_sb[:]).then_inc(h1_ready, 1)
                        for s in range(SHIFTS):
                            g = n * SHIFTS + s
                            act.wait_ge(gate_ready, g + 1)
                            if g >= GATE_RING:
                                act.wait_ge(gated_ready, g - GATE_RING + 1)
                            nc.scalar.activation(gate[:, g % GATE_RING], gate_ps[:, g % 2, 0:CT], ACT.Tanh,
                                                 bias=b2_sb[:, s:s + 1], scale=0.5).then_inc(tanh_ready, 1)
                            if s in POST_AT["act"]:
                                activation_stage(act, due(n), 2 + POST_AT["act"].index(s))
                            for stage in range(4):
                                if n == 0 and s == TEXT_AT["act"][stage]:
                                    activation_stage(act, 1, stage)

                @block.vector
                def _(dve):
                    def take_up(m):
                        t0, w = TAKEN[m]
                        dve.wait_ge(token_ready, m + 1)
                        if m == 0:
                            nc.vector.tensor_copy(h0[:, t0:t0 + w], token_ps[:, 0, 0:w]).then_inc(h0_ready, 1)
                        else:
                            nc.vector.tensor_scalar(h0[:, t0:t0 + w], token_ps[:, 0, 0:w], b3_sb[:], None,
                                                    ALU.add).then_inc(h0_ready, 1)

                    for n in range(CTILES):
                        r0 = n * IMG_ROWS
                        take_up(n)
                        vector_stage(dve, due(n), 1)
                        if n >= 1:
                            value_copies(dve, n)
                        for s in range(SHIFTS):
                            i, j = divmod(s, KS)
                            g = n * SHIFTS + s
                            dve.wait_ge(tanh_ready, g + 1)
                            if g >= GATE_RING:
                                dve.wait_ge(gated_used, g - GATE_RING + 1)
                            nc.vector.scalar_tensor_tensor(
                                out=gated[:, g % GATE_RING].rearrange("p (h w) -> p h w", h=IMG_ROWS),
                                in0=gate[:, g % GATE_RING].rearrange("p (h w) -> p h w", h=IMG_ROWS), scalar=1.0,
                                in1=x_pad[:, r0 + i:r0 + i + IMG_ROWS, j:j + W],
                                op0=ALU.add, op1=ALU.mult).then_inc(gated_ready, 1)
                            if s in POST_AT["dve"]:
                                vector_stage(dve, due(n), 2 + POST_AT["dve"].index(s))
                            if n == 0:
                                if s == POST_AT["dve"][1]:
                                    value_copies(dve, 0)
                                for stage in range(1, 4):
                                    if s == TEXT_AT["dve"][stage]:
                                        vector_stage(dve, 1, stage)
                    take_up(CTILES)
                    dve.wait_ge(reload, 32)
                    dve.wait_ge(hidden_ready, CTILES)
                    dve.wait_ge(gated_ready, CTILES * SHIFTS)
                    nc.vector.tensor_copy(x_pad[:, 1:H + 1, 1:W + 1],
                                          x_in[:].rearrange("p (h w) -> p h w", h=H)).then_inc(x_padded, 1)
                    dve.wait_ge(x_padded, 1)

                @block.gpsimd
                def _(pool):
                    for m in range(NPOST):
                        sum_and_rest(pool, m)
            nc.all_engine_barrier(sem_only=True)
            for s in step_sems:
                nc.sync.sem_clear(s)
            nc.all_engine_barrier(sem_only=True)

        with nc.Block(no_gpsimd_drain=True) as block:
            @block.sync
            def _(sp):
                store_parts(sp, PAIRS - 1, 0)
                store_values(sp, PAIRS - 1, 0)
                sp.wait_ge(stored, 16 * 2 * len(V_AT[0]))
                sp.wait_ge(parts_stored[0], 16 * 2 * TERMS)

            @block.tensor
            def _(pe):
                for stage in range(4):
                    product_stage(pe, 0, stage)
                value_products(pe, 0)

            @block.scalar
            def _(act):
                for stage in range(4):
                    activation_stage(act, 0, stage)

            @block.vector
            def _(dve):
                for stage in (1, 2, 3):
                    vector_stage(dve, 0, stage)
                value_copies(dve, 0)

            @block.gpsimd
            def _(pool):
                sum_and_rest(pool, 0)


def attention(nc, q_terms, k_terms, v_blocks, masks, heads_out):
    with ExitStack() as ctx:
        def sbuf(name, shape, dt):
            return ctx.enter_context(nc.sbuf_tensor(name, shape, dt))

        def sem(name):
            return ctx.enter_context(nc.semaphore(name))

        q_rows = sbuf("q_rows", [P, GROUPS, GH, S], BF16)
        k_rows = sbuf("k_rows", [P, STEP_B, GROUPS, S], BF16)
        v_keys = sbuf("v_keys", [P, STEP_B, GROUPS, KB, GKV * VW], F32)
        masks_f32 = sbuf("masks_f32", [P, 2, P], F32)
        masks_sb = sbuf("masks_sb", [P, 2, P], BF16)
        mask_qk, ident = (masks_sb[:, n] for n in range(2))
        part_max = sbuf("part_max", [P, 2, QB, GH, QT], F32)
        row_max = sbuf("row_max", [P, 2, QB, GH], F32)
        max_split = sbuf("max_split", [P, 2, QB, MAX_PARTS, GH], BF16)
        max_rows = sbuf("max_rows", [MAX_PARTS * GH, 2, TILE], BF16)
        probs = sbuf("probs", [P, P_RING, GH, TILE], F32)
        out_sb = sbuf("out_sb", [P, O_RING, TILE], F32)

        scores = ctx.enter_context(nc.psum_tensor("scores", [P, S_RING, TILE], F32))
        max_scores = ctx.enter_context(nc.psum_tensor("max_scores", [P, M_RING, TILE], F32))
        out_acc = ctx.enter_context(nc.psum_tensor("out_acc", [P, TILE], F32))

        q_cleared = sem("q_rows_cleared")
        cleared = sem("constants_set")
        first_in = sem("first_loads")
        rest_in = sem("rest_of_first_batch_loaded")
        Q_LOADS = GKV
        KV_LOADS = GROUPS * (GKV + 1)

        def load_queries(eng, b, g, t, done):
            t0, w = Q_TILES[t]
            for v in range(GKV):
                h = GH * g + 2 * v
                src = q_terms[b, h:h + 2].rearrange("h r s -> r h s")[:, :, t0:t0 + w]
                eng.dma_start(q_rows[HEAD_ROWS * v:HEAD_ROWS * (v + 1), g, 2 * v:2 * v + 2, t0:t0 + w], src).then_inc(done, 16)

        def load_keys(eng, b, e, done):
            for g in range(GROUPS):
                for v in range(GKV):
                    eng.dma_start(k_rows[HEAD_ROWS * v:HEAD_ROWS * (v + 1), e, g, :],
                                  k_terms[b, GKV * g + v]).then_inc(done, 16)
                eng.dma_start(v_keys[:, e, g].rearrange("p k v -> p (k v)"), v_blocks[b, g]).then_inc(done, 16)

        with nc.Block(no_gpsimd_drain=True) as block:
            @block.vector
            def _(dve):
                nc.vector.memset(q_rows[:, 0].rearrange("p h s -> p (h s)").bitcast(U32), 0).then_inc(q_cleared, 1)
                nc.vector.memset(part_max[:], 0.0).then_inc(cleared, 1)
                nc.vector.memset(k_rows[ROWS:ROWS + MAX_PARTS], -1.0).then_inc(cleared, 1)
                dve.wait_ge(first_in, 16)
                nc.vector.tensor_copy(masks_sb[:], masks_f32[:]).then_inc(cleared, 1)
                dve.wait_ge(cleared, 3)
                dve.wait_ge(q_cleared, GROUPS)

            @block.gpsimd
            def _(pool):
                for g in range(1, GROUPS):
                    nc.gpsimd.memset(q_rows[:, g].rearrange("p h s -> p (h s)").bitcast(U32), 0).then_inc(q_cleared, 1)

            @block.sync
            def _(sp):
                sp.dma_start(masks_f32[:], masks.rearrange("m p n -> p m n")).then_inc(first_in, 16)
                sp.wait_ge(first_in, 16)
                load_keys(sp, 0, 0, first_in)
                sp.wait_ge(q_cleared, GROUPS)
                for t in range(AHEAD // GROUPS):
                    for g in range(GROUPS):
                        load_queries(sp, 0, g, t, first_in)
                sp.wait_ge(first_in, 16 * (1 + AHEAD * Q_LOADS + KV_LOADS))

        keys_loaded = [sem("next_step_keys_loaded"), sem("second_batch_keys_loaded")]
        next_loaded = sem("next_step_rows_loaded")
        unit_loaded = [sem(f"next_unit{u}_loaded") for u in range((STEP_B - 1) * GROUPS * QT + AHEAD)]
        max_ready = sem("max_slot_ready")
        max_used = sem("max_slot_used")
        chain = sem("row_max_steps")
        split_ready = sem("max_split_ready")
        rows_copied = sem("max_rows_copied")
        rows_set = [sem("max_rows_in_q_even"), sem("max_rows_in_q_odd")]
        s_ready = sem("scores_ready")
        p_masked = sem("probs_masked")
        p_ready = sem("probs_ready")
        p_used = sem("probs_used")
        o_ready = sem("out_ready")
        o_copied = sem("out_copied")
        o_stored = [sem(f"out{r}_stored") for r in range(O_RING)]
        step_sems = [*keys_loaded, next_loaded, *unit_loaded, max_ready, max_used, chain, split_ready, rows_copied, *rows_set,
                     s_ready, p_ready, p_masked, p_used, o_ready, o_copied, *o_stored]

        def clear_step():
            nc.all_engine_barrier(sem_only=True)
            for s in step_sems:
                nc.sync.sem_clear(s)
            nc.all_engine_barrier(sem_only=True)

        BU = GROUPS * QT
        UNITS = [(g, t) for e in range(STEP_B) for t in range(QT) for g in range(GROUPS)]
        NU = len(UNITS)
        begin = [t0 for t0, w in Q_TILES]
        width = [w for t0, w in Q_TILES]

        STEPS = [(u, j) for u, (g, t) in enumerate(UNITS) for j in range(-(-(begin[t] + width[t]) // P))]
        DIAGONAL = [k for k, (u, j) in enumerate(STEPS) if j * P >= begin[UNITS[u][1]]]
        first_step = [min(k for k, (v, j) in enumerate(STEPS) if v == u) for u in range(NU)] + [len(STEPS)]
        began = [0]
        for u, j in STEPS:
            t = UNITS[u][1]
            began.append(began[-1] + width[t] - max(0, j * P - begin[t]))

        def key_chunks(t, i):
            return -(-min(S, begin[t] + (i + 1) * P) // TILE)

        LAST = NU + AHEAD

        def unit(u):
            return UNITS[u % NU]

        MAX_OPS = {}
        for u in range(AHEAD, LAST):
            t = unit(u)[1]
            MAX_OPS[u] = [(u, i, c, h) for i in range(-(-width[t] // P)) for c in range(key_chunks(t, i)) for h in range(GH)]

        place = [began[first_step[u]] for u in range(NU + 1)]
        place += [place[NU] + place[u] for u in range(1, AHEAD + 1)]
        complete = {u: place[u + 1] - place[AHEAD] for u in range(AHEAD, LAST)}
        TURN_AFTER = 300

        def turn_place(u):
            return min(complete[u] + TURN_AFTER, place[NU])

        timed = []
        for u in range(AHEAD, LAST):
            n = len(MAX_OPS[u])
            start = place[u] - place[AHEAD]
            timed += [(start + (complete[u] - start) * (m + 1) / n, op) for m, op in enumerate(MAX_OPS[u])]
            timed.append((turn_place(u), (u,)))
        timed.sort(key=lambda x: x[0])
        slots_at = [[] for _ in STEPS]
        for x, op in timed:
            slots_at[max(k for k in range(len(STEPS)) if began[k] < max(x, 1))].append(op)
        order = [op for ops in slots_at for op in ops]
        first_order = [op for u in range(NU, LAST) for op in MAX_OPS[u] + [(u,)]]

        transfers = [(turn_place(u), 0, u) for u in range(AHEAD, LAST)] + [(place[u + 1] + TURN_AFTER, 1, u) for u in range(NU)]
        transfers.sort()

        def geometry(op):
            u, i, c, h = op
            q0 = begin[unit(u)[1]] + i * P
            m = min(P, S - q0)
            n = min(TILE, q0 + m - c * TILE)
            return q0, m, c * TILE, n, c * TILE + n == q0 + m

        def maximum_products(pe, op, n, base):
            if n >= M_RING:
                pe.wait_ge(max_used, n - M_RING + 1)
            u = op[0]
            g, t = unit(u)
            if len(op) == 1:
                pe.wait_ge(split_ready, u - base + 1)
                turned = max_scores[0:MAX_PARTS * GH, n % M_RING, :].bitcast(BF16)
                for i in range(-(-width[t] // P)):
                    m = min(P, width[t] - i * P)
                    last = nc.tensor.transpose(turned[:, i * P:i * P + m],
                                               max_split[0:m, u % 2, i].rearrange("p a h -> p (a h)"),
                                               ident[0:m, 0:m])
                last.then_inc(max_ready, 1)
                return
            q0, m, k0, keys, diagonal = geometry(op)
            last = nc.tensor.matmul(max_scores[0:m, n % M_RING, 0:keys], q_rows[0:ROWS, g, op[3], q0:q0 + m],
                                    k_rows[0:ROWS, (u // BU) % STEP_B, g, k0:k0 + keys], start=True, stop=not diagonal)
            if diagonal:
                last = nc.tensor.matmul(max_scores[0:m, n % M_RING, keys - m:keys], ident[0:m, 0:m],
                                        mask_qk[0:m, 0:m], start=False, stop=True)
            last.then_inc(max_ready, 1)

        def maximum_reductions(dve, order, base):
            slot_of = {op: n for n, op in enumerate(order)}
            chained = [0]

            def link(ins):
                chained[0] += 1
                ins.then_inc(chain, 1)
                dve.wait_ge(chain, chained[0])

            for n, op in enumerate(order):
                dve.wait_ge(max_ready, n + 1)
                u = op[0]
                t = unit(u)[1]
                if len(op) == 1:
                    if u >= base + 2:
                        dve.wait_ge(rows_set[u % 2], 16 * MAX_PARTS * ((u - base) // 2))
                    turned = max_scores[0:MAX_PARTS * GH, n % M_RING, :].bitcast(BF16)
                    nc.vector.tensor_copy(max_rows[:, u % 2, 0:width[t]], turned[:, 0:width[t]]).then_inc(rows_copied, 1)
                    dve.wait_ge(rows_copied, u - base + 1)
                    nc.vector.sem_inc(max_used, 1)
                    continue
                _, i, c, h = op
                _, m, _, keys, _ = geometry(op)
                nc.vector.tensor_reduce(part_max[0:m, u % 2, i, h, c:c + 1], max_scores[0:m, n % M_RING, 0:keys],
                                        AX_X, ALU.max).then_inc(max_used, 1)
                if op != MAX_OPS[u][-1]:
                    continue
                dve.wait_ge(max_used, n + 1)
                if u >= base + 2:
                    dve.wait_ge(max_ready, slot_of[(u - 2,)] + 1)
                blocks = -(-width[t] // P)
                counts = [key_chunks(t, i) for i in range(blocks)]
                for c in sorted(set(counts)):
                    i, k = counts.index(c), counts.count(c)
                    link(nc.vector.tensor_reduce(row_max[:, u % 2, i:i + k], part_max[:, u % 2, i:i + k, :, 0:c],
                                                 AX_X, ALU.max))
                high = max_split[:, u % 2, 0:blocks, 0, :]
                link(nc.vector.tensor_copy(high, row_max[:, u % 2, 0:blocks]))
                nc.vector.tensor_tensor(max_split[:, u % 2, 0:blocks, 1, :], row_max[:, u % 2, 0:blocks], high,
                                        ALU.subtract).then_inc(split_ready, 1)

        def maximum_rows(sp, u, base):
            g, t = unit(u)
            sp.wait_ge(rows_copied, u - base + 1)
            for part in range(MAX_PARTS):
                sp.dma_start(q_rows[ROWS + part:ROWS + part + 1, g, :, begin[t]:begin[t] + width[t]],
                             max_rows[part * GH:(part + 1) * GH, u % 2, 0:width[t]]).then_inc(rows_set[u % 2], 16)

        with nc.Block(no_gpsimd_drain=True) as block:
            @block.tensor
            def _(pe):
                for n, op in enumerate(first_order):
                    maximum_products(pe, op, n, NU)

            @block.vector
            def _(dve):
                maximum_reductions(dve, first_order, NU)

            @block.sync
            def _(sp):
                for t in range(AHEAD // GROUPS, QT):
                    for g in range(GROUPS):
                        load_queries(sp, 0, g, t, rest_in)
                for u in range(NU, LAST):
                    maximum_rows(sp, u, NU)
                sp.wait_ge(rest_in, 16 * (BU - AHEAD) * Q_LOADS)
                for half in range(2):
                    sp.wait_ge(rows_set[half], 16 * MAX_PARTS * (AHEAD // 2))
        clear_step()

        with nc.Fori(0, B // STEP_B) as step:
            with nc.Block(no_gpsimd_drain=True) as block:
                @block.sync
                def _(sp):
                    def store(u):
                        g, t = UNITS[u]
                        sp.wait_ge(o_copied, u + 1)
                        for h in range(GH):
                            sp.dma_start(heads_out[STEP_B * step + u // BU, g * GH + h][:, begin[t]:begin[t] + width[t]],
                                         out_sb[VW * h:VW * h + HD + 1, u % O_RING, 0:width[t]]).then_inc(o_stored[u % O_RING], 16)

                    def reload(u):
                        g, t = UNITS[u]
                        sp.wait_ge(s_ready, GH * first_step[u + 1])
                        load_queries(sp, (STEP_B * step + u // BU + 1) & (B - 1), g, t,
                                     unit_loaded[u] if u < len(unit_loaded) else next_loaded)

                    load_keys(sp, STEP_B * step + 1, 1, keys_loaded[1])
                    for _, kind, u in transfers:
                        if kind == 0:
                            maximum_rows(sp, u, AHEAD)
                        else:
                            reload(u)
                            store(u)
                        if (kind, u) == (1, BU - 1):
                            sp.wait_ge(p_used, first_step[BU])
                            load_keys(sp, (STEP_B * step + STEP_B) & (B - 1), 0, keys_loaded[0])
                    for r in range(O_RING):
                        sp.wait_ge(o_stored[r], 16 * GH * len(range(r, NU, O_RING)))
                    for half in range(2):
                        sp.wait_ge(rows_set[half], 16 * MAX_PARTS * (NU // 2))
                    sp.wait_ge(next_loaded, 16 * (NU - len(unit_loaded)) * Q_LOADS)

                @block.vector
                def _(dve):
                    maximum_reductions(dve, order, AHEAD)

                @block.gpsimd
                def _(pool):
                    for n, k in enumerate(DIAGONAL):
                        u, j = STEPS[k]
                        o = j * P - begin[UNITS[u][1]]
                        keys = min(P, S - j * P)
                        pool.wait_ge(p_ready, GH * (k + 1))
                        block_probs = probs[0:keys, k % P_RING, :, o:o + keys]
                        nc.gpsimd.affine_select(block_probs, block_probs, [[0, GH], [1, keys]], ALU.is_ge, 0.0,
                                                base=0, channel_multiplier=-1).then_inc(p_masked, 1)

                @block.scalar
                def _(act):
                    def copy_out(u):
                        w = width[UNITS[u][1]]
                        act.wait_ge(o_ready, u + 1)
                        if u >= O_RING:
                            act.wait_ge(o_stored[u % O_RING], 16 * GH * (u // O_RING))
                        nc.scalar.copy(out_sb[:, u % O_RING, 0:w], out_acc[:, 0:w]).then_inc(o_copied, 1)

                    for k, (u, j) in enumerate(STEPS):
                        t = UNITS[u][1]
                        o = max(0, j * P - begin[t])
                        keys = min(P, S - j * P)
                        if k >= P_RING:
                            act.wait_ge(p_used, k - P_RING + 1)
                        for h in range(GH):
                            act.wait_ge(s_ready, GH * k + h + 1)
                            nc.scalar.activation(probs[0:keys, k % P_RING, h, o:width[t]],
                                                 scores[0:keys, (GH * k + h) % S_RING, o:width[t]], ACT.Exp,
                                                 scale=float(HD) ** -0.5).then_inc(p_ready, 1)
                        if u >= 1 and k == first_step[u]:
                            copy_out(u - 1)
                    copy_out(NU - 1)

                @block.tensor
                def _(pe):
                    slots = [0]

                    def run_slot(op):
                        if len(op) == 4 and op[0] >= BU and op == MAX_OPS[op[0]][0]:
                            pe.wait_ge(unit_loaded[op[0] - BU], 16 * Q_LOADS)
                            pe.wait_ge(keys_loaded[(op[0] // BU) % STEP_B], 16 * KV_LOADS)
                        maximum_products(pe, op, slots[0], AHEAD)
                        slots[0] += 1

                    def score(k, h):
                        u, j = STEPS[k]
                        g, t = UNITS[u]
                        o = max(0, j * P - begin[t])
                        keys = min(P, S - j * P)
                        n = GH * k + h
                        if n >= S_RING:
                            pe.wait_ge(p_ready, n - S_RING + 1)
                        if u >= AHEAD and k == first_step[u] and h == 0:
                            pe.wait_ge(rows_set[u % 2], 16 * MAX_PARTS * ((u - AHEAD) // 2 + 1))
                        nc.tensor.matmul(scores[0:keys, n % S_RING, o:width[t]],
                                         k_rows[0:ROWS + MAX_PARTS, u // BU, g, j * P:j * P + keys],
                                         q_rows[0:ROWS + MAX_PARTS, g, h, begin[t] + o:begin[t] + width[t]],
                                         start=True, stop=True).then_inc(s_ready, 1)

                    def outputs(k):
                        u, j = STEPS[k]
                        g, t = UNITS[u]
                        o = max(0, j * P - begin[t])
                        keys = min(P, S - j * P)
                        pe.wait_ge(p_ready, GH * (k + 1))
                        if k in DIAGONAL:
                            pe.wait_ge(p_masked, DIAGONAL.index(k) + 1)
                        if j == 0 and u >= 1:
                            pe.wait_ge(o_copied, u)
                        end = k == first_step[u + 1] - 1
                        for h in range(GH):
                            v = h // 2
                            last = nc.tensor.matmul(out_acc[VW * h:VW * h + VW, o:width[t]],
                                                    v_keys[0:keys, u // BU, g, j, v * VW:(v + 1) * VW],
                                                    probs[0:keys, k % P_RING, h, o:width[t]],
                                                    start=(j == 0), stop=end)
                        last.then_inc(p_used, 1)
                        if end:
                            pe.wait_ge(p_used, k + 1)
                            nc.tensor.sem_inc(o_ready, 1)

                    for k in range(len(STEPS)):
                        ops = slots_at[k]
                        cut = [(len(ops) * x + 2) // 5 for x in range(6)]
                        for h in range(GH):
                            score(k, h)
                            for op in ops[cut[h]:cut[h + 1]]:
                                run_slot(op)
                        if k >= 1:
                            outputs(k - 1)
                        for op in ops[cut[4]:]:
                            run_slot(op)
                    outputs(len(STEPS) - 1)
            clear_step()


def inverse_sums(nc, heads_out, inverse):
    with ExitStack() as ctx:
        sums = ctx.enter_context(nc.sbuf_tensor("sums", [P, B, NH * S // P], F32))
        inv = ctx.enter_context(nc.sbuf_tensor("inv", [P, B, NH * S // P], F32))
        loaded = [ctx.enter_context(nc.semaphore(f"sums{b}_loaded")) for b in range(B)]
        done = ctx.enter_context(nc.semaphore("sums_inverted"))
        stored = ctx.enter_context(nc.semaphore("inverses_stored"))
        with nc.Block(no_gpsimd_drain=True) as block:
            @block.sync
            def _(sp):
                per = P // NH
                for b in range(B):
                    sp.dma_start(sums[:, b, :], heads_out[b, :, HD].rearrange("h (c n) -> h c n", c=per)).then_inc(loaded[b], 16)
                for b in range(B):
                    sp.wait_ge(done, b + 1)
                    sp.dma_start(inverse[b].rearrange("h (c n) -> (h c) n", c=per), inv[:, b, :]).then_inc(stored, 16)
                sp.wait_ge(stored, 16 * B)

            @block.vector
            def _(dve):
                for b in range(B):
                    dve.wait_ge(loaded[b], 16)
                    nc.vector.reciprocal(inv[:, b], sums[:, b]).then_inc(done, 1)


def second_norm(nc, heads_out, inverse, h0_in, wo, wr, br, tables, normed_out, sum_out, weights_out):
    centre, mean = tables
    with ExitStack() as ctx:
        def sbuf(name, shape, dt=F32):
            return ctx.enter_context(nc.sbuf_tensor(name, shape, dt))

        def psum(name, shape):
            return ctx.enter_context(nc.psum_tensor(name, shape, F32))

        def sem(name):
            return ctx.enter_context(nc.semaphore(name))

        wo_sb = sbuf("wo_sb", [P, P])
        wr_sb = sbuf("wr_sb", [P, 2])
        br_sb = sbuf("br_sb", [2, 1])
        eps_sb = sbuf("eps2_sb", [P, 1])
        centre_sb = sbuf("centre2_sb", [P, P])
        mean_sb = sbuf("mean2_sb", [P, P])
        heads = sbuf("heads", [P, RING, TILE])
        inv = sbuf("inv_rows", [P, RING, TILE])
        h0 = sbuf("h0_tile", [P, RING, TILE])
        attn = sbuf("attn", [P, 2, TILE])
        h2 = sbuf("h2", [P, RING, TILE])
        square = sbuf("square2", [P, 2, TILE])
        std = sbuf("std2", [P, 2, TILE])
        rstd = sbuf("rstd2", [P, 2, TILE])
        normed = sbuf("normed2", [P, RING, TILE])
        total = sbuf("total", [P, RING, TILE])
        router = sbuf("router", [2, STEP_PAIRS, S])
        proj_ps = psum("proj2_ps", [P, 2, TILE])
        centred_ps = psum("centred2_ps", [P, 2, TILE])
        var_ps = psum("var2_ps", [P, 2, TILE])
        router_ps = psum("router_ps", [2, 2, TILE])

        const_in = sem("const2_loaded")
        with nc.Block(no_gpsimd_drain=True) as block:
            @block.sync
            def _(sp):
                pieces = [(wo_sb[:], wo), (wr_sb[:], wr), (br_sb[:], br), (centre_sb[:], centre), (mean_sb[:], mean)]
                for dst, src in pieces:
                    sp.dma_start(dst, src).then_inc(const_in, 16)
                sp.wait_ge(const_in, 16 * len(pieces) + 1)

            @block.vector
            def _(dve):
                nc.vector.memset(eps_sb[:], EPS).then_inc(const_in, 1)

        loaded = [sem(f"tile_loaded{n}") for n in range(RING)]
        stored = [sem(f"tile_stored{n}") for n in range(RING)]
        attn_ready = sem("attn_ready")
        proj_ready = sem("proj2_ready")
        h2_ready = sem("h2_ready")
        centred = sem("centred2")
        squared = sem("squared2")
        var_ready = sem("var2_ready")
        std_ready = sem("std2_ready")
        rstd_ready = sem("rstd2_ready")
        normed_ready = sem("normed2_ready")
        total_ready = sem("total_ready")
        router_ready = sem("router_ready")
        router_set = sem("router_set")
        router_out = sem("router_stored")
        step_sems = [*loaded, *stored, attn_ready, proj_ready, h2_ready, centred, squared, var_ready, std_ready,
                     rstd_ready, normed_ready, total_ready, router_ready, router_set, router_out]
        NT = len(STEP_TILES)

        with nc.Fori(0, PAIRS // STEP_PAIRS) as step:
            with nc.Block(no_gpsimd_drain=True) as block:
                def tile_in(m):
                    return m % RING, loaded[m % RING], 16 * 3 * (m // RING + 1)

                def tile_out(m):
                    return m % RING, stored[m % RING], 16 * 2 * (m // RING)

                @block.sync
                def _(sp):
                    def load(m):
                        q, t0, w = STEP_TILES[m]
                        r = m % RING
                        if m >= RING:
                            sp.wait_ge(attn_ready, m - RING + 1)
                            sp.wait_ge(h2_ready, m - RING + 1)
                        two = heads_out[bass.ds(2 * (STEP_PAIRS * step + q), 2)].rearrange("b h r s -> (b h) r s")
                        sp.dma_start(heads[:, r, 0:w], two[:, 0:HD, t0:t0 + w]).then_inc(loaded[r], 16)
                        ones = inverse[bass.ds(2 * (STEP_PAIRS * step + q), 2)].rearrange("b h s -> (b h) s")[:, None, t0:t0 + w]
                        sp.dma_start(inv[:, r, 0:w], ones.to_broadcast([2 * NH, HD, w])).then_inc(loaded[r], 16)
                        sp.dma_start(h0[:, r, 0:w], h0_in[STEP_PAIRS * step + q][:, t0:t0 + w]).then_inc(loaded[r], 16)

                    for m in range(min(RING, NT)):
                        load(m)
                    for m, (q, t0, w) in enumerate(STEP_TILES):
                        r = m % RING
                        sp.wait_ge(normed_ready, m + 1)
                        sp.dma_start(normed_out[STEP_PAIRS * step + q][:, t0:t0 + w], normed[:, r, 0:w]).then_inc(stored[r], 16)
                        sp.wait_ge(total_ready, m + 1)
                        sp.dma_start(sum_out[STEP_PAIRS * step + q][:, t0:t0 + w], total[:, r, 0:w]).then_inc(stored[r], 16)
                        if m + RING < NT:
                            load(m + RING)
                    sp.wait_ge(router_set, NT)
                    for q in range(STEP_PAIRS):
                        sp.dma_start(weights_out[bass.ds(2 * (STEP_PAIRS * step + q), 2)], router[:, q]).then_inc(router_out, 16)
                    sp.wait_ge(router_out, 16 * STEP_PAIRS)
                    for r in range(RING):
                        sp.wait_ge(stored[r], 16 * 2 * len(range(r, NT, RING)))

                @block.scalar
                def _(act):
                    def squares(m):
                        w = STEP_TILES[m][2]
                        act.wait_ge(centred, m + 1)
                        if m >= 2:
                            act.wait_ge(var_ready, m - 1)
                        nc.scalar.activation(square[:, m % 2, 0:w], centred_ps[:, m % 2, 0:w], ACT.Square).then_inc(squared, 1)

                    def route(m):
                        q, t0, w = STEP_TILES[m]
                        act.wait_ge(router_ready, m + 1)
                        nc.scalar.activation(router[:, q, t0:t0 + w], router_ps[:, m % 2, 0:w], ACT.Identity,
                                             bias=br_sb[:]).then_inc(router_set, 1)

                    squares(0)
                    for m, (q, t0, w) in enumerate(STEP_TILES):
                        act.wait_ge(var_ready, m + 1)
                        if m >= 2:
                            act.wait_ge(rstd_ready, m - 1)
                        nc.scalar.activation(std[:, m % 2, 0:w], var_ps[:, m % 2, 0:w], ACT.Sqrt,
                                             bias=eps_sb[:]).then_inc(std_ready, 1)
                        if m + 1 < NT:
                            squares(m + 1)
                        if m >= 2:
                            route(m - 2)
                    route(NT - 2)
                    route(NT - 1)

                @block.gpsimd
                def _(pool):
                    def multiply(m):
                        w = STEP_TILES[m][2]
                        r, landed, count = tile_in(m)
                        pool.wait_ge(landed, count)
                        if m >= 2:
                            pool.wait_ge(proj_ready, m - 1)
                        nc.gpsimd.tensor_tensor(attn[:, m % 2, 0:w], heads[:, r, 0:w], inv[:, r, 0:w],
                                                ALU.mult).then_inc(attn_ready, 1)

                    def add(m):
                        w = STEP_TILES[m][2]
                        r, left, count = tile_out(m)
                        pool.wait_ge(normed_ready, m + 1)
                        if m >= RING:
                            pool.wait_ge(left, count)
                        nc.gpsimd.tensor_tensor(total[:, r, 0:w], normed[:, r, 0:w], h2[:, r, 0:w],
                                                ALU.add).then_inc(total_ready, 1)

                    multiply(0)
                    multiply(1)
                    for m in range(NT):
                        if m + 2 < NT:
                            multiply(m + 2)
                        if m >= 1:
                            add(m - 1)
                    add(NT - 1)

                @block.vector
                def _(dve):
                    def residual(m):
                        w = STEP_TILES[m][2]
                        dve.wait_ge(proj_ready, m + 1)
                        r, landed, count = tile_in(m)
                        dve.wait_ge(landed, count)
                        if m >= RING:
                            dve.wait_ge(total_ready, m - RING + 1)
                            dve.wait_ge(centred, m - RING + 1)
                        nc.vector.tensor_tensor(h2[:, r, 0:w], proj_ps[:, m % 2, 0:w], h0[:, r, 0:w],
                                                ALU.add).then_inc(h2_ready, 1)

                    residual(0)
                    residual(1)
                    for m in range(NT):
                        w = STEP_TILES[m][2]
                        dve.wait_ge(std_ready, m + 1)
                        nc.vector.reciprocal(rstd[:, m % 2, 0:w], std[:, m % 2, 0:w]).then_inc(rstd_ready, 1)
                        if m + 2 < NT:
                            residual(m + 2)
                        dve.wait_ge(rstd_ready, m + 1)
                        r, left, count = tile_out(m)
                        if m >= RING:
                            dve.wait_ge(left, count)
                            dve.wait_ge(router_ready, m - RING + 1)
                        nc.vector.tensor_tensor(normed[:, r, 0:w], centred_ps[:, m % 2, 0:w], rstd[:, m % 2, 0:w],
                                                ALU.mult).then_inc(normed_ready, 1)

                @block.tensor
                def _(pe):
                    def project(m):
                        w = STEP_TILES[m][2]
                        pe.wait_ge(attn_ready, m + 1)
                        if m >= 2:
                            pe.wait_ge(h2_ready, m - 1)
                        nc.tensor.matmul(proj_ps[:, m % 2, 0:w], wo_sb[:], attn[:, m % 2, 0:w],
                                         start=True, stop=True).then_inc(proj_ready, 1)

                    def centre_tile(m):
                        w = STEP_TILES[m][2]
                        pe.wait_ge(h2_ready, m + 1)
                        if m >= 2:
                            pe.wait_ge(normed_ready, m - 1)
                        nc.tensor.matmul(centred_ps[:, m % 2, 0:w], centre_sb[:], h2[:, m % RING, 0:w],
                                         start=True, stop=True).then_inc(centred, 1)

                    def route(m):
                        w = STEP_TILES[m][2]
                        pe.wait_ge(normed_ready, m + 1)
                        if m >= 2:
                            pe.wait_ge(router_set, m - 1)
                        nc.tensor.matmul(router_ps[:, m % 2, 0:w], wr_sb[:], normed[:, m % RING, 0:w],
                                         start=True, stop=True).then_inc(router_ready, 1)

                    project(0)
                    project(1)
                    centre_tile(0)
                    for m in range(NT):
                        w = STEP_TILES[m][2]
                        pe.wait_ge(squared, m + 1)
                        if m >= 2:
                            pe.wait_ge(std_ready, m - 1)
                        nc.tensor.matmul(var_ps[:, m % 2, 0:w], mean_sb[:], square[:, m % 2, 0:w],
                                         start=True, stop=True).then_inc(var_ready, 1)
                        if m + 1 < NT:
                            centre_tile(m + 1)
                        if m + 2 < NT:
                            project(m + 2)
                        if m >= 1:
                            route(m - 1)
                    route(NT - 1)
            nc.all_engine_barrier(sem_only=True)
            for s in step_sems:
                nc.sync.sem_clear(s)
            nc.all_engine_barrier(sem_only=True)


def select(nc, weights_in, batch_sum, batch_before, chosen_out):
    with ExitStack() as ctx:
        def sbuf(name, shape, dt=F32):
            return ctx.enter_context(nc.sbuf_tensor(name, shape, dt))

        def sem(name):
            return ctx.enter_context(nc.semaphore(name))

        I32 = mybir.dt.int32
        w = sbuf("weights", [P, SPAN])
        v = sbuf("signed_weights", [P, SPAN])
        ones_block = sbuf("batch_sum_sb", [P, P])
        before_block = sbuf("batch_before_sb", [P, P])
        flags = sbuf("flags", [P, SPAN])
        equal = sbuf("equal", [P, SPAN])
        above = sbuf("above", [P, SPAN])
        rank = sbuf("rank", [P, SPAN])
        zeros = sbuf("zeros", [P, SPAN])
        chosen = sbuf("chosen", [P, SPAN])
        count = sbuf("count", [P, 2])
        level = sbuf("level", [P, 1], I32)
        trial = sbuf("trial", [P, 1], I32)
        keep = sbuf("keep", [P, 1], I32)
        positive = sbuf("positive", [P, 1])
        sign = sbuf("sign", [P, 1])
        wanted = sbuf("wanted", [P, 1])
        threshold = sbuf("threshold", [P, 1])
        room = sbuf("room", [P, 1])
        count_ps = ctx.enter_context(nc.psum_tensor("count_ps", [P, 2], F32))
        loaded = sem("weights_in")
        chain = sem("select_steps")
        counted = sem("counted")
        summed = sem("summed")
        stored = sem("chosen_stored")
        BITS = 31

        with nc.Block(no_gpsimd_drain=True) as block:
            @block.sync
            def _(sp):
                sp.dma_start(w[:], weights_in.rearrange("b (c n) -> (b c) n", c=ROWS_PER_BATCH)).then_inc(loaded, 16)
                sp.dma_start(ones_block[:], batch_sum).then_inc(loaded, 16)
                sp.dma_start(before_block[:], batch_before).then_inc(loaded, 16)
                sp.wait_ge(counted, BITS + 3)
                sp.dma_start(chosen_out.rearrange("b (c n) -> (b c) n", c=ROWS_PER_BATCH), chosen[:]).then_inc(stored, 16)
                sp.wait_ge(stored, 16)

            @block.tensor
            def _(pe):
                pe.wait_ge(loaded, 48)
                for n in range(BITS + 1):
                    pe.wait_ge(counted, n + 1)
                    nc.tensor.matmul(count_ps[:, 0:1], ones_block[:], count[:, 0:1], start=True, stop=True).then_inc(summed, 1)
                pe.wait_ge(counted, BITS + 2)
                nc.tensor.matmul(count_ps[:, 0:1], ones_block[:], count[:, 0:1], start=True, stop=True)
                nc.tensor.matmul(count_ps[:, 1:2], before_block[:], count[:, 1:2], start=True, stop=True).then_inc(summed, 1)

            @block.vector
            def _(dve):
                steps = [0]

                def link(ins):
                    steps[0] += 1
                    ins.then_inc(chain, 1)
                    dve.wait_ge(chain, steps[0])

                link(nc.vector.memset(level[:], 0))
                link(nc.vector.memset(zeros[:], 0.0))
                dve.wait_ge(loaded, 48)
                nc.vector.tensor_scalar(flags[:], w[:], 0.0, 0.0, ALU.is_ge, ALU.add, accum_out=count[:, 0:1]).then_inc(counted, 1)
                dve.wait_ge(summed, 1)
                link(nc.vector.tensor_scalar(positive[:], count_ps[:, 0:1], float(TOP), None, ALU.is_ge))
                link(nc.vector.tensor_scalar(sign[:], positive[:], 2.0, -1.0, ALU.mult, ALU.add))
                link(nc.vector.tensor_scalar(wanted[:], positive[:], float(2 * TOP - S - 1), float(S - TOP + 1), ALU.mult, ALU.add))
                link(nc.vector.tensor_scalar(v[:], w[:], sign[:], None, ALU.mult))
                for n in range(BITS):
                    link(nc.vector.tensor_scalar(trial[:], level[:], 1 << (BITS - 1 - n), None, ALU.bitwise_or))
                    nc.vector.tensor_scalar(flags[:], v[:], trial[:].bitcast(F32), 0.0, ALU.is_ge, ALU.add,
                                            accum_out=count[:, 0:1]).then_inc(counted, 1)
                    dve.wait_ge(summed, n + 2)
                    link(nc.vector.tensor_scalar(keep[:], count_ps[:, 0:1], wanted[:], None, ALU.is_ge))
                    link(nc.vector.copy_predicated(level[:], keep[:], trial[:]))
                link(nc.vector.tensor_scalar(threshold[:], level[:].bitcast(F32), sign[:], None, ALU.mult))
                link(nc.vector.tensor_scalar(equal[:], w[:], threshold[:], None, ALU.is_equal))
                link(nc.vector.tensor_scalar(above[:], w[:], threshold[:], 0.0, ALU.is_gt, ALU.add, accum_out=count[:, 0:1]))
                link(nc.vector.tensor_tensor_scan(rank[:], equal[:], zeros[:], 0.0, ALU.add, ALU.add))
                nc.vector.tensor_copy(count[:, 1:2], rank[:, SPAN - 1:SPAN]).then_inc(counted, 1)
                dve.wait_ge(summed, BITS + 2)
                link(nc.vector.tensor_scalar(room[:], count_ps[:, 0:1], -1.0, float(TOP), ALU.mult, ALU.add))
                link(nc.vector.tensor_tensor(room[:], room[:], count_ps[:, 1:2], ALU.subtract))
                link(nc.vector.scalar_tensor_tensor(out=flags[:], in0=rank[:], scalar=room[:], in1=equal[:],
                                                    op0=ALU.is_le, op1=ALU.mult))
                link(nc.vector.tensor_tensor(above[:], above[:], flags[:], ALU.add))
                nc.vector.tensor_tensor(chosen[:], w[:], above[:], ALU.mult).then_inc(counted, 1)


def feed_forward(nc, normed_in, sum_in, chosen_in, ff_w, ff_b, identity, out):
    w1, w2 = ff_w
    b1, b2 = ff_b
    with ExitStack() as ctx:
        def sbuf(name, shape, dt=F32):
            return ctx.enter_context(nc.sbuf_tensor(name, shape, dt))

        def psum(name, shape):
            return ctx.enter_context(nc.psum_tensor(name, shape, F32))

        def sem(name):
            return ctx.enter_context(nc.semaphore(name))

        w1_sb = sbuf("ff_w1_sb", [P, CHUNKS, P])
        w2_sb = sbuf("ff_w2_sb", [P, 2, C])
        b1_sb = sbuf("ff_b1_sb", [P, 2])
        b2_sb = sbuf("ff_b2_sb", [P, 1])
        ident_sb = sbuf("ident3_sb", [P, P])
        normed = sbuf("normed3", [P, RING, TILE])
        total = sbuf("total3", [P, RING, TILE])
        chosen = sbuf("chosen3", [P, RING, TILE])
        hidden = sbuf("hidden3", [P, 2, CHUNKS, TILE])
        scaled = sbuf("scaled3", [P, 2, TILE])
        final = sbuf("final3", [P, 2, TILE])
        turned = sbuf("turned3", [P, 2, TILE // P, P])
        hidden_ps = psum("hidden3_ps", [P, CHUNKS, TILE])
        y_ps = psum("y3_ps", [P, 2, TILE])
        turned_ps = psum("turned3_ps", [P, 2, TILE // P, P])

        const_in = sem("const3_loaded")
        with nc.Block(no_gpsimd_drain=True) as block:
            @block.sync
            def _(sp):
                pieces = [(w1_sb[:].rearrange("p c m -> p (c m)"), w1), (w2_sb[:].rearrange("p c m -> p (c m)"), w2),
                          (b1_sb[:], b1), (b2_sb[:], b2), (ident_sb[:], identity)]
                for dst, src in pieces:
                    sp.dma_start(dst, src).then_inc(const_in, 16)
                sp.wait_ge(const_in, 16 * len(pieces))

        loaded = [sem(f"tile3_loaded{n}") for n in range(RING)]
        hidden_ready = sem("hidden3_ready")
        gelu_ready = sem("gelu_ready")
        y_ready = sem("y3_ready")
        scaled_ready = sem("scaled_ready")
        final_ready = sem("final_ready")
        turned_ready = sem("turned3_ready")
        turned_set = sem("turned3_set")
        stored = [sem("out3_stored_even"), sem("out3_stored_odd")]
        step_sems = [*loaded, hidden_ready, gelu_ready, y_ready, scaled_ready, final_ready, turned_ready,
                     turned_set, *stored]
        NT = len(STEP_TILES)

        def stores(m):
            w = STEP_TILES[m][2]
            return 2 * ((w >= P) + (w % P > 0))

        def stored_by(m, half):
            return 16 * sum(stores(n) for n in range(m) if n % 2 == half)

        with nc.Fori(0, PAIRS // STEP_PAIRS) as step:
            with nc.Block(no_gpsimd_drain=True) as block:
                @block.sync
                def _(sp):
                    def store(m):
                        q, t0, w = STEP_TILES[m]
                        sp.wait_ge(turned_set, m + 1)
                        k, rest = divmod(w, P)
                        for e in range(2):
                            rows = out[bass.ds(2 * (STEP_PAIRS * step + q) + e, 1)].rearrange("o s c -> (o s) c")
                            sp.dma_start(rows[t0:t0 + k * P].rearrange("(k p) c -> p k c", p=P),
                                         turned[:, m % 2, 0:k, e * C:(e + 1) * C]).then_inc(stored[m % 2], 16)
                            if rest:
                                sp.dma_start(rows[t0 + k * P:t0 + w],
                                             turned[0:rest, m % 2, k, e * C:(e + 1) * C]).then_inc(stored[m % 2], 16)

                    def load(m):
                        q, t0, w = STEP_TILES[m]
                        r = m % RING
                        if m >= RING:
                            sp.wait_ge(hidden_ready, CHUNKS * (m - RING + 1))
                            sp.wait_ge(final_ready, m - RING + 1)
                        sp.dma_start(normed[:, r, 0:w], normed_in[STEP_PAIRS * step + q][:, t0:t0 + w]).then_inc(loaded[r], 16)
                        sp.dma_start(total[:, r, 0:w], sum_in[STEP_PAIRS * step + q][:, t0:t0 + w]).then_inc(loaded[r], 16)
                        rows = chosen_in[bass.ds(2 * (STEP_PAIRS * step + q), 2)][:, None, t0:t0 + w]
                        sp.dma_start(chosen[:, r, 0:w], rows.to_broadcast([2, C, w])).then_inc(loaded[r], 16)

                    for m in range(min(RING, NT)):
                        load(m)
                    for m in range(NT):
                        if m + RING < NT:
                            load(m + RING)
                        store(m)
                    for half in range(2):
                        sp.wait_ge(stored[half], stored_by(NT, half))

                @block.tensor
                def _(pe):
                    def turn(m):
                        w = STEP_TILES[m][2]
                        pe.wait_ge(final_ready, m + 1)
                        if m >= 2:
                            pe.wait_ge(turned_set, m - 1)
                        for k in range(-(-w // P)):
                            n = min(P, w - k * P)
                            last = nc.tensor.transpose(turned_ps[0:n, m % 2, k], final[:, m % 2, k * P:k * P + n],
                                                       ident_sb[:])
                        last.then_inc(turned_ready, 1)

                    def second(m):
                        w = STEP_TILES[m][2]
                        if m >= 2:
                            pe.wait_ge(scaled_ready, m - 1)
                        for half in range(2):
                            for e in range(2):
                                pe.wait_ge(gelu_ready, CHUNKS * m + 2 * e + half + 1)
                                last = nc.tensor.matmul(y_ps[e * C:(e + 1) * C, m % 2, 0:w], w2_sb[:, half],
                                                        hidden[:, m % 2, 2 * e + half, 0:w],
                                                        start=(half == 0), stop=(half == 1))
                        last.then_inc(y_ready, 1)

                    for m in range(NT):
                        w = STEP_TILES[m][2]
                        pe.wait_ge(loaded[m % RING], 16 * 3 * (m // RING + 1))
                        for c in range(CHUNKS):
                            if m >= 1:
                                pe.wait_ge(gelu_ready, CHUNKS * (m - 1) + c + 1)
                            nc.tensor.matmul(hidden_ps[:, c, 0:w], w1_sb[:, c], normed[:, m % RING, 0:w],
                                             start=True, stop=True).then_inc(hidden_ready, 1)
                        if m >= 1:
                            second(m - 1)
                        if m >= 2:
                            turn(m - 2)
                    second(NT - 1)
                    turn(NT - 2)
                    turn(NT - 1)

                @block.scalar
                def _(act):
                    def copy_turned(m):
                        w = STEP_TILES[m][2]
                        act.wait_ge(turned_ready, m + 1)
                        if m >= 2:
                            act.wait_ge(stored[m % 2], stored_by(m, m % 2))
                        k, rest = divmod(w, P)
                        last = nc.scalar.copy(turned[:, m % 2, 0:k], turned_ps[:, m % 2, 0:k])
                        if rest:
                            last = nc.scalar.copy(turned[0:rest, m % 2, k], turned_ps[0:rest, m % 2, k])
                        last.then_inc(turned_set, 1)

                    for m in range(NT):
                        w = STEP_TILES[m][2]
                        for c in range(CHUNKS):
                            act.wait_ge(hidden_ready, CHUNKS * m + c + 1)
                            if m >= 2:
                                act.wait_ge(y_ready, m - 1)
                            nc.scalar.activation(hidden[:, m % 2, c, 0:w], hidden_ps[:, c, 0:w], ACT.Gelu_apprx_tanh,
                                                 bias=b1_sb[:, c % 2:c % 2 + 1]).then_inc(gelu_ready, 1)
                        if m >= 3:
                            copy_turned(m - 3)
                    for m in range(NT - 3, NT):
                        copy_turned(m)

                @block.vector
                def _(dve):
                    for m in range(NT):
                        w = STEP_TILES[m][2]
                        dve.wait_ge(y_ready, m + 1)
                        dve.wait_ge(loaded[m % RING], 16 * 3 * (m // RING + 1))
                        nc.vector.scalar_tensor_tensor(out=scaled[:, m % 2, 0:w], in0=y_ps[:, m % 2, 0:w], scalar=b2_sb[:],
                                                       in1=chosen[:, m % RING, 0:w], op0=ALU.add,
                                                       op1=ALU.mult).then_inc(scaled_ready, 1)
                        dve.wait_ge(scaled_ready, m + 1)
                        if m >= 2:
                            dve.wait_ge(turned_ready, m - 1)
                        nc.vector.tensor_tensor(final[:, m % 2, 0:w], scaled[:, m % 2, 0:w], total[:, m % RING, 0:w],
                                                ALU.add).then_inc(final_ready, 1)
            nc.all_engine_barrier(sem_only=True)
            for s in step_sems:
                nc.sync.sem_clear(s)
            nc.all_engine_barrier(sem_only=True)


def program(nc, a, out):
    def scratch(name, shape, dt=F32):
        return nc.dram_tensor(name, shape, dt, kind="Internal").ap()

    h0 = scratch("h0_dram", (PAIRS, P, S))
    q_terms = scratch("q_terms_dram", (B, NH, HEAD_ROWS, S), BF16)
    k_terms = scratch("k_terms_dram", (B, KV, HEAD_ROWS, S), BF16)
    v_blocks = scratch("v_blocks_dram", (B, GROUPS, P, KB * GKV * VW))
    heads = scratch("heads_dram", (B, NH, HD + 1, S))
    inverse = scratch("inverse_dram", (B, NH, S))
    normed = scratch("normed_dram", (PAIRS, P, S))
    total = scratch("total_dram", (PAIRS, P, S))
    weights = scratch("weights_dram", (B, S))
    chosen = scratch("chosen_dram", (B, S))
    tokens(nc, a["x"], a["txt"], (a["w1"], a["w2"], a["w3"]), (a["b1"], a["b2"], a["b3"]),
           (a["wq"], a["wq_turned"], a["wk"], a["wk_turned"], a["wv"]),
           (a["centre"], a["mean"], a["cos"], a["sin"], a["identity"]), h0, q_terms, k_terms, v_blocks)
    attention(nc, q_terms, k_terms, v_blocks, a["masks"], heads)
    inverse_sums(nc, heads, inverse)
    second_norm(nc, heads, inverse, h0, a["wo"], a["wr"], a["br"], (a["centre"], a["mean"]), normed, total, weights)
    select(nc, weights, a["batch_sum"], a["batch_before"], chosen)
    feed_forward(nc, normed, total, chosen, (a["ff_w1"], a["ff_w2"]), (a["ff_b1"], a["ff_b2"]), a["identity"], out)


def arranged(i):
    import numpy as np

    def two(w):
        k, m = w.shape
        o = np.zeros((2 * k, 2 * m), w.dtype)
        o[:k, :m] = w
        o[k:, m:] = w
        return o

    def by_shift(w):
        return np.ascontiguousarray(np.stack([two(w[:, s, :]) for s in range(SHIFTS)], 1).reshape(P, SHIFTS * P))

    def both(b):
        return np.ascontiguousarray(np.concatenate([b.reshape(C, -1)] * 2, 0))

    turn = np.arange(NH * HD).reshape(NH, 2, HD // 2)[:, ::-1].reshape(NH * HD)
    wq, wk, wv = i["L0_attn_Wq"], i["L0_attn_Wk"], i["L0_attn_Wv"]
    inv_freq = (1.0 / 10000.0 ** (np.arange(0, HD, 2, dtype=np.float32) / np.float32(HD))).astype(np.float32)
    angle = np.outer(np.arange(S, dtype=np.float32), inv_freq).astype(np.float32)
    angle = np.concatenate([angle, angle], -1)
    sign = np.where(np.arange(HD) < HD // 2, -1, 1).astype(np.float32)
    mean = two(np.full((C, C), 1 / C, np.float32))
    at = np.arange(P)
    after = np.where(at[:, None] > at[None, :], -3e38, 0).astype(np.float32)
    same = at[:, None] // ROWS_PER_BATCH == at[None, :] // ROWS_PER_BATCH
    ff_w1 = np.zeros((2, C, CHUNKS, P), np.float32)
    for e in range(2):
        for half in range(2):
            ff_w1[e, :, 2 * e + half] = i["L0_ffn_w1"][:, half * P:(half + 1) * P]
    return {
        "x": i["x"].reshape(PAIRS, P, IMG),
        "txt": i["txt"].reshape(PAIRS, 2, TXT, C),
        "w1": by_shift(i["L0_tok_W1"].reshape(C, SHIFTS, C)),
        "w2": by_shift(i["L0_tok_W2"].reshape(C, C, SHIFTS).transpose(0, 2, 1)),
        "w3": by_shift(i["L0_tok_W3"].reshape(C, SHIFTS, C)),
        "b1": both(i["L0_tok_b1"]),
        "b2": both(i["L0_tok_b2"]),
        "b3": both(i["L0_tok_b3"]),
        "wq": two(wq.T),
        "wq_turned": two(wq[turn].T),
        "wk": two(wk.T),
        "wk_turned": two(wk[turn[:KV * HD]].T),
        "wv": two(wv.T),
        "wo": two(i["L0_attn_Wo"].T),
        "wr": two(i["L0_ffn_wr"]),
        "br": np.concatenate([i["L0_ffn_br"].reshape(1, 1)] * 2, 0),
        "ff_w1": ff_w1.reshape(P, CHUNKS * P),
        "ff_w2": np.ascontiguousarray(i["L0_ffn_w2"].reshape(2, P, C).transpose(1, 0, 2).reshape(P, 2 * C)),
        "ff_b1": np.ascontiguousarray(i["L0_ffn_b1"].reshape(2, P).T),
        "ff_b2": both(i["L0_ffn_b2"]),
        "centre": np.eye(P, dtype=np.float32) - mean,
        "mean": mean,
        "cos": np.ascontiguousarray(np.tile(np.cos(angle).T, (P // HD, 1))),
        "sin": np.ascontiguousarray(np.tile((np.sin(angle) * sign).T, (P // HD, 1))),
        "identity": np.eye(P, dtype=np.float32),
        "masks": np.stack([after.T, np.eye(P, dtype=np.float32)]),
        "batch_sum": same.astype(np.float32),
        "batch_before": (same & (at[:, None] < at[None, :])).astype(np.float32),
    }


def kernel(**inputs):
    import numpy as np
    import concourse.bacc as bacc
    from concourse.bass_utils import run_bass_kernel_spmd

    nc = bacc.Bacc("TRN2", target_bir_lowering=False, num_devices=1)
    arrays, aps = {}, {}
    for name, array in arranged({k: np.asarray(v) for k, v in inputs.items()}).items():
        arrays["in_" + name] = np.ascontiguousarray(array)
        aps[name] = nc.dram_tensor("in_" + name, array.shape, mybir.dt.from_np(array.dtype), kind="ExternalInput").ap()
    out = nc.dram_tensor("out_0", (B, S, C), F32, kind="ExternalOutput").ap()
    program(nc, aps, out)
    r = run_bass_kernel_spmd(nc, [arrays], core_ids=[0])
    return r.results[0]["out_0"]
```
